# Optimizing a Trainium2 kernel written in Bass

```python
import numpy as np
import jax
import jax.numpy as jnp

def _softmax(x, axis=-1):
    return jax.nn.softmax(x, axis=axis)
def _gelu(x):
    return jax.nn.gelu(x, approximate=True)
def _silu(x):
    return jax.nn.silu(x)
def _sigmoid(x):
    return jax.nn.sigmoid(x)
def _layernorm(x, axis=-1, eps=1e-5):
    m = jnp.mean(x, axis=axis, keepdims=True)
    v = jnp.var(x, axis=axis, keepdims=True)
    return (x - m) / jnp.sqrt(v + eps)
def _scatter_add(tgt, idx, src, axis=0):
    return tgt.at[idx].add(src)
def _segment_sum(src, seg, n):
    return jax.ops.segment_sum(src, seg, n)

kernel_name = 'mk_conv_preact_d2_conv_nhwc256_3256a6'

def setup_inputs(seed: int = 0):
    np.random.seed(seed)
    _w = jnp.asarray
    def _rec_inputs():
        import jax
        import jax.numpy as jnp
        _gk = jax.random.key(seed)
        x = -0.0005207 + 1.001 * jax.random.normal(jax.random.fold_in(_gk, 1), (8, 32, 32, 256), jnp.float32)
        return x
    x = _rec_inputs()
    def _L0_conv_setup():
        import jax, jax.numpy as jnp
        import numpy as np
        HEAD_DIM = 16

        def _conv2d_same(x_nchw, w_oihw, b):
            y = jax.lax.conv_general_dilated(x_nchw, w_oihw, window_strides=(1, 1), padding='SAME', dimension_numbers=('NCHW', 'OIHW', 'NCHW'))
            return y + b[None, :, None, None]
        key = jax.random.key(seed)
        ks = jax.random.split(key, 9)
        dim = 256
        B, H, W = (8, 32, 32)
        x = jax.random.normal(ks[0], (B, H, W, dim), jnp.float32)
        w3 = jax.random.normal(ks[1], (dim, dim, 1, 1), jnp.float32) * 0.05
        b3 = jax.random.normal(ks[2], (dim,), jnp.float32) * 0.01
        w5 = jax.random.normal(ks[3], (dim, dim, 3, 3), jnp.float32) * 0.02
        b5 = jax.random.normal(ks[4], (dim,), jnp.float32) * 0.01
        w7 = jax.random.normal(ks[5], (dim, dim, 5, 5), jnp.float32) * 0.01
        b7 = jax.random.normal(ks[6], (dim,), jnp.float32) * 0.01
        wp = jax.random.normal(ks[7], (dim, dim), jnp.float32) * 0.05
        return {'x': x, 'w3': w3, 'b3': b3, 'w5': w5, 'b5': b5, 'w7': w7, 'b7': b7, 'wp': wp}
    _L0_conv_all = _L0_conv_setup()
    _L0_conv_in = {k: v for k, v in _L0_conv_all.items() if k in ('w3', 'b3', 'w5', 'b5', 'w7', 'b7', 'wp', )}
    del _L0_conv_all

    def _L1_conv_setup():
        import jax, jax.numpy as jnp
        import numpy as np
        import math
        from jax import lax
        DEC_LO = np.array([-0.00011747678400228192, 0.0006754494059985568, -0.0003917403729959771, -0.00487035299301066, 0.008746094047015655, 0.013981027917015516, -0.04408825393106472, -0.01736930100202211, 0.128747426620186, 0.00047248457399797254, -0.2840155429624281, -0.015829105256023893, 0.5853546836548691, 0.6756307362980128, 0.3128715909144659, 0.05441584224308161], dtype=np.float64)
        BAND_LEN = 16
        HALF = 8
        REC_LO = DEC_LO[::-1]
        REC_HI = DEC_LO * (-1.0) ** np.arange(BAND_LEN)

        def _band_matrices(size):
            s2 = size // 2
            m_lo = np.zeros((s2, size + BAND_LEN - 2))
            m_hi = np.zeros((size - s2, size + BAND_LEN - 2))
            for i in range(s2):
                m_lo[i, 2 * i:2 * i + BAND_LEN] = REC_LO
            for i in range(size - s2):
                m_hi[i, 2 * i:2 * i + BAND_LEN] = REC_HI
            m_lo = m_lo[:, HALF - 1:-(HALF - 1)]
            m_hi = m_hi[:, HALF - 1:-(HALF - 1)]
            return (jnp.asarray(m_lo, jnp.float32), jnp.asarray(m_hi, jnp.float32))

        def dwt2d(x):
            H, W = (x.shape[-2], x.shape[-1])
            lo0, hi0 = _band_matrices(H)
            lo1, hi1 = _band_matrices(W)
            lo1, hi1 = (lo1.T, hi1.T)
            Lp = jnp.matmul(lo0, x)
            Hp = jnp.matmul(hi0, x)
            return (Lp @ lo1, Lp @ hi1, Hp @ lo1, Hp @ hi1)

        def idwt2d(LL, LH, HL, HH):
            H = LL.shape[-2] + HH.shape[-2]
            W = LL.shape[-1] + HH.shape[-1]
            lo0, hi0 = _band_matrices(H)
            lo1, hi1 = _band_matrices(W)
            L = LL @ lo1 + LH @ hi1
            Hh = HL @ lo1 + HH @ hi1
            return jnp.matmul(lo0.T, L) + jnp.matmul(hi0.T, Hh)

        def inception(x, ws, bs):
            outs = []
            for i, (w, b) in enumerate(zip(ws, bs)):
                y = lax.conv_general_dilated(x, w, (1, 1), [(i, i), (i, i)], dimension_numbers=('NCHW', 'OIHW', 'NCHW')) + b.reshape(1, -1, 1, 1)
                outs.append(y)
            return jnp.mean(jnp.stack(outs, -1), -1)

        def median_low(x):
            n = x.shape[-1]
            return jnp.sort(x, axis=-1)[..., (n - 1) // 2][..., None]
        key = jax.random.key(seed)
        ks = jax.random.split(key, 16)
        B, T, N, D = (8, 128, 100, 256)
        inp = {'x': jax.random.normal(ks[0], (B, T, N, D), jnp.float32), 'adj': jax.random.uniform(ks[1], (N, N), jnp.float32)}
        for i in range(6):
            k = 2 * i + 1
            std = math.sqrt(2.0 / (k * k))
            inp[f'w{i}'] = jax.random.normal(ks[2 + i], (1, 1, k, k), jnp.float32) * std
            inp[f'b{i}'] = jnp.zeros((1,), jnp.float32)
        inp['out_w'] = jax.random.normal(ks[10], (D, D), jnp.float32) / math.sqrt(D)
        inp['out_b'] = jnp.zeros((D,), jnp.float32)
        return inp
    _L1_conv_all = _L1_conv_setup()
    _L1_conv_in = {k: v for k, v in _L1_conv_all.items() if k in ('adj', 'w0', 'w1', 'w2', 'w3', 'w4', 'w5', 'b0', 'b1', 'b2', 'b3', 'b4', 'b5', 'out_w', 'out_b', )}
    del _L1_conv_all

    return {
        "x": x,
        "L0_conv_w3": _L0_conv_in["w3"],
        "L0_conv_b3": _L0_conv_in["b3"],
        "L0_conv_w5": _L0_conv_in["w5"],
        "L0_conv_b5": _L0_conv_in["b5"],
        "L0_conv_w7": _L0_conv_in["w7"],
        "L0_conv_b7": _L0_conv_in["b7"],
        "L0_conv_wp": _L0_conv_in["wp"],
        "L1_conv_adj": _L1_conv_in["adj"],
        "L1_conv_w0": _L1_conv_in["w0"],
        "L1_conv_w1": _L1_conv_in["w1"],
        "L1_conv_w2": _L1_conv_in["w2"],
        "L1_conv_w3": _L1_conv_in["w3"],
        "L1_conv_w4": _L1_conv_in["w4"],
        "L1_conv_w5": _L1_conv_in["w5"],
        "L1_conv_b0": _L1_conv_in["b0"],
        "L1_conv_b1": _L1_conv_in["b1"],
        "L1_conv_b2": _L1_conv_in["b2"],
        "L1_conv_b3": _L1_conv_in["b3"],
        "L1_conv_b4": _L1_conv_in["b4"],
        "L1_conv_b5": _L1_conv_in["b5"],
        "L1_conv_out_w": _L1_conv_in["out_w"],
        "L1_conv_out_b": _L1_conv_in["out_b"],
    }

def reference(x, L0_conv_w3, L0_conv_b3, L0_conv_w5, L0_conv_b5, L0_conv_w7, L0_conv_b7, L0_conv_wp, L1_conv_adj, L1_conv_w0, L1_conv_w1, L1_conv_w2, L1_conv_w3, L1_conv_w4, L1_conv_w5, L1_conv_b0, L1_conv_b1, L1_conv_b2, L1_conv_b3, L1_conv_b4, L1_conv_b5, L1_conv_out_w, L1_conv_out_b):
    import jax
    import jax.numpy as jnp
    def _L0_conv_ref(x, w3, b3, w5, b5, w7, b7, wp):
        import jax, jax.numpy as jnp
        import numpy as np
        HEAD_DIM = 16

        def _conv2d_same(x_nchw, w_oihw, b):
            y = jax.lax.conv_general_dilated(x_nchw, w_oihw, window_strides=(1, 1), padding='SAME', dimension_numbers=('NCHW', 'OIHW', 'NCHW'))
            return y + b[None, :, None, None]
        B, H, W, C = x.shape
        N = H * W
        nh = C // HEAD_DIM
        scale = HEAD_DIM ** (-0.5)
        xc = jnp.transpose(x, (0, 3, 1, 2))
        q = _conv2d_same(xc, w3, b3).reshape(B, nh, N, HEAD_DIM)
        v = _conv2d_same(xc, w5, b5).reshape(B, nh, N, HEAD_DIM)
        k = _conv2d_same(xc, w7, b7).reshape(B, nh, N, HEAD_DIM)
        attn = jax.nn.softmax(jnp.einsum('bhnd,bhmd->bhnm', q, k) * scale, axis=-1)
        out = jnp.einsum('bhnm,bhmd->bhnd', attn, v)
        out = jnp.transpose(out, (0, 2, 1, 3)).reshape(B, H, W, nh * HEAD_DIM)
        return out @ wp.T

    def _L1_conv_ref(x, adj, w0, w1, w2, w3, w4, w5, b0, b1, b2, b3, b4, b5, out_w, out_b):
        import jax, jax.numpy as jnp
        import numpy as np
        import math
        from jax import lax
        DEC_LO = np.array([-0.00011747678400228192, 0.0006754494059985568, -0.0003917403729959771, -0.00487035299301066, 0.008746094047015655, 0.013981027917015516, -0.04408825393106472, -0.01736930100202211, 0.128747426620186, 0.00047248457399797254, -0.2840155429624281, -0.015829105256023893, 0.5853546836548691, 0.6756307362980128, 0.3128715909144659, 0.05441584224308161], dtype=np.float64)
        BAND_LEN = 16
        HALF = 8
        REC_LO = DEC_LO[::-1]
        REC_HI = DEC_LO * (-1.0) ** np.arange(BAND_LEN)

        def _band_matrices(size):
            s2 = size // 2
            m_lo = np.zeros((s2, size + BAND_LEN - 2))
            m_hi = np.zeros((size - s2, size + BAND_LEN - 2))
            for i in range(s2):
                m_lo[i, 2 * i:2 * i + BAND_LEN] = REC_LO
            for i in range(size - s2):
                m_hi[i, 2 * i:2 * i + BAND_LEN] = REC_HI
            m_lo = m_lo[:, HALF - 1:-(HALF - 1)]
            m_hi = m_hi[:, HALF - 1:-(HALF - 1)]
            return (jnp.asarray(m_lo, jnp.float32), jnp.asarray(m_hi, jnp.float32))

        def dwt2d(x):
            H, W = (x.shape[-2], x.shape[-1])
            lo0, hi0 = _band_matrices(H)
            lo1, hi1 = _band_matrices(W)
            lo1, hi1 = (lo1.T, hi1.T)
            Lp = jnp.matmul(lo0, x)
            Hp = jnp.matmul(hi0, x)
            return (Lp @ lo1, Lp @ hi1, Hp @ lo1, Hp @ hi1)

        def idwt2d(LL, LH, HL, HH):
            H = LL.shape[-2] + HH.shape[-2]
            W = LL.shape[-1] + HH.shape[-1]
            lo0, hi0 = _band_matrices(H)
            lo1, hi1 = _band_matrices(W)
            L = LL @ lo1 + LH @ hi1
            Hh = HL @ lo1 + HH @ hi1
            return jnp.matmul(lo0.T, L) + jnp.matmul(hi0.T, Hh)

        def inception(x, ws, bs):
            outs = []
            for i, (w, b) in enumerate(zip(ws, bs)):
                y = lax.conv_general_dilated(x, w, (1, 1), [(i, i), (i, i)], dimension_numbers=('NCHW', 'OIHW', 'NCHW')) + b.reshape(1, -1, 1, 1)
                outs.append(y)
            return jnp.mean(jnp.stack(outs, -1), -1)

        def median_low(x):
            n = x.shape[-1]
            return jnp.sort(x, axis=-1)[..., (n - 1) // 2][..., None]
        ws = [w0, w1, w2, w3, w4, w5]
        bs = [b0, b1, b2, b3, b4, b5]
        B, T, N, D = x.shape
        dwt_level = 3
        xd = jnp.transpose(x, (0, 2, 1, 3)).reshape(-1, T, D)[:, None, :, :]
        s2logT = math.sqrt(2.0 * math.log(T))
        LLd, LHd, HLd, HHd = ({}, {}, {}, {})
        LL = xd
        for i in range(dwt_level):
            LL, LH, HL, HH = dwt2d(LL)
            thr = median_low(jnp.abs(HH)) / 0.6745 * s2logT
            soft = lambda v: jnp.sign(v) * jnp.maximum(jnp.abs(v) - thr, 0.0)
            LL = inception(LL, ws, bs)
            LLd[i] = LL
            LHd[i] = inception(soft(LH), ws, bs)
            HLd[i] = inception(soft(HL), ws, bs)
            HHd[i] = inception(soft(HH), ws, bs)
        LL = LLd[dwt_level - 1]
        for i in range(dwt_level):
            j = dwt_level - 1 - i
            LL = idwt2d(LL, LHd[j], HLd[j], HHd[j])
        y = jnp.transpose(LL, (0, 2, 1, 3))
        y = y @ out_w.T + out_b
        y = y[:, :, 0, :].reshape(B, N, T, D)
        return jnp.transpose(y, (0, 2, 1, 3))

    def _gn(v, G=32, eps=1e-5):
        B_, H_, W_, C_ = v.shape
        g = v.reshape(B_, H_, W_, G, C_ // G)
        m = jnp.mean(g, axis=(1, 2, 4), keepdims=True)
        s = jnp.var(g, axis=(1, 2, 4), keepdims=True)
        return ((g - m) / jnp.sqrt(s + eps)).reshape(v.shape)

    def _ln_c(v, eps=1e-6):
        m = jnp.mean(v, axis=-1, keepdims=True)
        s = jnp.var(v, axis=-1, keepdims=True)
        return (v - m) / jnp.sqrt(s + eps)

    def _ln_t(v, eps=1e-5):
        m = jnp.mean(v, axis=-1, keepdims=True)
        s = jnp.var(v, axis=-1, keepdims=True)
        return (v - m) / jnp.sqrt(s + eps)

    def _to_tokens(v):
        B_, H_, W_, C_ = v.shape
        return v.reshape(B_, H_ * W_, C_)
    def _from_tokens(t, like):
        return t.reshape(like.shape)

    x = x + _L0_conv_ref(_gn(x), L0_conv_w3, L0_conv_b3, L0_conv_w5, L0_conv_b5, L0_conv_w7, L0_conv_b7, L0_conv_wp)
    x = x + _L1_conv_ref(_gn(x), L1_conv_adj, L1_conv_w0, L1_conv_w1, L1_conv_w2, L1_conv_w3, L1_conv_w4, L1_conv_w5, L1_conv_b0, L1_conv_b1, L1_conv_b2, L1_conv_b3, L1_conv_b4, L1_conv_b5, L1_conv_out_w, L1_conv_out_b)
    return x


_drawn_inputs = setup_inputs


def setup_inputs(seed=0):
    import zlib

    import numpy as np

    out = dict(_drawn_inputs(seed))
    spreads = {'L1_conv_out_b': (0.0, 0.1)}
    factors = {'L0_conv_w3': 3.21,
     'L0_conv_b3': 8.0,
     'L0_conv_b5': 8.0,
     'L0_conv_w7': 2.958,
     'L0_conv_b7': 8.0,
     'L1_conv_w2': 3.323}
    for name, (base, spread) in spreads.items():
        noise = np.random.default_rng([zlib.crc32(name.encode()), seed]).standard_normal(out[name].shape)
        drawn = base * np.exp(spread * noise) if base else spread * noise
        out[name] = jnp.asarray(drawn.astype(out[name].dtype))
    for name, factor in factors.items():
        out[name] = (out[name] * factor).astype(out[name].dtype)
    return out
```

```python
from contextlib import ExitStack

import numpy as np

import concourse.bass as bass
from concourse import mybir
from concourse.alu_op_type import AluOpType as ALU

F32 = mybir.dt.float32
F16 = mybir.dt.float16
ACT = mybir.ActivationFunctionType
AX = mybir.AxisListType

P = 128
B, H, W, C = 8, 32, 32, 256
N = H * W
CT = C // P
G = 32
CG = C // G
NT = N // P
HD = 16
NH = C // HD
HEADS = B * NH
EPS = 1e-5
BANK = 512

PAD = 2
PW = W + 2 * PAD
PH = H + 2 * PAD
CONVS = (("q", 1, 0), ("v", 3, 1), ("k", 5, 10))
TAPS = 35
X_SCALE = 256.0
W_SCALE = 256.0
QK_SCALE = 16.0


def wait(engine, sem, value):
    if not (isinstance(value, int) and value <= 0):
        engine.wait_ge(sem, value)


def bank_free(b, n):
    return 4 * b + max(n - 1, 0)


def conv_phase(nc, x, wq, wv, wk, bq, bv, bk, mean_op, ident, q_s, k_s, v_s):
    CHUNK = 5
    chunks = []
    for w, (_, side, base) in zip((wq, wv, wk), CONVS):
        for t in range(0, side * side, CHUNK):
            chunks.append((w, t, min(CHUNK, side * side - t), base + t))
    chunks_of = {"q": 1, "v": 3, "k": 8}
    tiles = [(c, co, half) for c in range(3) for co in range(CT) for half in range(2)]
    NTILE = len(tiles)
    NACC, NST = 3, 4
    STATS1_AFTER, STATS2_AFTER, TRANSPOSE_AFTER = 4, 6, (8, 8, 9, 9)

    with ExitStack() as ctx:
        sb = lambda name, shape, dt=F32: ctx.enter_context(nc.sbuf_tensor(name, shape, dt))
        sem = lambda name: ctx.enter_context(nc.semaphore(name))

        w_hi = sb("w_hi", [P, TAPS * CT, C], F16)
        w_lo = sb("w_lo", [P, TAPS * CT, C], F16)
        w_stage = sb("w_stage", [P, 2, CHUNK * CT, C])
        x_tok = sb("x_tok", [P, 2, NT, C])
        x_sq = sb("x_sq", [P, NT, C])
        x_hi = [[sb(f"x_hi{e}{ct}", [P, PH, PW], F16) for ct in range(CT)] for e in range(2)]
        x_lo = [[sb(f"x_lo{e}{ct}", [P, PH, PW], F16) for ct in range(CT)] for e in range(2)]
        group_part = sb("group_part", [P, 2, G])
        spread = sb("spread", [P, G])
        spread_inv = sb("spread_inv", [P, G])
        eps = sb("eps", [P, 1])
        bias = sb("bias", [P, 3, CT])
        bias_s = sb("bias_s", [P, 3, CT])
        mean_w = sb("mean_w", [P, P])
        ident_w = sb("ident_w", [P, P])
        out_stage = sb("out_stage", [P, NST, BANK])

        acc = [ctx.enter_context(nc.psum_tensor(f"acc{i}", [P, BANK], F32)) for i in range(NACC)]
        stat = ctx.enter_context(nc.psum_tensor("stat", [P, BANK], F32))
        turned = [ctx.enter_context(nc.psum_tensor(f"turned{i}", [P, BANK], F32)) for i in range(2)]

        consts_in = sem("consts_in")
        chunk_in = [sem("chunk_in0"), sem("chunk_in1")]
        chunk_hi = sem("chunk_hi")
        chunk_lo = sem("chunk_lo")
        x_in = [sem("x_in0"), sem("x_in1")]
        border_set = sem("border_set")
        bias_ready = sem("bias_ready")
        part_ready = sem("part_ready")
        stat_ready = sem("stat_ready")
        centred = sem("centred")
        squared = sem("squared")
        spread_ready = sem("spread_ready")
        inv_ready = sem("inv_ready")
        normed = sem("normed")
        turned_ready = sem("turned_ready")
        hi_ready = sem("hi_ready")
        lo_ready = sem("lo_ready")
        conv_done = sem("conv_done")
        staged = sem("staged")
        stored = [sem(f"stored{i}") for i in range(NST)]

        outs = (q_s, v_s, k_s)
        block = ctx.enter_context(nc.Block())

        def over_images(engine, body):
            with engine.Fori(0, B // 2 - 1) as i:
                body(2 * i, 0, True)
                body(2 * i + 1, 1, True)
            body(B - 2, 0, True)
            body(B - 1, 1, False)

        @block.sync
        def _(sp):
            sp.dma_start(x_tok[:, 0], x[0:N, :].rearrange("(t p) c -> p t c", p=P)).then_inc(x_in[0], 16)
            sp.dma_start(mean_w[:, :], mean_op).then_inc(consts_in, 16)
            sp.dma_start(ident_w[:, :], ident).then_inc(consts_in, 16)
            for i, b in enumerate((bq, bv, bk)):
                sp.dma_start(bias[:, i, :], b.rearrange("(a p) -> p a", p=P),
                             allow_slow_non_contiguous=True).then_inc(consts_in, 16)
            for n, (w, t0, taps, _) in enumerate(chunks):
                if n >= 2:
                    sp.wait_ge(chunk_hi, n - 1)
                    sp.wait_ge(chunk_lo, n - 1)
                sp.dma_start(w_stage[:, n % 2, 0:taps * CT],
                             w[t0 * C:(t0 + taps) * C, :].rearrange("(t p) c -> p t c", p=P)
                             ).then_inc(chunk_in[n % 2], 16)

            def image(b, e, more):
                if more:
                    wait(sp, lo_ready, 4 * b)
                    sp.dma_start(x_tok[:, 1 - e],
                                 x[bass.ds((b + 1) * N, N), :].rearrange("(t p) c -> p t c", p=P)
                                 ).then_inc(x_in[1 - e], 16)
                for n, (c, co, half) in enumerate(tiles):
                    sp.wait_ge(staged, NACC + NTILE * b + n + 1)
                    sp.dma_start(outs[c][bass.ds(b * C + co * P, P), half * BANK:(half + 1) * BANK],
                                 out_stage[:, n % NST]).then_inc(stored[n % NST], 16)
            over_images(sp, image)
            for s in stored:
                sp.wait_ge(s, 16 * B * NTILE // NST)

        @block.gpsimd
        def _(pool):
            for e in range(2):
                for ct in range(CT):
                    pool.memset(x_hi[e][ct][:, :, :], 0.0).then_inc(border_set, 1)
                    pool.memset(x_lo[e][ct][:, :, :], 0.0).then_inc(border_set, 1)
            pool.memset(eps[:, :], EPS / X_SCALE ** 2).then_inc(border_set, 1)

        def inside(pad, half):
            return pad[:, PAD + half * H // 2:PAD + (half + 1) * H // 2, PAD:PAD + W]

        def turned_image(t):
            return t[:, :].rearrange("p (h w) -> p h w", w=W)

        @block.vector
        def _(dve):
            def prepare(b, e):
                grouped = x_tok[:, e].rearrange("p t (g c) -> p g t c", g=G)
                tiled = x_tok[:, e].rearrange("p t (g c) -> p t g c", g=G)
                over = lambda s: s.unsqueeze(1).unsqueeze(3).broadcast_to([P, NT, G, CG])
                dve.wait_ge(x_in[e], 16 * (b // 2 + 1) if isinstance(b, int) else 16 * turn(b, e))
                dve.tensor_reduce(group_part[:, 0], grouped, AX.XY, ALU.add).then_inc(part_ready, 1)
                dve.wait_ge(stat_ready, 2 * b + 1)
                dve.tensor_tensor(tiled, tiled, over(stat[:, 0:G]), ALU.subtract).then_inc(centred, 1)
                dve.wait_ge(squared, b + 1)
                dve.tensor_reduce(group_part[:, 1], x_sq[:, :, :].rearrange("p t (g c) -> p g t c", g=G),
                                  AX.XY, ALU.add).then_inc(part_ready, 1)
                dve.wait_ge(spread_ready, b + 1)
                dve.reciprocal(spread_inv[:, :], spread[:, :]).then_inc(inv_ready, 1)
                dve.wait_ge(inv_ready, b + 1)
                dve.tensor_tensor(tiled, tiled, over(spread_inv[:, :]), ALU.mult).then_inc(normed, 1)
                for n in range(4):
                    ct, half = n // 2, n % 2
                    dve.wait_ge(hi_ready, 4 * b + n + 1)
                    dve.tensor_tensor(inside(x_lo[e][ct], half), turned_image(turned[n % 2]),
                                      inside(x_hi[e][ct], half), ALU.subtract).then_inc(lo_ready, 1)

            def turn(b, e):
                return (b - e) // 2 + 1

            dve.wait_ge(consts_in, 5 * 16)
            dve.tensor_scalar(bias_s[:, :, :], bias[:, :, :], QK_SCALE, None, ALU.mult).then_inc(bias_ready, 1)
            dve.wait_ge(border_set, 9)
            prepare(0, 0)
            for n, (_, _, taps, t0) in enumerate(chunks):
                dve.wait_ge(chunk_hi, n + 1)
                dve.scalar_tensor_tensor(w_lo[:, t0 * CT:(t0 + taps) * CT], w_stage[:, n % 2, 0:taps * CT],
                                         W_SCALE, w_hi[:, t0 * CT:(t0 + taps) * CT],
                                         ALU.mult, ALU.subtract).then_inc(chunk_lo, 1)

            def image(b, e, more):
                if more:
                    prepare(b + 1, 1 - e)
            over_images(dve, image)

        @block.scalar
        def _(act):
            def square(b, e):
                act.wait_ge(centred, b + 1)
                act.activation(x_sq[:, :, :], x_tok[:, e], ACT.Square).then_inc(squared, 1)

            def spread_of(b):
                act.wait_ge(stat_ready, 2 * b + 2)
                act.activation(spread[:, :], stat[:, G:2 * G], ACT.Sqrt, bias=eps[:, 0:1],
                               scale=X_SCALE ** -2).then_inc(spread_ready, 1)

            def high(b, e, n):
                ct, half = n // 2, n % 2
                act.wait_ge(turned_ready, 4 * b + n + 1)
                act.activation(inside(x_hi[e][ct], half), turned_image(turned[n % 2]),
                               ACT.Copy).then_inc(hi_ready, 1)

            act.wait_ge(border_set, 9)
            for n, (_, _, taps, t0) in enumerate(chunks):
                if n == 1:
                    square(0, 0)
                    spread_of(0)
                    for m in range(4):
                        high(0, 0, m)
                act.wait_ge(chunk_in[n % 2], 16 * (n // 2 + 1))
                act.activation(w_hi[:, t0 * CT:(t0 + taps) * CT], w_stage[:, n % 2, 0:taps * CT],
                               ACT.Copy, scale=W_SCALE).then_inc(chunk_hi, 1)
            act.wait_ge(bias_ready, 1)
            act.sem_inc(staged, NACC)

            def image(b, e, more):
                for n, (c, co, half) in enumerate(tiles):
                    act.wait_ge(conv_done, NTILE * b + n + 1)
                    wait(act, stored[n % NST], 16 * (NTILE // NST * b + n // NST))
                    src = bias if CONVS[c][0] == "v" else bias_s
                    scale = (1.0 if CONVS[c][0] == "v" else QK_SCALE) / (X_SCALE * W_SCALE)
                    act.activation(out_stage[:, n % NST], acc[n % NACC][:, :], ACT.Identity,
                                   bias=src[:, c, co:co + 1], scale=scale).then_inc(staged, 1)
                    if more:
                        if n == STATS1_AFTER:
                            square(b + 1, 1 - e)
                        if n == STATS2_AFTER:
                            spread_of(b + 1)
                        for m in range(4):
                            if n == TRANSPOSE_AFTER[m]:
                                high(b + 1, 1 - e, m)
            over_images(act, image)

        @block.tensor
        def _(pe):
            def stats(b, k):
                pe.wait_ge(part_ready, 2 * b + k + 1)
                if k == 0:
                    wait(pe, spread_ready, b)
                pe.matmul(stat[:, k * G:(k + 1) * G], mean_w[:, :], group_part[:, k],
                          start=True, stop=True).then_inc(stat_ready, 1)

            def transposes(b, e, n):
                ct, half = n // 2, n % 2
                pe.wait_ge(normed, b + 1)
                wait(pe, lo_ready, 4 * b + n - 1)
                for t in range(4):
                    m = pe.transpose(turned[n % 2][:, t * P:(t + 1) * P],
                                     x_tok[:, e, 4 * half + t, ct * P:(ct + 1) * P], ident_w[:, :])
                m.then_inc(turned_ready, 1)

            def conv_tile(b, e, n):
                c, co, half = tiles[n]
                name, side, base = CONVS[c]
                if co == 0 and half == 0:
                    pe.wait_ge(chunk_lo, chunks_of[name])
                pe.wait_ge(staged, NTILE * b + n + 1)
                r = PAD - side // 2
                for tap in range(side * side):
                    y = r + tap // side + half * H // 2
                    z = r + tap % side
                    for ct in range(CT):
                        k = (base + tap) * CT + ct
                        cols = slice(co * P, (co + 1) * P)
                        first = tap == 0 and ct == 0
                        last = tap == side * side - 1 and ct == CT - 1
                        hi = x_hi[e][ct][:, y:y + H // 2, z:z + W]
                        lo = x_lo[e][ct][:, y:y + H // 2, z:z + W]
                        pe.matmul(acc[n % NACC][:, :], w_hi[:, k, cols], hi, start=first, stop=False)
                        pe.matmul(acc[n % NACC][:, :], w_hi[:, k, cols], lo, start=False, stop=False)
                        m = pe.matmul(acc[n % NACC][:, :], w_lo[:, k, cols], hi, start=False, stop=last)
                m.then_inc(conv_done, 1)

            pe.wait_ge(consts_in, 5 * 16)
            stats(0, 0)
            stats(0, 1)
            for m in range(4):
                transposes(0, 0, m)

            def image(b, e, more):
                pe.wait_ge(lo_ready, 4 * b + 4)
                for n in range(NTILE):
                    conv_tile(b, e, n)
                    if more:
                        if n == STATS1_AFTER:
                            stats(b + 1, 0)
                        if n == STATS2_AFTER:
                            stats(b + 1, 1)
                        for m in range(4):
                            if n == TRANSPOSE_AFTER[m]:
                                transposes(b + 1, 1 - e, m)
            over_images(pe, image)


def attention_phase(nc, q_s, k_s, v_s, ident16, ident, heads_out):
    D2 = 4 * HD
    ROWS = D2 + 2
    K_ONE = 256.0
    NKT = 4
    NPT = 4
    VW = 32
    CH = 2
    CG4 = 4
    QW = N // CG4
    EXP_SCALE = HD ** -0.5 / QK_SCALE ** 2

    with ExitStack() as ctx:
        sb = lambda name, shape, dt=F32: ctx.enter_context(nc.sbuf_tensor(name, shape, dt))
        sem = lambda name: ctx.enter_context(nc.semaphore(name))
        pb = lambda name, shape, dt=F32: ctx.enter_context(nc.psum_tensor(name, shape, dt))

        raw = {c: [sb(f"raw_{c}{e}", [P, NT, HD]) for e in range(2)] for c in "qkv"}
        q_tok = [sb(f"q_tok{e}", [P, NT, ROWS], F16) for e in range(NKT)]
        k_tok = [sb(f"k_tok{e}", [P, NT, ROWS], F16) for e in range(NKT)]
        v_tok = [sb(f"v_tok{e}", [P, NT, VW]) for e in range(NKT)]
        k_t = [sb(f"k_t{e}", [ROWS, N], F16) for e in range(NKT)]
        qa_t = [sb(f"qa_t{e}", [ROWS, N], F16) for e in range(2)]
        qb_t = [sb(f"qb_t{e}", [ROWS, N], F16) for e in range(2)]
        probs = [sb(f"probs{e}", [P, N]) for e in range(NPT)]
        maxima = sb("maxima", [P, 2, NT, CH])
        neg_max = sb("neg_max", [P, NT])
        o_t = sb("o_t", [P, QW])
        inv_sum = sb("inv_sum", [P, 2, CG4])
        id16 = sb("id16", [P, P], F16)
        id32 = sb("id32", [P, P])

        a_bank = [pb(f"a_bank{i}", [P, BANK]) for i in range(2)]
        b_bank = [pb(f"b_bank{i}", [P, CH, BANK]) for i in range(2)]
        pv_bank = pb("pv_bank", [P, BANK])
        t_bank = pb("t_bank", [P, BANK])
        t16 = t_bank[:, :].bitcast(F16)

        consts_in = sem("a_consts_in")
        raw_in = {c: [sem(f"raw_in_{c}{e}") for e in range(2)] for c in "qkv"}
        pads_set = sem("pads_set")
        passed = sem("passed")
        hi_cut = sem("hi_cut")
        tok_ready = sem("tok_ready")
        k_turned = sem("k_turned")
        qa_turned = sem("qa_turned")
        qb_turned = sem("qb_turned")
        o_turned = sem("o_turned")
        k_ready = sem("k_ready")
        qa_ready = sem("qa_ready")
        qb_ready = sem("qb_ready")
        a_done = sem("a_done")
        a_read = sem("a_read")
        max_ready = sem("max_ready")
        neg_hi_cut = sem("neg_hi_cut")
        max_rows_set = sem("max_rows_set")
        b_done = sem("b_done")
        exp_done = sem("exp_done")
        pv_done = sem("pv_done")
        o_copied = sem("o_copied")
        inv_done = sem("inv_done")
        o_out = sem("o_out")

        A_AHEAD = 3
        K_STEP, O_STEP, QA_STEP, QB_STEP = 1, 2, 3, 6
        LEAD = 2

        def a_tile(h, t):
            t += A_AHEAD
            return h + 1 + t // NT, t % NT

        def over_heads(engine, body):
            exists = lambda x: 0 <= x < HEADS
            for h in range(-LEAD, 4):
                body(h, h % 4, exists)
            with engine.Fori(1, HEADS // 4 - 1) as i:
                for e in range(4):
                    body(4 * i + e, e, lambda x: True)
            for h in range(HEADS - 4, HEADS + 1):
                body(h, h % 4, exists)

        def there(exists, h, d):
            return exists(h + d) if isinstance(h, int) else True

        block = ctx.enter_context(nc.Block())

        @block.sync
        def _(sp):
            sp.dma_start(id16[:, :], ident16).then_inc(consts_in, 16)
            sp.dma_start(id32[:, :], ident).then_inc(consts_in, 16)

            def load(h, e):
                for c, src in (("q", q_s), ("k", k_s), ("v", v_s)):
                    wait(sp, tok_ready, h - 1)
                    sp.dma_start(raw[c][e % 2][:, :, :],
                                 src[bass.ds(h * HD, HD), :].rearrange("c (r t d) -> (c r) t d", t=NT, d=HD)
                                 ).then_inc(raw_in[c][e % 2], 16)
            for h in range(4):
                load(h, h % 4)
            with sp.Fori(1, HEADS // 4) as i:
                for e in range(4):
                    load(4 * i + e, e)

        @block.gpsimd
        def _(pool):
            for e in range(NKT):
                pool.memset(k_tok[e][:, :, D2:ROWS], K_ONE).then_inc(pads_set, 1)
                pool.memset(v_tok[e][:, :, HD:HD + 1], 1.0).then_inc(pads_set, 1)
                pool.memset(v_tok[e][:, :, HD + 1:VW], 0.0).then_inc(pads_set, 1)
            pool.wait_ge(pads_set, 3 * NKT)

            def cut(h, e):
                turn = 16 * (2 * h // 4 + 1) if isinstance(h, int) else None
                qv = q_tok[e][:, :, 0:D2].rearrange("p t (r l d) -> p t r l d", r=2, l=2)
                kv = k_tok[e][:, :, 0:D2].rearrange("p t (l r d) -> p t r l d", r=2, l=2)
                raws = {c: raw[c][e % 2][:, :, :].unsqueeze(2).broadcast_to([P, NT, 2, HD]) for c in "qk"}
                fills = (h - e % 2) // 2 + 1 if isinstance(h, int) else h_fills(h, e)
                wait(pool, qb_turned, h - NKT + 1)
                wait(pool, pv_done, NT * (h - NKT + 1))
                pool.wait_ge(raw_in["q"][e % 2], 16 * fills)
                pool.sem_inc(passed, 1)
                pool.memset(q_tok[e][:, :, D2:ROWS], 0.0)
                pool.tensor_copy(qv[:, :, :, 0], raws["q"]).then_inc(hi_cut, 1)
                pool.wait_ge(raw_in["k"][e % 2], 16 * fills)
                pool.sem_inc(passed, 1)
                pool.tensor_copy(kv[:, :, :, 0], raws["k"]).then_inc(hi_cut, 1)
                pool.wait_ge(raw_in["v"][e % 2], 16 * fills)
                pool.sem_inc(passed, 1)
                pool.tensor_copy(v_tok[e][:, :, 0:HD], raw["v"][e % 2][:, :, :])
                pool.wait_ge(hi_cut, 2 * h + 2)
                pool.tensor_tensor(qv[:, :, :, 1], raws["q"], qv[:, :, :, 0], ALU.subtract)
                pool.tensor_tensor(kv[:, :, :, 1], raws["k"], kv[:, :, :, 0], ALU.subtract).then_inc(tok_ready, 1)

            def h_fills(h, e):
                return (h - e) // 2 + e // 2 + 1

            for h in range(4):
                cut(h, h % 4)
            with pool.Fori(1, HEADS // 4) as i:
                for e in range(4):
                    cut(4 * i + e, e)

        @block.tensor
        def _(pe):
            pe.wait_ge(consts_in, 32)

            def turn_tokens(tok, done):
                for t in range(NT):
                    m = pe.transpose(t16[0:ROWS, t * P:(t + 1) * P], tok[:, t, :], id16[:, :])
                m.then_inc(done, 1)

            def scores_a(h, e, t):
                if t == 0:
                    pe.wait_ge(k_ready, h + 1)
                    pe.wait_ge(qa_ready, h + 1)
                for c in range(CH):
                    wait(pe, a_read, (h * NT + t) * CH + c - 1)
                    pe.matmul(a_bank[c][:, :], qa_t[e % 2][:, t * P:(t + 1) * P],
                              k_t[e][:, c * BANK:(c + 1) * BANK], start=True, stop=True).then_inc(a_done, 1)

            def scores_b(h, e, t):
                if t == 0:
                    pe.wait_ge(qb_ready, h + 1)
                wait(pe, exp_done, h * NT + t - 1)
                for c in range(CH):
                    m = pe.matmul(b_bank[t % 2][:, c, :], k_t[e][:, t * P:(t + 1) * P],
                                  qb_t[e % 2][:, c * BANK:(c + 1) * BANK], start=True, stop=True)
                m.then_inc(b_done, 1)

            def times_v(h, e, t):
                if t == 0:
                    wait(pe, o_copied, h)
                pe.wait_ge(exp_done, h * NT + t + 1)
                for j in range(CG4):
                    m = pe.matmul(pv_bank[VW * j:VW * (j + 1), 0:QW], v_tok[e][:, t, :],
                                  probs[t % NPT][:, j * QW:(j + 1) * QW], start=(t == 0), stop=(t == NT - 1),
                                  tile_position=(0, VW * j))
                m.then_inc(pv_done, 1)

            def head(h, e, exists):
                ok = lambda d: there(exists, h, d)
                for t in range(NT):
                    if ok(0):
                        scores_b(h, e, t)
                    if t == 0 and ok(-1):
                        times_v(h - 1, (e - 1) % 4, NT - 1)
                    if t > 0 and ok(0):
                        times_v(h, e, t - 1)
                    d = 1 + (t + A_AHEAD) // NT
                    if ok(d):
                        scores_a(h + d, (e + d) % 4, (t + A_AHEAD) % NT)
                    if t == K_STEP and ok(LEAD):
                        pe.wait_ge(tok_ready, h + LEAD + 1)
                        wait(pe, qb_ready, h + 1)
                        turn_tokens(k_tok[(e + LEAD) % 4], k_turned)
                    if t == O_STEP and ok(-1):
                        wait(pe, k_ready, min_heads(h + LEAD + 1))
                        pe.wait_ge(o_copied, h)
                        for i in range(2):
                            m = pe.transpose(t_bank[:, i * P:(i + 1) * P], o_t[:, i * P:(i + 1) * P], id32[:, :])
                        m.then_inc(o_turned, 1)
                    if t == QA_STEP and ok(LEAD):
                        wait(pe, o_out, h)
                        wait(pe, k_ready, h + LEAD + 1)
                        turn_tokens(q_tok[(e + LEAD) % 4], qa_turned)
                    if t == QB_STEP and ok(1):
                        pe.wait_ge(max_rows_set, h + 2)
                        wait(pe, qa_ready, min_heads(h + LEAD + 1))
                        wait(pe, o_out, h)
                        turn_tokens(q_tok[(e + 1) % 4], qb_turned)

            def min_heads(v):
                return min(v, HEADS) if isinstance(v, int) else v

            over_heads(pe, head)

        @block.scalar
        def _(act):
            def head(h, e, exists):
                ok = lambda d: there(exists, h, d)
                for t in range(NT):
                    if ok(0):
                        act.wait_ge(b_done, h * NT + t + 1)
                        wait(act, pv_done, h * NT + t - NPT + 1)
                        act.activation(probs[t % NPT][:, :], b_bank[t % 2][:, :, :].rearrange("p c n -> p (c n)"),
                                       ACT.Exp, scale=EXP_SCALE).then_inc(exp_done, 1)
                    if t == K_STEP and ok(LEAD):
                        act.wait_ge(k_turned, h + LEAD + 1)
                        act.activation(k_t[(e + LEAD) % 4][:, :], t16[0:ROWS, :], ACT.Copy).then_inc(k_ready, 1)
                    if t == QA_STEP and ok(LEAD):
                        act.wait_ge(qa_turned, h + LEAD + 1)
                        act.activation(qa_t[e % 2][:, :], t16[0:ROWS, :], ACT.Copy).then_inc(qa_ready, 1)
            over_heads(act, head)

        @block.vector
        def _(dve):
            def maximum(h, e):
                dve.wait_ge(a_read, (h + 1) * NT * CH)
                dve.tensor_reduce(neg_max[:, :], maxima[:, e % 2], AX.X, ALU.max, negate=True).then_inc(max_ready, 1)
                dve.wait_ge(max_ready, h + 1)
                hi = q_tok[e][:, :, D2:D2 + 1].rearrange("p t o -> p (t o)")
                lo = q_tok[e][:, :, D2 + 1:ROWS].rearrange("p t o -> p (t o)")
                dve.tensor_scalar(hi, neg_max[:, :], 1 / K_ONE, None, ALU.mult).then_inc(neg_hi_cut, 1)
                dve.wait_ge(neg_hi_cut, h + 1)
                dve.scalar_tensor_tensor(lo, neg_max[:, :], 1 / K_ONE, hi, ALU.mult,
                                         ALU.subtract).then_inc(max_rows_set, 1)

            def head(h, e, exists):
                ok = lambda d: there(exists, h, d)
                for t in range(NT):
                    d = 1 + (t + A_AHEAD) // NT
                    ta = (t + A_AHEAD) % NT
                    if ok(d):
                        for c in range(CH):
                            dve.wait_ge(a_done, ((h + d) * NT + ta) * CH + c + 1)
                            dve.tensor_reduce(maxima[:, (e + d) % 2, ta, c:c + 1], a_bank[c][:, :], AX.X,
                                              ALU.max).then_inc(a_read, 1)
                        if ta == NT - 1:
                            maximum(h + d, (e + d) % 4)
                    if t == 0 and ok(-1):
                        dve.wait_ge(pv_done, h * NT)
                        dve.tensor_copy(o_t[:, :], pv_bank[:, 0:QW]).then_inc(o_copied, 1)
                    if t == O_STEP and ok(-1):
                        dve.wait_ge(o_turned, h)
                        o = t_bank[:, 0:QW].rearrange("p (i j w) -> p i j w", i=2, w=VW)
                        dve.reciprocal(inv_sum[:, :, :], o[:, :, :, HD]).then_inc(inv_done, 1)
                        dve.wait_ge(inv_done, h)
                        dst = heads_out[:, :, bass.ds(h - 1, 1), :]
                        dve.tensor_tensor(dst.rearrange("p (j i) o d -> p (i o) j d", i=2),
                                          o[:, :, :, 0:HD],
                                          inv_sum[:, :, :].unsqueeze(3).broadcast_to([P, 2, CG4, HD]),
                                          ALU.mult).then_inc(o_out, 1)
                    if t == QB_STEP and ok(1):
                        dve.wait_ge(qb_turned, h + 2)
                        dve.tensor_copy(qb_t[(e + 1) % 2][:, :], t16[0:ROWS, :]).then_inc(qb_ready, 1)
            over_heads(dve, head)


def band_matrices(size):
    dec_lo = np.array([
        -0.00011747678400228192, 0.0006754494059985568, -0.0003917403729959771, -0.00487035299301066,
        0.008746094047015655, 0.013981027917015516, -0.04408825393106472, -0.01736930100202211,
        0.128747426620186, 0.00047248457399797254, -0.2840155429624281, -0.015829105256023893,
        0.5853546836548691, 0.6756307362980128, 0.3128715909144659, 0.05441584224308161], dtype=np.float64)
    taps = len(dec_lo)
    both = (dec_lo[::-1], dec_lo * (-1.0) ** np.arange(taps))
    m = np.zeros((2, size // 2, size + taps - 2))
    for band in range(2):
        for i in range(size // 2):
            m[band, i, 2 * i:2 * i + taps] = both[band]
    half = taps // 2
    return m[:, :, half - 1:-(half - 1)].astype(np.float32)


LEVELS = 3
TL = [16, 8, 4]
DL = [128, 64, 32]
DB = [8, 16, 32]
NB = [16, 4, 1]
DELTAS = range(-1, 5)


def wavelet_constants():
    def block(tm, dm, t_in, d_in, t_out, d_out, rev_in, rev_out):
        m = np.einsum("tT,dD->tdTD", tm, dm[d_in][:, d_out])
        m = m.reshape(P, P)
        if rev_in:
            m = m[::-1]
        if rev_out:
            m = m[:, ::-1]
        return np.ascontiguousarray(m)
    w = {n: band_matrices(n) for n in (8, 16, 32, 64, 128, 256)}
    bands = [(bt, bd) for bt in range(2) for bd in range(2)]
    out = {}
    eye4 = np.eye(4, dtype=np.float32)
    out["t_op"] = np.einsum("bih,wv->hwbiv", w[32], eye4).reshape(P, P)
    out["t_inv"] = np.einsum("bih,wv->biwhv", w[32][:, ::-1], eye4).reshape(P, P)
    out["d_op"] = w[256].transpose(2, 0, 1).reshape(CT, P, 2, P).transpose(1, 0, 2, 3).reshape(P, -1)
    rev = w[256].reshape(2, NB[0], DB[0], C)[:, :, ::-1].reshape(2, P, C)
    out["d_inv"] = rev.transpose(2, 0, 1).reshape(CT, P, 2, P).transpose(1, 0, 2, 3).reshape(P, -1)
    sl = lambda k, n: slice(k * n, (k + 1) * n)
    out["dwt1"] = np.concatenate([
        block(w[16][bt].T, w[128][bd].T, None, sl(4 + e, 8), None, sl(1, 16), True, False)
        for bt, bd in bands for e in DELTAS], 1)
    out["dwt2"] = np.concatenate([
        block(w[8][bt].T, w[64][bd].T, None, sl(k, 16), None, sl(0, 32), True, False)
        for bt, bd in bands for k in range(4)], 1)
    out["inv2"] = np.concatenate([
        block(w[8][bt], w[64][bd], None, sl(0, 32), None, sl(k, 16), True, True)
        for bt, bd in bands for k in range(4)], 1)
    out["inv1"] = np.concatenate([
        block(w[16][bt], w[128][bd], None, sl(1, 16), None, sl(4 + e, 8), True, True)
        for bt, bd in bands for e in DELTAS], 1)
    return {k: np.ascontiguousarray(v, dtype=np.float32) for k, v in out.items()}


KS = 11
KROWS, KCOLS = 31, 64
KY0, KX0 = 10, 26


def analysis_phase(nc, x, heads_out, wp, mean_op, ident, t_op, d_op, kernels, biases,
                   conv_ops, conv_bias, ktab_s, x1_s, bands_s):
    with ExitStack() as ctx:
        sb = lambda name, shape, dt=F32: ctx.enter_context(nc.sbuf_tensor(name, shape, dt))
        sem = lambda name: ctx.enter_context(nc.semaphore(name))
        pb = lambda name, shape, dt=F32: ctx.enter_context(nc.psum_tensor(name, shape, dt))

        bands = sb("bands", [P, 2, 2 * TL[0], C])
        o_in = [sb(f"o_in{e}", [P, NT, C]) for e in range(2)]
        x1 = [sb(f"x1_{e}", [P, NT, C]) for e in range(2)]
        xc = sb("xc", [P, NT, C])
        xn = sb("xn", [P, NT, C])
        o_t = sb("o_turned_sb", [P, CT, NT, P])
        rows = sb("rows", [P, CT, NT, P])
        sq = rows[:, :, :, :].rearrange("p k t n -> p (k t n)").rearrange("p (t c) -> p t c", c=C)
        wp_w = sb("wp_w", [P, CT, C])
        t_w = sb("t_w", [P, P])
        d_w = sb("d_w", [P, CT, 2, P])
        mean_w = sb("mean_w2", [P, P])
        id32 = sb("id32b", [P, P])
        group_part = sb("group_part2", [P, 2, G])
        spread = sb("spread2", [P, G])
        spread_inv = sb("spread_inv2", [P, G])
        eps = sb("eps2", [P, 1])
        ktab6 = sb("ktab6", [KS, 6, KS])
        kmean = sb("kmean", [KS, KS])
        ktab = sb("ktab", [KROWS, KCOLS])
        bias6 = sb("bias6", [P, 6])

        turned = [pb(f"turned2{i}", [P, BANK]) for i in range(2)]
        proj = [pb(f"proj{i}", [P, BANK]) for i in range(2)]
        cols = [pb(f"cols{i}", [P, BANK]) for i in range(2)]
        stat = pb("stat2", [P, BANK])

        consts_in = sem("f_consts_in")
        heads_in = [sem(f"heads_in{e}") for e in range(2)]
        x_in = [sem(f"x_in2{e}") for e in range(2)]
        eps_set = sem("eps_set")
        o_turned = sem("o_turned2")
        o_sb = sem("o_sb")
        proj_done = sem("proj_done")
        x1_done = sem("x1_done")
        x1_stored = [sem(f"x1_stored{e}") for e in range(2)]
        part_ready = sem("part_ready2")
        stat_ready = sem("stat_ready2")
        centred = sem("centred2")
        squared = sem("squared2")
        spread_ready = sem("spread_ready2")
        inv_ready = sem("inv_ready2")
        normed = sem("normed2")
        rows_done = sem("rows_done")
        rows_sb = sem("rows_sb")
        cols_done = sem("cols_done")
        cols_sb = sem("cols_sb")
        bands_stored = sem("bands_stored")
        k_zero = sem("k_zero")
        k_in = sem("k_in")
        k_step = sem("k_step")
        k_out = sem("k_out")
        ops_in = sem("ops_in")
        b_step = sem("b_step")

        block = ctx.enter_context(nc.Block())

        def over_images(engine, front, back):
            front(0, 0)
            with engine.Fori(0, B // 2 - 1) as i:
                for e in (1, 0):
                    front(2 * i + 2 - e, e)
                    back(2 * i + 1 - e, 1 - e)
            front(B - 1, 1)
            back(B - 2, 0)
            back(B - 1, 1)

        @block.sync
        def _(sp):
            for dst, src in ((wp_w[:, :, :], wp.rearrange("(k p) o -> p k o", p=P)), (id32[:, :], ident),
                             (mean_w[:, :], mean_op), (t_w[:, :], t_op),
                             (d_w[:, :, :, :].rearrange("p a b c -> p (a b c)"), d_op)):
                sp.dma_start(dst, src).then_inc(consts_in, 16)

            def front(b, e):
                wait(sp, o_turned, 4 * (b - 1))
                sp.dma_start(o_in[e][:, :, :].rearrange("p t (h d) -> p t h d", d=HD),
                             heads_out[:, :, bass.ds(b * NH, NH), :]).then_inc(heads_in[e], 16)
                wait(sp, centred, b - 1)
                wait(sp, x1_stored[e], 16 * ((b - e) // 2))
                sp.dma_start(x1[e][:, :, :], x[bass.ds(b * N, N), :].rearrange("(p t) c -> p t c", t=NT)
                             ).then_inc(x_in[e], 16)
                if isinstance(b, int) and b == 0:
                    return
                store(b - 1, 1 - e)

            def store(b, e):
                sp.wait_ge(x1_done, 4 * b + 4)
                sp.dma_start(x1_s[bass.ds(b * N, N), :].rearrange("(p t) c -> p t c", t=NT),
                             x1[e][:, :, :]).then_inc(x1_stored[e], 16)
            over_images(sp, front, lambda b, e: None)
            store(B - 1, 1)
            sp.wait_ge(cols_sb, 4 * B)
            for bt, bd in ((1, 1), (0, 0), (0, 1), (1, 0)):
                sp.dma_start(bands_s[2 * bt + bd].rearrange("i d m -> d i m"),
                             bands[:, bd, bt * TL[0]:(bt + 1) * TL[0], :]).then_inc(bands_stored, 16)
            sp.wait_ge(bands_stored, 64)
            for e in range(2):
                sp.wait_ge(x1_stored[e], 16 * B // 2)

        @block.gpsimd
        def _(pool):
            pool.memset(eps[:, :], EPS).then_inc(eps_set, 1)
            pool.memset(ktab6[:, :, :], 0.0).then_inc(k_zero, 1)
            pool.memset(ktab[:, :], 0.0).then_inc(k_zero, 1)
            pool.wait_ge(k_zero, 2)
            pool.dma_start(ktab_s.rearrange("o (y x) -> (o y) x", x=KCOLS), ktab[:, :]).then_inc(k_out, 16)
            for n, (kern, bias) in enumerate(zip(kernels, biases)):
                r = KS // 2
                pool.dma_start(ktab6[r - n:r + n + 1, n, r - n:r + n + 1], kern.rearrange("o y x -> (o y) x")).then_inc(k_in, 16)
                pool.dma_start(bias6[:, n:n + 1], bias.unsqueeze(0).broadcast_to([P, 1])).then_inc(k_in, 16)
            pool.wait_ge(k_in, 16 * 12)
            for n in range(1, 6):
                pool.tensor_tensor(ktab6[:, 0], ktab6[:, 0], ktab6[:, n], ALU.add).then_inc(k_step, 1)
                pool.tensor_tensor(bias6[:, 0:1], bias6[:, 0:1], bias6[:, n:n + 1], ALU.add).then_inc(b_step, 1)
                pool.wait_ge(k_step, n)
                pool.wait_ge(b_step, n)
            pool.tensor_scalar(kmean[:, :], ktab6[:, 0], 1 / 6, None, ALU.mult).then_inc(k_step, 1)
            pool.tensor_scalar(conv_bias[:, :], bias6[:, 0:1], 1 / 6, None, ALU.mult).then_inc(b_step, 1)
            pool.wait_ge(k_step, 6)
            pool.wait_ge(b_step, 6)
            pool.wait_ge(k_out, 16)
            pool.dma_start(ktab_s.rearrange("o (y x) -> (o y) x", x=KCOLS)[KY0:KY0 + KS, KX0:KX0 + KS],
                           kmean[:, :]).then_inc(k_out, 16)
            pool.wait_ge(k_out, 32)
            n = 0
            for level in range(LEVELS):
                t, nd = TL[level], DB[level]
                for k, op in enumerate(conv_ops[level]):
                    delta = k - len(conv_ops[level]) // 2
                    for i in range(t):
                        at = (i + KY0 + 6 - t) * KCOLS + KX0 + KS // 2 - (nd - 1) + nd * delta
                        src = bass.AP(tensor=ktab_s.tensor, offset=at, ap=[[1, nd], [KCOLS, t], [1, nd]])
                        pool.dma_start(op[i * nd:(i + 1) * nd, :].rearrange("p (i d) -> p i d", d=nd),
                                       src).then_inc(ops_in, 16)
                        n += 1
            pool.wait_ge(ops_in, 16 * n)

        @block.tensor
        def _(pe):
            pe.wait_ge(consts_in, 5 * 16)

            def front(b, e):
                pe.wait_ge(heads_in[e], 16 * ((b - e) // 2 + 1))
                for n in range(4):
                    kt, half = n // 2, n % 2
                    wait(pe, o_sb, bank_free(b, n))
                    if n == 0:
                        wait(pe, rows_sb, 4 * (b - 1))
                    for t in range(4):
                        m = pe.transpose(turned[n % 2][:, t * P:(t + 1) * P],
                                         o_in[e][:, 4 * half + t, kt * P:(kt + 1) * P], id32[:, :])
                    m.then_inc(o_turned, 1)
                for n in range(4):
                    pe.wait_ge(o_sb, 4 * b + 4)
                    wait(pe, x1_done, bank_free(b, n))
                    for t in range(2):
                        for kt in range(CT):
                            m = pe.matmul(proj[n % 2][:, t * C:(t + 1) * C], o_t[:, kt, 2 * n + t, :],
                                          wp_w[:, kt, :], start=(kt == 0), stop=(kt == CT - 1))
                    m.then_inc(proj_done, 1)
                stats(b, 0)

            def stats(b, k):
                pe.wait_ge(part_ready, 2 * b + k + 1)
                if k == 0:
                    wait(pe, spread_ready, b)
                pe.matmul(stat[:, k * G:(k + 1) * G], mean_w[:, :], group_part[:, k],
                          start=True, stop=True).then_inc(stat_ready, 1)

            def rows_of(b, e):
                pe.wait_ge(normed, b + 1)
                for n in range(4):
                    ch, half = n // 2, n % 2
                    if n == 0:
                        wait(pe, o_sb, 4 * min(b + 2, B) if isinstance(b, int) else 4 * b + 8)
                    wait(pe, rows_sb, bank_free(b, n))
                    for t in range(4):
                        m = pe.matmul(turned[n % 2][:, t * P:(t + 1) * P],
                                      xn[:, 4 * half + t, ch * P:(ch + 1) * P], t_w[:, :],
                                      start=True, stop=True)
                    m.then_inc(rows_done, 1)

            def back(b, e):
                rows_of(b, e)
                if not (isinstance(b, int) and b == B - 1):
                    stats(b + 1, 1)
                for n in range(4):
                    bd, half = n // 2, n % 2
                    pe.wait_ge(rows_sb, 4 * b + 4)
                    wait(pe, cols_sb, bank_free(b, n))
                    for ch in range(CT):
                        m = pe.matmul(cols[n % 2][:, :], d_w[:, ch, bd, :],
                                      rows[:, ch, 4 * half:4 * half + 4, :].rearrange("p t n -> p (t n)"),
                                      start=(ch == 0), stop=(ch == CT - 1))
                    m.then_inc(cols_done, 1)

            def first_front(b, e):
                front(b, e)
                if isinstance(b, int) and b == 0:
                    stats(0, 1)
            over_images(pe, first_front, back)

        @block.scalar
        def _(act):
            act.wait_ge(eps_set, 1)

            def front(b, e):
                for n in range(4):
                    kt, half = n // 2, n % 2
                    act.wait_ge(o_turned, 4 * b + n + 1)
                    if n == 0:
                        wait(act, proj_done, 4 * b)
                    act.activation(o_t[:, kt, 4 * half:4 * half + 4, :].rearrange("p t n -> p (t n)"),
                                   turned[n % 2][:, :], ACT.Copy).then_inc(o_sb, 1)
                act.wait_ge(centred, b + 1)
                wait(act, cols_done, 4 * (b - 1))
                act.activation(sq, xc[:, :, :], ACT.Square).then_inc(squared, 1)
                if isinstance(b, int) and b == 0:
                    spread_of(0)

            def spread_of(b):
                act.wait_ge(stat_ready, 2 * b + 2)
                act.activation(spread[:, :], stat[:, G:2 * G], ACT.Sqrt, bias=eps[:, 0:1]).then_inc(spread_ready, 1)

            def back(b, e):
                for n in range(4):
                    ch, half = n // 2, n % 2
                    act.wait_ge(rows_done, 4 * b + n + 1)
                    if n == 0:
                        wait(act, cols_done, 4 * b)
                        wait(act, part_ready, min(2 * b + 4, 2 * B) if isinstance(b, int) else 2 * b + 4)
                    act.activation(rows[:, ch, 4 * half:4 * half + 4, :].rearrange("p t n -> p (t n)"),
                                   turned[n % 2][:, :], ACT.Copy).then_inc(rows_sb, 1)
                if not (isinstance(b, int) and b == B - 1):
                    spread_of(b + 1)
                for n in range(4):
                    bd, half = n // 2, n % 2
                    act.wait_ge(cols_done, 4 * b + n + 1)
                    dst = bands[:, bd, :, bass.ds(b * W, W)].rearrange("p r (w t) -> p t r w", t=NT)
                    act.activation(dst[:, 4 * half:4 * half + 4],
                                   cols[n % 2][:, :].rearrange("p (t r w) -> p t r w", t=4, w=4),
                                   ACT.Copy).then_inc(cols_sb, 1)
            over_images(act, front, back)

        @block.vector
        def _(dve):
            over = lambda s: s.unsqueeze(1).unsqueeze(3).broadcast_to([P, NT, G, CG])
            tiled = lambda s: s[:, :, :].rearrange("p t (g c) -> p t g c", g=G)

            def group_sum(src, k):
                dve.tensor_reduce(group_part[:, k], src.rearrange("p t (g c) -> p g t c", g=G),
                                  AX.XY, ALU.add).then_inc(part_ready, 1)

            def front(b, e):
                dve.wait_ge(x_in[e], 16 * ((b - e) // 2 + 1))
                for n in range(4):
                    dve.wait_ge(proj_done, 4 * b + n + 1)
                    part = x1[e][:, 2 * n:2 * n + 2, :].rearrange("p t c -> p (t c)")
                    dve.tensor_tensor(part, proj[n % 2][:, :], part, ALU.add).then_inc(x1_done, 1)
                dve.wait_ge(x1_done, 4 * b + 4)
                group_sum(x1[e][:, :, :], 0)
                dve.wait_ge(stat_ready, 2 * b + 1)
                wait(dve, normed, b)
                wait(dve, squared, b)
                dve.tensor_tensor(tiled(xc), tiled(x1[e]), over(stat[:, 0:G]), ALU.subtract).then_inc(centred, 1)
                dve.wait_ge(squared, b + 1)
                group_sum(sq, 1)
                if isinstance(b, int) and b == 0:
                    scale(0)

            def scale(b):
                dve.wait_ge(spread_ready, b + 1)
                dve.reciprocal(spread_inv[:, :], spread[:, :]).then_inc(inv_ready, 1)
                dve.wait_ge(inv_ready, b + 1)
                wait(dve, rows_done, 4 * b)
                dve.tensor_tensor(tiled(xn), tiled(xc), over(spread_inv[:, :]), ALU.mult).then_inc(normed, 1)

            def back(b, e):
                if not (isinstance(b, int) and b == B - 1):
                    scale(b + 1)
            over_images(dve, front, back)


def bands_phase(nc, bands_s, conv_ops, conv_bias, ident, dwt1, dwt2, inv2, inv1, synth_s):
    LL, LH, HL, HH = range(4)
    HIGH = (HH, LH, HL)
    IM = C
    HALF = IM // P
    ROUNDS = [d // 16 for d in DL]
    NMM, NST = 4, 4
    THR = -float(np.sqrt(2.0 * np.log(32.0)) / 0.6745)

    with ExitStack() as ctx:
        sb = lambda name, shape, dt=F32: ctx.enter_context(nc.sbuf_tensor(name, shape, dt))
        sem = lambda name: ctx.enter_context(nc.semaphore(name))
        pb = lambda name, shape, dt=F32: ctx.enter_context(nc.psum_tensor(name, shape, dt))

        raw = [sb(f"raw_l{v}", [P, 4, NB[v], IM]) for v in range(LEVELS)]
        ll0 = sb("ll0", [P, NB[0], IM])
        done = [None, sb("done_l1", [P, 4, NB[1], IM]), sb("done_l2", [P, 4, NB[2], IM])]
        ll1 = sb("ll1", [P, NB[1], IM])
        keys = sb("keys", [P, HALF, TL[0] * DL[0]])
        eight = sb("eight", [P, HALF * TL[0], 8])
        thr_rows = sb("thr_rows", [P, HALF, P])
        clipped = sb("clipped", [P, 2, 4, IM])
        stage = sb("stage", [P, NST, 2, IM])
        id32 = sb("id32c", [P, P])
        w_dwt1 = sb("w_dwt1", [P, 4, len(DELTAS), P])
        w_dwt2 = sb("w_dwt2", [P, 4, NB[1], P])
        w_inv2 = sb("w_inv2", [P, 4, NB[1], P])
        w_inv1 = sb("w_inv1", [P, 4, len(DELTAS), P])

        mm = [pb(f"mm{i}", [P, 2, IM]) for i in range(NMM)]
        kbank = [pb(f"kbank{i}", [P, BANK]) for i in range(2)]
        thr = pb("thr", [P, BANK])

        raw_in = [sem(f"raw_in{b}") for b in range(4)]
        w_in = {n: sem("in_" + n) for n in ("id", "dwt1", "dwt2", "inv2", "inv1")}
        key_done = sem("key_done")
        key_read = sem("key_read")
        keys_set = sem("keys_set")
        med = sem("med")
        thr_rows_set = sem("thr_rows_set")
        thr_done = sem("thr_done")
        low_cut = sem("low_cut")
        clip_done = sem("clip_done")
        soft_done = sem("soft_done")
        mm_done = sem("mm_done")
        mm_read = sem("mm_read")
        stored = [sem(f"synth_stored{i}") for i in range(NST)]

        plan = [("conv", 0, LL, q) for q in range(8)]
        plan += [("dwt", 1, b, q) for b in (HH, LL, LH, HL) for q in range(2)]
        plan += [("conv", 1, LL, q) for q in range(2)]
        plan += [("dwt", 2, 2 * q, q) for q in range(2)]
        plan += [("conv", 0, b, q) for b in HIGH for q in range(8)]
        plan += [("conv", 1, b, q) for b in HIGH for q in range(2)]
        plan += [("conv", 2, 2 * q, q) for q in range(2)]
        plan += [("inv", 1, LL, q) for q in range(2)]
        plan += [("inv", 0, LL, q) for q in range(8)]
        number = {p: n for n, p in enumerate(plan)}
        staged = [n for n, p in enumerate(plan) if p[1] == 0 and (p[0] == "inv" or p[2] != LL)]
        stage_no = {n: s for s, n in enumerate(staged)}
        cuts = [(0, b, k, 4) for b in HIGH for k in range(0, 16, 4)]
        cuts += [(1, b, 0, 4) for b in HIGH] + [(2, LH, 0, 3)]
        cut_no = {c: n for n, c in enumerate(cuts)}
        key_banks = [8, 2, 1]
        keys_before = [0, 8, 10]

        block = ctx.enter_context(nc.Block())

        @block.sync
        def _(sp):
            def load_band(b):
                for i in range(TL[0]):
                    sp.dma_start(raw[0][i * DB[0]:(i + 1) * DB[0], b],
                                 bands_s[b, i].rearrange("(k d) m -> d k m", d=DB[0])).then_inc(raw_in[b], 16)
            sp.dma_start(id32[:, :], ident).then_inc(w_in["id"], 16)
            load_band(HH)
            load_band(LL)
            for n, (t, src) in (("dwt1", (w_dwt1, dwt1)), ("dwt2", (w_dwt2, dwt2))):
                sp.dma_start(t[:, :, :, :].rearrange("p a b c -> p (a b c)"), src).then_inc(w_in[n], 16)
            load_band(LH)
            load_band(HL)
            for n, (t, src) in (("inv2", (w_inv2, inv2)), ("inv1", (w_inv1, inv1))):
                sp.dma_start(t[:, :, :, :].rearrange("p a b c -> p (a b c)"), src).then_inc(w_in[n], 16)
            for s, n in enumerate(staged):
                _, _, band, q = plan[n]
                sp.wait_ge(mm_read, n + 1)
                sp.dma_start(synth_s[band, :, 2 * q:2 * q + 2, :], stage[:, s % NST]).then_inc(stored[s % NST], 16)
            for s in stored:
                sp.wait_ge(s, 16 * len(staged) // NST)

        @block.tensor
        def _(pe):
            def turn_keys(v):
                src = raw[v][:, HH]
                n = keys_before[v]
                jobs = {0: [(h, range(4 * g, 4 * g + 4)) for h in range(HALF) for g in range(4)],
                        1: [(h, range(4)) for h in range(HALF)], 2: [(None, None)]}[v]
                if v == 0:
                    pe.wait_ge(raw_in[HH], 16 * TL[0])
                    pe.wait_ge(w_in["id"], 16)
                else:
                    pe.wait_ge(mm_read, number[("dwt", v, HH if v == 1 else HL, 1)] + 1)
                for h, blocks in jobs:
                    wait(pe, key_read, n - 1)
                    if v == 2:
                        pieces = [(src[:, 0, hh * P:(hh + 1) * P]) for hh in range(HALF)]
                    else:
                        pieces = [src[:, k, h * P:(h + 1) * P] for k in blocks]
                    for j, piece in enumerate(pieces):
                        m = pe.transpose(kbank[n % 2][:, j * P:(j + 1) * P], piece, id32[:, :])
                    m.then_inc(key_done, 1)
                    n += 1

            def spread_thr(v):
                pe.wait_ge(thr_rows_set, v + 1)
                if v:
                    pe.wait_ge(low_cut, {1: 12, 2: 15}[v])
                for h in range(HALF):
                    m = pe.matmul(thr[:, h * P:(h + 1) * P], thr_rows[:, h, :], id32[:, :], start=True, stop=True)
                m.then_inc(thr_done, 1)

            def conv(v, band, q, bank):
                if v == 2:
                    if band:
                        pe.wait_ge(soft_done, len(cuts))
                    else:
                        pe.wait_ge(soft_done, len(cuts))
                    return pe.matmul(bank[:, :, :], conv_ops[2][0][:, :], raw[2][:, band:band + 2, 0, :],
                                     start=True, stop=True)
                if band == LL:
                    if v == 0:
                        pe.wait_ge(raw_in[LL], 16 * TL[0])
                    else:
                        pe.wait_ge(mm_read, number[("dwt", 1, LL, 1)] + 1)
                else:
                    k = min((2 * q + 2) // 4 * 4, NB[v] - 4)
                    pe.wait_ge(soft_done, cut_no[(v, band, k, 4)] + 1)
                src = raw[v][:, band]
                m = pe.matmul(bank[:, :, :], conv_ops[v][1][:, :], src[:, 2 * q:2 * q + 2, :], start=True, stop=False)
                lo, hi = (1 if q == 0 else 0), (1 if 2 * q + 2 == NB[v] else 2)
                m = pe.matmul(bank[:, lo:2, :], conv_ops[v][0][:, :], src[:, 2 * q - 1 + lo:2 * q + 1, :],
                              start=False, stop=False)
                return pe.matmul(bank[:, 0:hi, :], conv_ops[v][2][:, :], src[:, 2 * q + 1:2 * q + 1 + hi, :],
                                 start=False, stop=True)

            def dwt(v, band, q, bank):
                if v == 2:
                    pe.wait_ge(w_in["dwt2"], 16)
                    pe.wait_ge(mm_read, number[("conv", 1, LL, 1)] + 1)
                    for b in range(2):
                        for k in range(NB[1]):
                            m = pe.matmul(bank[:, b, :], w_dwt2[:, band + b, k, :], done[1][:, LL, k, :],
                                          start=(k == 0), stop=(k == NB[1] - 1))
                    return m
                pe.wait_ge(w_in["dwt1"], 16)
                pe.wait_ge(mm_read, number[("conv", 0, LL, 7)] + 1)
                terms = [(0, 0), (1, 0), (2, 0), (3, 0), (-1, 0), (4, 0)]
                for n, (delta, _) in enumerate(terms):
                    js = [j for j in range(2) if 0 <= 4 * (2 * q + j) + delta < NB[0]]
                    a, z = js[0], js[-1] + 1
                    first = 4 * (2 * q + a) + delta
                    m = pe.matmul(bank[:, a:z, :], w_dwt1[:, band, delta + 1, :],
                                  ll0[:, first:first + 4 * (z - a - 1) + 1:4, :], start=(n == 0), stop=(n == 5))
                return m

            def inv(v, q, bank):
                if v == 1:
                    pe.wait_ge(w_in["inv2"], 16)
                    pe.wait_ge(mm_read, number[("conv", 2, HL, 1)] + 1)
                    for j in range(2):
                        for b in range(4):
                            m = pe.matmul(bank[:, j, :], w_inv2[:, b, 2 * q + j, :], done[2][:, b, 0, :],
                                          start=(b == 0), stop=(b == 3))
                    return m
                pe.wait_ge(w_in["inv1"], 16)
                pe.wait_ge(mm_read, number[("inv", 1, LL, 1)] + 1)
                for j in range(2):
                    terms = [(b, k) for b in range(4) for k in range(NB[1]) if -1 <= 2 * q + j - 4 * k <= 4]
                    for n, (b, k) in enumerate(terms):
                        src = ll1[:, k, :] if b == LL else done[1][:, b, k, :]
                        m = pe.matmul(bank[:, j, :], w_inv1[:, b, 2 * q + j - 4 * k + 1, :], src,
                                      start=(n == 0), stop=(n == len(terms) - 1))
                return m

            turn_keys(0)
            for n, (what, v, band, q) in enumerate(plan):
                if n == number[("conv", 0, HH, 0)]:
                    spread_thr(0)
                if n == number[("conv", 1, HH, 0)]:
                    turn_keys(1)
                    spread_thr(1)
                if n == number[("conv", 2, LL, 0)]:
                    turn_keys(2)
                    spread_thr(2)
                wait(pe, mm_read, n - NMM + 1)
                bank = mm[n % NMM]
                if what == "conv":
                    m = conv(v, band, q, bank)
                elif what == "dwt":
                    m = dwt(v, band, q, bank)
                else:
                    m = inv(v, q, bank)
                m.then_inc(mm_done, 1)

        @block.scalar
        def _(act):
            def magnitudes(v):
                t, d, nd = TL[v], DL[v], DB[v]
                flat = keys[:, :, 0:t * d]
                wait(act, thr_rows_set, v)
                for j in range(key_banks[v]):
                    n = keys_before[v] + j
                    act.wait_ge(key_done, n + 1)
                    if v == 2:
                        src = kbank[n % 2][:, 0:HALF * P].rearrange("p (h n) -> p h n", h=HALF)
                        dst = flat
                    else:
                        h, g = j // (key_banks[v] // HALF), j % (key_banks[v] // HALF)
                        src = kbank[n % 2][:, :].rearrange("p (k i d) -> p k i d", k=4, d=nd)
                        dst = flat[:, h].rearrange("p (i k d) -> p k i d", i=t, d=nd)[:, 4 * g:4 * g + 4]
                    act.activation(dst, src, ACT.Abs).then_inc(key_read, 1)

            magnitudes(0)
            for n, (what, v, band, q) in enumerate(plan):
                if n == number[("conv", 1, HH, 0)]:
                    magnitudes(1)
                if n == number[("conv", 2, LL, 0)]:
                    magnitudes(2)
                act.wait_ge(mm_done, n + 1)
                if n in stage_no:
                    s = stage_no[n]
                    wait(act, stored[s % NST], 16 * (s // NST))
                    dst = stage[:, s % NST]
                elif what == "dwt":
                    dst = raw[v][:, band, 2 * q:2 * q + 2, :] if v == 1 else raw[2][:, band:band + 2, 0, :]
                elif what == "inv":
                    dst = ll1[:, 2 * q:2 * q + 2, :]
                elif v == 0:
                    dst = ll0[:, 2 * q:2 * q + 2, :]
                else:
                    dst = done[1][:, band, 2 * q:2 * q + 2, :] if v == 1 else done[2][:, band:band + 2, 0, :]
                if what == "conv":
                    act.activation(dst, mm[n % NMM][:, :, :], ACT.Identity, bias=conv_bias[:, 0:1]).then_inc(mm_read, 1)
                else:
                    act.activation(dst, mm[n % NMM][:, :, :], ACT.Copy).then_inc(mm_read, 1)

        @block.vector
        def _(dve):
            steps = [0]

            def medians(v):
                t, d, nd = TL[v], DL[v], DB[v]
                flat = keys[:, :, 0:t * d]
                dve.wait_ge(key_read, keys_before[v] + key_banks[v])
                dve.tensor_scalar(flat, flat, -1.0, None, ALU.mult).then_inc(keys_set, 1)
                dve.wait_ge(keys_set, v + 1)
                for r in range(ROUNDS[v]):
                    begin = steps[0]
                    for row in range(HALF * t):
                        part = keys[:, row // t, row % t * d:(row % t + 1) * d]
                        if r:
                            dve.wait_ge(med, begin - HALF * t + row + 1)
                        dve.max(eight[:, row, :], part).then_inc(med, 1)
                    steps[0] += HALF * t
                    if r == ROUNDS[v] - 1:
                        break
                    for row in range(HALF * t):
                        part = keys[:, row // t, row % t * d:(row % t + 1) * d]
                        dve.wait_ge(med, steps[0] - HALF * t + row + 1)
                        dve.match_replace(part, eight[:, row, :], part, -3.0e38).then_inc(med, 1)
                    steps[0] += HALF * t
                dve.wait_ge(med, steps[0])
                wait(dve, thr_done, v)
                dve.tensor_scalar(thr_rows[:, :, :].rearrange("p h (i d) -> p (h i) d", d=nd),
                                  eight[:, 0:HALF * t, 7:8].broadcast_to([P, HALF * t, nd]),
                                  THR, None, ALU.mult).then_inc(thr_rows_set, 1)

            def clip(n, v, band, k, blocks):
                part = raw[v][:, band, k:k + blocks, :] if v < 2 else raw[2][:, LH:HH + 1, 0, :]
                dst = clipped[:, n % 2, 0:blocks, :]
                bound = thr[:, 0:IM].unsqueeze(1).broadcast_to([P, blocks, IM])
                wait(dve, soft_done, n - 1)
                if v == 0:
                    dve.wait_ge(raw_in[band], 16 * TL[0])
                dve.tensor_tensor(dst, part, bound, ALU.min).then_inc(low_cut, 1)
                dve.wait_ge(low_cut, n + 1)
                dve.scalar_tensor_tensor(dst, bound, -1.0, dst, ALU.mult, ALU.max).then_inc(clip_done, 1)

            for v in range(LEVELS):
                medians(v)
                dve.wait_ge(thr_done, v + 1)
                for n, (level, band, k, blocks) in enumerate(cuts):
                    if level == v:
                        clip(n, level, band, k, blocks)

        @block.gpsimd
        def _(pool):
            for n, (v, band, k, blocks) in enumerate(cuts):
                part = raw[v][:, band, k:k + blocks, :] if v < 2 else raw[2][:, LH:HH + 1, 0, :]
                pool.wait_ge(clip_done, n + 1)
                pool.tensor_tensor(part, part, clipped[:, n % 2, 0:blocks, :], ALU.subtract).then_inc(soft_done, 1)


def synthesis_phase(nc, synth_s, x1_s, out_w, out_b, d_inv, t_inv, out):
    with ExitStack() as ctx:
        sb = lambda name, shape, dt=F32: ctx.enter_context(nc.sbuf_tensor(name, shape, dt))
        sem = lambda name: ctx.enter_context(nc.semaphore(name))
        pb = lambda name, shape, dt=F32: ctx.enter_context(nc.psum_tensor(name, shape, dt))
        R = 2 * TL[0]

        z = sb("z", [P, 2, R, C])
        zc = [sb(f"zc{e}", [P, 2, NT, R, 4]) for e in range(2)]
        x1 = [sb(f"x1s_{e}", [P, NT, C]) for e in range(2)]
        res = [sb(f"res{e}", [P, NT, C]) for e in range(2)]
        v_sb = [sb(f"v_sb{e}", [P, BANK]) for e in range(2)]
        w_out = sb("w_out", [P, CT, C])
        w_dinv = sb("w_dinv", [P, CT, 2, P])
        wd = sb("wd", [P, 2, C])
        w_tinv = sb("w_tinv", [P, P])
        b_out = sb("b_out", [P, C])

        vbank = [pb(f"vbank{i}", [P, BANK]) for i in range(2)]
        fbank = [pb(f"fbank{i}", [P, BANK]) for i in range(2)]
        wbank = pb("wbank", [P, BANK])

        consts_in = sem("s_consts_in")
        z_in = sem("z_in")
        x1_in = [sem(f"x1_in{e}") for e in range(2)]
        wd_done = sem("wd_done")
        wd_ready = sem("wd_ready")
        zc_ready = sem("zc_ready")
        passed = sem("s_passed")
        with_bias = sem("with_bias")
        v_done = sem("v_done")
        v_ready = sem("v_ready")
        f_done = sem("f_done")
        res_ready = sem("res_ready")
        out_stored = [sem(f"out_stored{e}") for e in range(2)]

        block = ctx.enter_context(nc.Block())

        def over_images(engine, body):
            body(0, 0)
            body(1, 1)
            with engine.Fori(1, B // 2) as i:
                body(2 * i, 0)
                body(2 * i + 1, 1)

        @block.sync
        def _(sp):
            for dst, src in ((w_out[:, :, :], out_w.rearrange("(k p) o -> p k o", p=P)),
                             (w_dinv[:, :, :, :].rearrange("p a b c -> p (a b c)"), d_inv),
                             (w_tinv[:, :], t_inv),
                             (b_out[:, :], out_b.unsqueeze(0).broadcast_to([P, C]))):
                sp.dma_start(dst, src).then_inc(consts_in, 16)
            for band in range(4):
                for k in range(NB[0]):
                    bt, bd = band // 2, band % 2
                    sp.dma_start(z[k * DB[0]:(k + 1) * DB[0], bd, bt * TL[0]:(bt + 1) * TL[0], :],
                                 synth_s[band, :, k, :].rearrange("(i d) m -> d i m", d=DB[0])
                                 ).then_inc(z_in, 16)

            def image(b, e):
                wait(sp, res_ready, 4 * b - 4)
                sp.dma_start(x1[e][:, :, :], x1_s[bass.ds(b * N, N), :].rearrange("(p t) c -> p t c", t=NT)
                             ).then_inc(x1_in[e], 16)
                sp.wait_ge(res_ready, 4 * b + 4)
                sp.dma_start(out[bass.ds(b * N, N), :].rearrange("(p t) c -> p t c", t=NT),
                             res[e][:, :, :]).then_inc(out_stored[e], 16)
            over_images(sp, image)
            for s in out_stored:
                sp.wait_ge(s, 16 * B // 2)

        @block.gpsimd
        def _(pool):
            pool.wait_ge(consts_in, 64)
            pool.wait_ge(z_in, 16 * 64)

            def image(b, e):
                wait(pool, v_done, 4 * b - 4)
                pool.sem_inc(passed, 1)
                for bd in range(2):
                    src = z[:, bd, :, bass.ds(b * W, W)].rearrange("p r (w t) -> p t r w", t=NT)
                    m = pool.tensor_copy(zc[e][:, bd], src)
                m.then_inc(zc_ready, 1)
                pool.wait_ge(x1_in[e], 16 * ((b - e) // 2 + 1))
                pool.tensor_tensor(x1[e][:, :, :], x1[e][:, :, :],
                                   b_out[:, :].unsqueeze(1).broadcast_to([P, NT, C]), ALU.add).then_inc(with_bias, 1)
            over_images(pool, image)

        @block.tensor
        def _(pe):
            pe.wait_ge(consts_in, 64)
            for bd in range(2):
                for kt in range(CT):
                    m = pe.matmul(wbank[:, bd * C:(bd + 1) * C], w_dinv[:, kt, bd, :], w_out[:, kt, :],
                                  start=(kt == 0), stop=(kt == CT - 1))
            m.then_inc(wd_done, 1)
            pe.wait_ge(wd_ready, 1)

            def columns(b, e, n):
                if n == 0:
                    pe.wait_ge(zc_ready, b + 1)
                wait(pe, v_ready, bank_free(b, n))
                for t in range(2):
                    for bd in range(2):
                        m = pe.matmul(vbank[n % 2][:, t * C:(t + 1) * C],
                                      zc[e][:, bd, 2 * n + t].rearrange("p r w -> p (r w)"),
                                      wd[:, bd, :], start=(bd == 0), stop=(bd == 1))
                m.then_inc(v_done, 1)

            def rows(b, e, n):
                pe.wait_ge(v_ready, 4 * b + n + 1)
                wait(pe, res_ready, bank_free(b, n))
                pe.matmul(fbank[n % 2][:, :], w_tinv[:, :], v_sb[n % 2][:, :],
                          start=True, stop=True).then_inc(f_done, 1)

            def image(b, e):
                for n in range(4):
                    columns(b, e, n)
                    if n:
                        rows(b, e, n - 1)
                rows(b, e, 3)
            over_images(pe, image)

        @block.scalar
        def _(act):
            act.wait_ge(wd_done, 1)
            act.activation(wd[:, :, :].rearrange("p a b -> p (a b)"), wbank[:, :], ACT.Copy).then_inc(wd_ready, 1)

            def image(b, e):
                for n in range(4):
                    act.wait_ge(v_done, 4 * b + n + 1)
                    wait(act, f_done, bank_free(b, n))
                    act.activation(v_sb[n % 2][:, :], vbank[n % 2][:, :], ACT.Copy).then_inc(v_ready, 1)
            over_images(act, image)

        @block.vector
        def _(dve):
            def image(b, e):
                dve.wait_ge(with_bias, b + 1)
                wait(dve, out_stored[e], 16 * ((b - e) // 2))
                for n in range(4):
                    dve.wait_ge(f_done, 4 * b + n + 1)
                    cols = lambda s: s[:, 2 * n:2 * n + 2, :].rearrange("p t c -> p (t c)")
                    dve.tensor_tensor(cols(res[e]), fbank[n % 2][:, :], cols(x1[e]), ALU.add).then_inc(res_ready, 1)
            over_images(dve, image)


def build(nc, a):
    scratch = lambda name, *shape: nc.dram_tensor(name, shape, F32).ap()
    q_s, k_s, v_s = (scratch(n, B * C, N) for n in ("q_s", "k_s", "v_s"))
    conv_phase(nc, a["x"], a["wq"], a["wv"], a["wk"], a["bq"], a["bv"], a["bk"], a["mean_op"], a["ident"],
               q_s, k_s, v_s)
    x1_s = scratch("x1_s", B * N, C)
    bands_s = scratch("bands_s", 4, TL[0], DL[0], C)
    synth_s = scratch("synth_s", 4, P, NB[0], C)
    ktab_s = scratch("ktab_s", 1, KROWS * KCOLS)
    with ExitStack() as ctx:
        sb = lambda name, shape: ctx.enter_context(nc.sbuf_tensor(name, shape, F32))
        conv_ops = [[sb(f"conv_op{v}{k}", [P, P]) for k in range(3 if NB[v] > 1 else 1)] for v in range(LEVELS)]
        conv_bias = sb("conv_bias", [P, 1])
        with nc.sbuf_tensor("heads_out", [P, NT, HEADS, HD], F32) as heads_out:
            attention_phase(nc, q_s, k_s, v_s, a["ident16"], a["ident"], heads_out)
            analysis_phase(nc, a["x"], heads_out, a["wp"], a["mean_op"], a["ident"], a["t_op"], a["d_op"],
                           [a[f"w{i}"] for i in range(6)], [a[f"b{i}"] for i in range(6)],
                           conv_ops, conv_bias, ktab_s, x1_s, bands_s)
        bands_phase(nc, bands_s, conv_ops, conv_bias, a["ident"], a["dwt1"], a["dwt2"], a["inv2"], a["inv1"], synth_s)
        synthesis_phase(nc, synth_s, x1_s, a["out_w"], a["out_b"], a["d_inv"], a["t_inv"], a["out"])


def arrays_of(inputs):
    taps_first = lambda w: np.ascontiguousarray(np.transpose(w, (2, 3, 1, 0))).reshape(-1, C)
    a = {
        "x": np.ascontiguousarray(inputs["x"]).reshape(B * N, C),
        "wq": taps_first(inputs["L0_conv_w3"]), "bq": inputs["L0_conv_b3"],
        "wv": taps_first(inputs["L0_conv_w5"]), "bv": inputs["L0_conv_b5"],
        "wk": taps_first(inputs["L0_conv_w7"]), "bk": inputs["L0_conv_b7"],
        "wp": np.ascontiguousarray(np.transpose(inputs["L0_conv_wp"])),
        "out_w": np.ascontiguousarray(np.transpose(inputs["L1_conv_out_w"])), "out_b": inputs["L1_conv_out_b"],
        "mean_op": np.full((P, P), 1.0 / (N * CG), np.float32),
        "ident": np.eye(P, dtype=np.float32), "ident16": np.eye(P, dtype=np.float16),
        **wavelet_constants(),
    }
    for i in range(6):
        a[f"w{i}"] = np.ascontiguousarray(inputs[f"L1_conv_w{i}"]).reshape(1, 2 * i + 1, 2 * i + 1)
        a[f"b{i}"] = inputs[f"L1_conv_b{i}"]
    return a


def kernel(**inputs):
    import concourse.bacc as bacc
    from concourse.bass_utils import run_bass_kernel_spmd

    arrays = {f"in_{k}": np.ascontiguousarray(v) for k, v in arrays_of(inputs).items()}
    nc = bacc.Bacc("TRN2", target_bir_lowering=False, num_devices=1)
    a = {k[3:]: nc.dram_tensor(k, v.shape, mybir.dt.from_np(v.dtype), kind="ExternalInput").ap()
         for k, v in arrays.items()}
    a["out"] = nc.dram_tensor("out_0", (B * N, C), F32, kind="ExternalOutput").ap()
    build(nc, a)
    results = run_bass_kernel_spmd(nc, [arrays], core_ids=[0]).results
    return results[0]["out_0"].reshape(B, H, W, C)
```

```python
from contextlib import ExitStack

import numpy as np

import concourse.bass as bass
from concourse import mybir
from concourse.alu_op_type import AluOpType as ALU

F32 = mybir.dt.float32
F16 = mybir.dt.float16
ACT = mybir.ActivationFunctionType
AX = mybir.AxisListType

P = 128
B, H, W, C = 8, 32, 32, 256
N = H * W
CT = C // P
G = 32
CG = C // G
NT = N // P
HD = 16
NH = C // HD
HEADS = B * NH
EPS = 1e-5
BANK = 512

PAD = 2
PW = W + 2 * PAD
PH = H + 2 * PAD
CONVS = (("q", 1, 0), ("v", 3, 1), ("k", 5, 10))
TAPS = 35
X_SCALE = 64.0
W_SCALE = 256.0
QK_SCALE = 16.0


def wait(engine, sem, value):
    if not (isinstance(value, int) and value <= 0):
        engine.wait_ge(sem, value)


def bank_free(b, n):
    return 4 * b + max(n - 1, 0)




POINTS = {"v": 4, "k": 6}


def conv_phase(nc, x, wq, wv, wk, bq, bv, bk, mean_op, ident, q_s, k_s, v_s):
    tiles = [("q", co, half) for co in range(CT) for half in range(2)]
    tiles += [("v", co, p) for co in range(CT) for p in (1, 2, 0, 3)]
    tiles += [("k", co, p) for co in range(CT) for p in (1, 2, 3, 4, 0, 5)]
    NTILE = len(tiles)
    Q_TILES, V_TILES = 4, 8
    NACC = 4
    SIDE = {"q": 1, "v": 3, "k": 5}
    HALF_W = W // 2
    FIRST = {"q": 0, "v": 1, "k": 1 + 3 * POINTS["v"]}
    NSIDES = FIRST["k"] + 5 * POINTS["k"]
    pieces = [("q", wq, 0, 1, kt, 0) for kt in range(CT)]
    pieces += [(n, w, y * SIDE[n], SIDE[n], kt, FIRST[n] + y * POINTS[n])
               for n, w in (("v", wv), ("k", wk)) for y in range(SIDE[n]) for kt in range(CT)]
    parts_of = {"q": CT, "v": CT * 4, "k": CT * 9}
    STATS1_AFTER, STATS2_AFTER, TURN_AFTER = 12, 16, (19, 19, 21, 21)

    with ExitStack() as ctx:
        sb = lambda name, shape, dt=F32: ctx.enter_context(nc.sbuf_tensor(name, shape, dt))
        sem = lambda name: ctx.enter_context(nc.semaphore(name))

        w_hi = sb("w_hi", [P, NSIDES, CT, C], F16)
        w_lo = sb("w_lo", [P, NSIDES, CT, C], F16)
        w_stage = sb("w_stage", [P, 2, 5, C])
        w_work = sb("w_work", [P, 6, C])
        w_side, w_sum = w_work[:, 0:4], w_work[:, 4:6]
        x_tok = sb("x_tok", [P, NT, C])
        x_pad = [sb(f"x_pad{ct}", [P, PH, PW]) for ct in range(CT)]
        q_hi = [sb(f"q_hi{ct}", [P, H, W], F16) for ct in range(CT)]
        q_lo = [sb(f"q_lo{ct}", [P, H, W], F16) for ct in range(CT)]
        v_hi = [sb(f"v_hi{ct}", [P, POINTS["v"], H + 2, HALF_W], F16) for ct in range(CT)]
        v_lo = [sb(f"v_lo{ct}", [P, POINTS["v"], H + 2, HALF_W], F16) for ct in range(CT)]
        k_hi = [sb(f"k_hi{ct}", [P, POINTS["k"], PH, HALF_W], F16) for ct in range(CT)]
        k_lo = [sb(f"k_lo{ct}", [P, POINTS["k"], PH, HALF_W], F16) for ct in range(CT)]
        work = sb("work", [P, 2, PH, PW - 2])
        diff, diff4 = work[:, 0], work[:, 1]
        x_sq = work[:, :, :, :].rearrange("p a y x -> p (a y x)")[:, 0:NT * C].rearrange("p (t c) -> p t c", c=C)
        side = sb("side", [P, 2, PH, HALF_W])
        side_b = w_work[:, :, :].rearrange("p a c -> p (a c)")[:, 0:2 * PH * HALF_W].rearrange(
            "p (i y x) -> p i y x", i=2, y=PH)
        k_side = lambda ct, r: (side, side_b)[(3 * ct + r) % 2]
        group_part = sb("group_part", [P, 2, G])
        spread = sb("spread", [P, G])
        spread_inv = sb("spread_inv", [P, G])
        eps = sb("eps", [P, 1])
        bias = sb("bias", [P, 3, CT])
        bias_s = sb("bias_s", [P, 3, CT])
        mean_w = sb("mean_w", [P, P])
        ident_w = sb("ident_w", [P, P])
        prod = sb("prod", [P, 3, BANK])
        both = sb("both", [P, 2, BANK])
        out_stage = sb("out_stage", [P, 2, N])

        acc = [ctx.enter_context(nc.psum_tensor(f"acc{i}", [P, BANK], F32)) for i in range(NACC)]
        stat = ctx.enter_context(nc.psum_tensor("stat", [P, BANK], F32))
        turned = [ctx.enter_context(nc.psum_tensor(f"turned{i}", [P, BANK], F32)) for i in range(2)]

        consts_in = sem("consts_in")
        piece_in = [sem("piece_in0"), sem("piece_in1")]
        w_step = sem("w_step")
        w_made = sem("w_made")
        w_hi_ready = sem("w_hi_ready")
        w_lo_ready = sem("w_lo_ready")
        piece_done = sem("piece_done")
        x_in = sem("x_in")
        borders_set = sem("borders_set")
        bias_ready = sem("bias_ready")
        part_ready = sem("part_ready")
        stat_ready = sem("stat_ready")
        centred = sem("centred")
        squared = sem("squared")
        spread_ready = sem("spread_ready")
        inv_ready = sem("inv_ready")
        normed = sem("normed")
        turned_ready = sem("turned_ready")
        pad_ready = sem("pad_ready")
        q_hi_ready = sem("q_hi_ready")
        q_ready = sem("q_ready")
        v_made = sem("v_made")
        v_hi_ready = sem("v_hi_ready")
        v_ready = sem("v_ready")
        k_diff = sem("k_diff")
        k_made = sem("k_made")
        k_hi_ready = sem("k_hi_ready")
        k_ready = sem("k_ready")
        conv_done = sem("conv_done")
        emptied = {e: sem("emptied_by_" + e) for e in ("act", "dve")}
        summed = sem("summed")
        out_q = sem("out_q")
        out_vk = sem("out_vk")
        out_stored = [sem(f"out_stored{i}") for i in range(CT)]

        by = ["dve" if (name == "v" and p == 2) or (name == "k" and p in (2, 4)) else "act"
              for name, _, p in tiles]
        place = [by[:n].count(by[n]) for n in range(NTILE)]
        per_image = {e: by.count(e) for e in ("act", "dve")}
        number = {t: n for n, t in enumerate(tiles)}
        SLOT = {("v", 1): 0, ("v", 0): 1, ("v", 3): 2, ("k", 1): 0, ("k", 3): 0, ("k", 0): 1, ("k", 5): 2}
        SUMS = {"v": 4, "k": 8}
        SUMS_IMAGE = CT * (SUMS["v"] + SUMS["k"])
        SUMS_BEFORE = {("v", 0): 0, ("v", 1): 4, ("k", 0): 8, ("k", 1): 16}

        block = ctx.enter_context(nc.Block())

        def over_images(engine, body):
            body(0, True)
            with engine.Fori(1, B - 1) as b:
                body(b, True)
            body(B - 1, False)

        def filter_cuts(name):
            if name == "q":
                return ((slice(0, 1), ("stage", 0), W_SCALE),)
            if name == "v":
                return ((slice(0, 1), ("stage", 0), -W_SCALE), (slice(3, 4), ("stage", 2), W_SCALE),
                        (slice(1, 3), ("made", 0), W_SCALE / 2))
            return ((slice(0, 1), ("stage", 0), W_SCALE / 4), (slice(5, 6), ("stage", 4), W_SCALE),
                    (slice(1, 3), ("made", 0), -W_SCALE / 6), (slice(3, 5), ("made", 2), W_SCALE / 24))

        def cut_source(n, source):
            kind, at = source
            return w_stage[:, n % 2, at:at + 1] if kind == "stage" else w_side[:, at:at + 2]

        cuts_before = [sum(len(filter_cuts(p[0])) for p in pieces[:n]) for n in range(len(pieces) + 1)]
        made_in = {"q": 0, "v": 1, "k": 2}
        made_before = [sum(made_in[p[0]] for p in pieces[:n]) for n in range(len(pieces) + 1)]
        EARLY, MIDDLE, LATE = range(0, 5), range(5, 8), range(8, len(pieces))

        def out_scale(name):
            return (1.0 if name == "v" else QK_SCALE) / (X_SCALE * W_SCALE)

        @block.sync
        def _(sp):
            sp.dma_start(x_tok[:, :, :], x[0:N, :].rearrange("(t p) c -> p t c", p=P)).then_inc(x_in, 16)
            sp.dma_start(mean_w[:, :], mean_op).then_inc(consts_in, 16)
            sp.dma_start(ident_w[:, :], ident).then_inc(consts_in, 16)
            for i, b in enumerate((bq, bv, bk)):
                sp.dma_start(bias[:, i, :], b.rearrange("(a p) -> p a", p=P),
                             allow_slow_non_contiguous=True).then_inc(consts_in, 16)

            def load_piece(n):
                _, w, t0, taps, kt, _ = pieces[n]
                wait(sp, piece_done, n - 1)
                rows = w.rearrange("(t k p) c -> k p t c", k=CT, p=P)[kt][:, t0:t0 + taps]
                sp.dma_start(w_stage[:, n % 2, 0:taps], rows).then_inc(piece_in[n % 2], 16)

            def next_x(b):
                sp.wait_ge(turned_ready, 4 * b + 4)
                sp.dma_start(x_tok[:, :, :],
                             x[bass.ds((b + 1) * N, N), :].rearrange("(t p) c -> p t c", p=P)).then_inc(x_in, 16)

            def store(b, c, co):
                if c == 0:
                    sp.wait_ge(out_q, 4 * b + 2 * co + 2)
                else:
                    sp.wait_ge(out_vk, 4 * b + 2 * (c - 1) + co + 1)
                dst = (q_s, v_s, k_s)[c]
                sp.dma_start(dst[bass.ds(b * C + co * P, P), :], out_stage[:, co]).then_inc(out_stored[co], 16)

            stores = [(c, co) for c in range(3) for co in range(CT)]

            for n in range(len(pieces)):
                if n == LATE[0] + 2:
                    next_x(0)
                if n == LATE[4] + 2:
                    for c, co in stores[:3]:
                        store(0, c, co)
                load_piece(n)

            def image(b, more):
                first = isinstance(b, int) and b == 0
                if more and not first:
                    next_x(b)
                for c, co in stores[3 if first else 0:]:
                    store(b, c, co)
            over_images(sp, image)
            for s in out_stored:
                sp.wait_ge(s, 16 * 3 * B)

        @block.gpsimd
        def _(pool):
            for ct in range(CT):
                pool.memset(x_pad[ct][:, :, :], 0.0).then_inc(borders_set, 1)
            pool.memset(eps[:, :], EPS / X_SCALE ** 2).then_inc(borders_set, 1)

        def inside(pad, half):
            return pad[:, PAD + half * H // 2:PAD + (half + 1) * H // 2, PAD:PAD + W]

        VY = slice(PAD - 1, PAD + H + 1)

        def columns(a, c):
            return a[:, :, c:c + 2 * HALF_W - 1:2]

        def v_sources():
            return (diff[:, VY, 1:1 + W].rearrange("p y (j s) -> p s y j", s=2), side[:, :, VY])

        V_SIDES = (slice(0, 4, 3), slice(1, 3))
        K_SIDES = (slice(0, 6, 5), slice(1, 3), slice(3, 5))

        @block.vector
        def _(dve):
            over = lambda s: s.unsqueeze(1).unsqueeze(3).broadcast_to([P, NT, G, CG])
            tiled = x_tok[:, :, :].rearrange("p t (g c) -> p t g c", g=G)
            steps = [0]

            def make_filters(which):
                def step(instruction):
                    steps[0] += 1
                    instruction.then_inc(w_step, 1)

                def settle():
                    dve.wait_ge(w_step, steps[0])

                for n in which:
                    name, _, _, taps, kt, first = pieces[n]
                    dve.wait_ge(piece_in[n % 2], 16 * (n // 2 + 1))
                    tap = lambda i: w_stage[:, n % 2, i]
                    even, odd = w_sum[:, 0], w_sum[:, 1]
                    wait(dve, w_hi_ready, cuts_before[n])
                    wait(dve, w_lo_ready, cuts_before[n])
                    if name == "v":
                        step(dve.tensor_tensor(even, tap(0), tap(2), ALU.add))
                        settle()
                        dve.tensor_tensor(w_side[:, 0], even, tap(1), ALU.add)
                        dve.tensor_tensor(w_side[:, 1], even, tap(1), ALU.subtract).then_inc(w_made, 1)
                    if name == "k":
                        step(dve.tensor_tensor(even, tap(0), tap(2), ALU.add))
                        step(dve.tensor_tensor(odd, tap(1), tap(3), ALU.add))
                        settle()
                        step(dve.tensor_tensor(even, even, tap(4), ALU.add))
                        settle()
                        step(dve.tensor_tensor(w_side[:, 0], even, odd, ALU.add))
                        dve.tensor_tensor(w_side[:, 1], even, odd, ALU.subtract).then_inc(w_made, 1)
                        dve.wait_ge(w_made, made_before[n] + 1)
                        step(dve.scalar_tensor_tensor(even, tap(2), 4.0, tap(0), ALU.mult, ALU.add))
                        step(dve.scalar_tensor_tensor(odd, tap(3), 4.0, tap(1), ALU.mult, ALU.add))
                        settle()
                        step(dve.scalar_tensor_tensor(even, tap(4), 16.0, even, ALU.mult, ALU.add))
                        settle()
                        dve.scalar_tensor_tensor(w_side[:, 2], odd, 2.0, even, ALU.mult, ALU.add)
                        dve.scalar_tensor_tensor(w_side[:, 3], odd, -2.0, even, ALU.mult, ALU.add).then_inc(w_made, 1)
                    for i, (sides, source, scale) in enumerate(filter_cuts(name)):
                        at = slice(first + sides.start, first + sides.stop)
                        dve.wait_ge(w_hi_ready, cuts_before[n] + i + 1)
                        if source[0] == "made":
                            dve.wait_ge(w_made, made_before[n] + source[1] // 2 + 1)
                        m = dve.scalar_tensor_tensor(w_lo[:, at, kt], cut_source(n, source), scale,
                                                     w_hi[:, at, kt], ALU.mult, ALU.subtract)
                        m.then_inc(w_lo_ready, 1)
                    dve.wait_ge(w_lo_ready, cuts_before[n + 1])
                    dve.sem_inc(piece_done, 1)

            def first_sum(b):
                dve.wait_ge(x_in, 16 * (b + 1))
                dve.tensor_reduce(group_part[:, 0], x_tok[:, :, :].rearrange("p t (g c) -> p g t c", g=G),
                                  AX.XY, ALU.add).then_inc(part_ready, 1)

            def centre(b):
                dve.wait_ge(stat_ready, 2 * b + 1)
                dve.tensor_tensor(tiled, tiled, over(stat[:, 0:G]), ALU.subtract).then_inc(centred, 1)

            def second_sum(b):
                dve.wait_ge(squared, b + 1)
                dve.tensor_reduce(group_part[:, 1], x_sq.rearrange("p t (g c) -> p g t c", g=G),
                                  AX.XY, ALU.add).then_inc(part_ready, 1)

            def scale(b):
                dve.wait_ge(spread_ready, b + 1)
                dve.reciprocal(spread_inv[:, :], spread[:, :]).then_inc(inv_ready, 1)
                dve.wait_ge(inv_ready, b + 1)
                dve.tensor_tensor(tiled, tiled, over(spread_inv[:, :]), ALU.mult).then_inc(normed, 1)

            def pad(b, n):
                ct, half = n // 2, n % 2
                dve.wait_ge(turned_ready, 4 * b + n + 1)
                dve.tensor_copy(inside(x_pad[ct], half),
                                turned[n % 2][:, :].rearrange("p (h w) -> p h w", w=W)).then_inc(pad_ready, 1)

            def cut_q(b):
                for ct in range(CT):
                    dve.wait_ge(q_hi_ready, 2 * b + ct + 1)
                    dve.tensor_tensor(q_lo[ct][:, :, :], x_pad[ct][:, PAD:PAD + H, PAD:PAD + W],
                                      q_hi[ct][:, :, :], ALU.subtract).then_inc(q_ready, 1)

            def sides_v(b):
                dve.wait_ge(pad_ready, 4 * b + 4)
                for ct in range(CT):
                    a = x_pad[ct]
                    wait(dve, v_ready, 4 * b + 2 * ct)
                    dve.tensor_tensor(diff[:, VY], a[:, VY, 2:PW], a[:, VY, 0:PW - 2],
                                      ALU.subtract).then_inc(v_made, 1)
                    dve.tensor_tensor(side[:, 0, VY], columns(a, 3)[:, VY], columns(a, 2)[:, VY], ALU.add)
                    dve.tensor_tensor(side[:, 1, VY], columns(a, 3)[:, VY], columns(a, 2)[:, VY],
                                      ALU.subtract).then_inc(v_made, 1)
                    for i, (src, sides) in enumerate(zip(v_sources(), V_SIDES)):
                        n = 4 * b + 2 * ct + i
                        dve.wait_ge(v_hi_ready, n + 1)
                        dve.tensor_tensor(v_lo[ct][:, sides], src, v_hi[ct][:, sides], ALU.subtract).then_inc(v_ready, 1)

            def sides_k(b, ct):
                a = x_pad[ct]
                wait(dve, k_ready, 6 * b + 3 * ct)
                dve.tensor_tensor(diff, a[:, :, 2:PW], a[:, :, 0:PW - 2], ALU.subtract).then_inc(k_diff, 1)
                dve.scalar_tensor_tensor(diff4, a[:, :, 0:PW - 2], -4.0, a[:, :, 2:PW],
                                         ALU.mult, ALU.add).then_inc(k_diff, 1)
                dve.wait_ge(k_diff, 4 * b + 2 * ct + 2)
                pairs = (((diff, 0, -4.0, 2), (diff, 1, -4.0, 3)),
                         ((diff4, 1, 1.0, 2), (diff4, 1, -1.0, 2)),
                         ((diff, 1, 2.0, 2), (diff, 1, -2.0, 2)))

                def make(r):
                    n = 6 * b + 3 * ct + r
                    wait(dve, k_ready, n - 1)
                    for i, (t, c0, f, c1) in enumerate(pairs[r]):
                        m = dve.scalar_tensor_tensor(k_side(ct, r)[:, i], columns(t, c0), f, columns(t, c1),
                                                     ALU.mult, ALU.add)
                    m.then_inc(k_made, 1)

                def cut(r):
                    n = 6 * b + 3 * ct + r
                    dve.wait_ge(k_made, n + 1)
                    dve.wait_ge(k_hi_ready, n + 1)
                    dve.tensor_tensor(k_lo[ct][:, K_SIDES[r]], k_side(ct, r)[:, :], k_hi[ct][:, K_SIDES[r]],
                                      ALU.subtract).then_inc(k_ready, 1)

                make(0)
                make(1)
                cut(0)
                make(2)
                cut(1)
                cut(2)

            def take(b, n):
                name, co, p = tiles[n]
                s = SUMS_IMAGE * b + SUMS_BEFORE[name, co]
                psum = acc[n % NACC][:, :]
                before = tiles.index((name, co, p - 1))
                dve.wait_ge(emptied["act"], per_image["act"] * b + place[before] + 1)
                dve.wait_ge(conv_done, NTILE * b + n + 1)
                if p == 2:
                    wait(dve, summed, s)
                    dve.tensor_tensor(both[:, 0], psum, prod[:, 0], ALU.add).then_inc(summed, 1)
                    dve.scalar_tensor_tensor(both[:, 1], psum, -1.0, prod[:, 0], ALU.mult, ALU.add).then_inc(summed, 1)
                    dve.wait_ge(summed, s + 2)
                else:
                    dve.tensor_tensor(both[:, 0], both[:, 0], prod[:, 0], ALU.add).then_inc(summed, 1)
                    dve.scalar_tensor_tensor(both[:, 1], prod[:, 0], 2.0, both[:, 1], ALU.mult, ALU.add).then_inc(summed, 1)
                    dve.wait_ge(summed, s + 4)
                    dve.tensor_tensor(both[:, 0], psum, both[:, 0], ALU.add).then_inc(summed, 1)
                    dve.scalar_tensor_tensor(both[:, 1], psum, -2.0, both[:, 1], ALU.mult, ALU.add).then_inc(summed, 1)
                    dve.wait_ge(summed, s + 6)
                dve.sem_inc(emptied["dve"], 1)

            def put(b, name, co):
                s = SUMS_IMAGE * b + SUMS_BEFORE[name, co] + SUMS[name] - 2
                for i, p in enumerate((0, 3 if name == "v" else 5)):
                    n = number[name, co, p]
                    dve.wait_ge(emptied["act"], per_image["act"] * b + place[n] + 1)
                    if i == 0:
                        dve.wait_ge(out_stored[co], 16 * (3 * b + (1 if name == "v" else 2)))
                    m = dve.scalar_tensor_tensor(out_stage[:, co, i:N:2], both[:, i], out_scale(name),
                                                 prod[:, 1 + i], ALU.mult, ALU.add)
                    m.then_inc(summed, 1)
                dve.wait_ge(summed, s + 2)
                dve.sem_inc(out_vk, 1)

            def ready(b):
                for n in range(4):
                    pad(b, n)
                cut_q(b)
                sides_v(b)

            dve.wait_ge(consts_in, 5 * 16)
            dve.tensor_scalar(bias_s[:, :, :], bias[:, :, :], QK_SCALE, None, ALU.mult).then_inc(bias_ready, 1)
            dve.wait_ge(borders_set, CT + 1)
            first_sum(0)
            make_filters(EARLY)
            centre(0)
            make_filters(MIDDLE)
            second_sum(0)
            scale(0)
            ready(0)

            def image(b, more):
                if isinstance(b, int) and b == 0:
                    make_filters(LATE[:4])
                sides_k(b, 0)
                take(b, number["v", 0, 2])
                put(b, "v", 0)
                if isinstance(b, int) and b == 0:
                    make_filters(LATE[4:])
                sides_k(b, 1)
                take(b, number["v", 1, 2])
                put(b, "v", 1)
                if more:
                    first_sum(b + 1)
                take(b, number["k", 0, 2])
                if more:
                    centre(b + 1)
                take(b, number["k", 0, 4])
                if more:
                    second_sum(b + 1)
                put(b, "k", 0)
                if more:
                    scale(b + 1)
                take(b, number["k", 1, 2])
                if more:
                    pad(b + 1, 0)
                    pad(b + 1, 1)
                take(b, number["k", 1, 4])
                if more:
                    pad(b + 1, 2)
                    pad(b + 1, 3)
                    cut_q(b + 1)
                    sides_v(b + 1)
                put(b, "k", 1)
            over_images(dve, image)

        @block.scalar
        def _(act):
            def cut_filters(which):
                for n in which:
                    name, _, _, _, kt, first = pieces[n]
                    act.wait_ge(piece_in[n % 2], 16 * (n // 2 + 1))
                    for sides, source, scale in filter_cuts(name):
                        at = slice(first + sides.start, first + sides.stop)
                        if source[0] == "made":
                            act.wait_ge(w_made, made_before[n] + source[1] // 2 + 1)
                        act.activation(w_hi[:, at, kt], cut_source(n, source), ACT.Copy, scale=scale).then_inc(w_hi_ready, 1)

            def square(b):
                act.wait_ge(centred, b + 1)
                wait(act, k_ready, 6 * b)
                act.activation(x_sq, x_tok[:, :, :], ACT.Square).then_inc(squared, 1)

            def spread_of(b):
                act.wait_ge(stat_ready, 2 * b + 2)
                act.activation(spread[:, :], stat[:, G:2 * G], ACT.Sqrt, bias=eps[:, 0:1],
                               scale=X_SCALE ** -2).then_inc(spread_ready, 1)

            def high_q(b):
                for ct in range(CT):
                    act.wait_ge(pad_ready, 4 * b + 2 * ct + 2)
                    act.activation(q_hi[ct][:, :, :], x_pad[ct][:, PAD:PAD + H, PAD:PAD + W], ACT.Copy).then_inc(q_hi_ready, 1)

            def high_v(b):
                for ct in range(CT):
                    for i, (src, sides) in enumerate(zip(v_sources(), V_SIDES)):
                        act.wait_ge(v_made, 4 * b + 2 * ct + i + 1)
                        act.activation(v_hi[ct][:, sides], src, ACT.Copy).then_inc(v_hi_ready, 1)

            def high_k(b, ct):
                wait(act, conv_done, NTILE * b)
                for r in range(3):
                    act.wait_ge(k_made, 6 * b + 3 * ct + r + 1)
                    act.activation(k_hi[ct][:, K_SIDES[r]], k_side(ct, r)[:, :], ACT.Copy).then_inc(k_hi_ready, 1)

            def empty(b, n):
                name, co, p = tiles[n]
                act.wait_ge(conv_done, NTILE * b + n + 1)
                psum = acc[n % NACC][:, :]
                if name == "q":
                    if p == 0:
                        wait(act, out_stored[co], 48 * b)
                    act.activation(out_stage[:, co, p * BANK:(p + 1) * BANK], psum, ACT.Identity,
                                   bias=bias_s[:, 0, co:co + 1], scale=out_scale("q")).then_inc(emptied["act"], 1)
                    act.wait_ge(emptied["act"], per_image["act"] * b + place[n] + 1)
                    act.sem_inc(out_q, 1)
                    return
                slot = SLOT[name, p]
                s = SUMS_IMAGE * b + SUMS_BEFORE[name, co]
                if name == "k" and p == 3:
                    s += 2
                wait(act, summed, s)
                if slot == 0:
                    act.activation(prod[:, 0], psum, ACT.Copy).then_inc(emptied["act"], 1)
                else:
                    src = bias if name == "v" else bias_s
                    act.activation(prod[:, slot], psum, ACT.Identity, bias=src[:, 1 if name == "v" else 2, co:co + 1],
                                   scale=out_scale(name)).then_inc(emptied["act"], 1)

            act.wait_ge(borders_set, CT + 1)
            cut_filters(EARLY)
            square(0)
            cut_filters(MIDDLE)
            spread_of(0)
            high_q(0)
            high_v(0)
            act.wait_ge(bias_ready, 1)

            def image(b, more):
                for n in range(NTILE):
                    if n == 4:
                        if isinstance(b, int) and b == 0:
                            cut_filters(LATE[:4])
                        high_k(b, 0)
                    if n == 8:
                        if isinstance(b, int) and b == 0:
                            cut_filters(LATE[4:])
                        high_k(b, 1)
                    if by[n] == "act":
                        empty(b, n)
                    if more:
                        if n == 14:
                            square(b + 1)
                        if n == 17:
                            spread_of(b + 1)
                        if n == 21:
                            high_q(b + 1)
                            high_v(b + 1)
            over_images(act, image)

        @block.tensor
        def _(pe):
            def stats(b, k):
                pe.wait_ge(part_ready, 2 * b + k + 1)
                if k == 0:
                    wait(pe, spread_ready, b)
                pe.matmul(stat[:, k * G:(k + 1) * G], mean_w[:, :], group_part[:, k],
                          start=True, stop=True).then_inc(stat_ready, 1)

            def transposes(b, n):
                ct, half = n // 2, n % 2
                pe.wait_ge(normed, b + 1)
                wait(pe, pad_ready, 4 * b + max(n - 1, 0))
                for t in range(4):
                    m = pe.transpose(turned[n % 2][:, t * P:(t + 1) * P],
                                     x_tok[:, 4 * half + t, ct * P:(ct + 1) * P], ident_w[:, :])
                m.then_inc(turned_ready, 1)

            def products(b, n):
                name, co, p = tiles[n]
                last = n - NACC
                if last >= 0:
                    pe.wait_ge(emptied[by[last]], per_image[by[last]] * b + place[last] + 1)
                elif not (isinstance(b, int) and b == 0):
                    last += NTILE
                    pe.wait_ge(emptied[by[last]], per_image[by[last]] * (b - 1) + place[last] + 1)
                if n == 0:
                    pe.wait_ge(q_ready, 2 * b + 2)
                if n == Q_TILES:
                    pe.wait_ge(v_ready, 4 * b + 4)
                if n == Q_TILES + V_TILES:
                    pe.wait_ge(k_ready, 6 * b + 6)
                if n in (0, Q_TILES, Q_TILES + V_TILES) and isinstance(b, int) and b == 0:
                    pe.wait_ge(w_lo_ready, cuts_before[parts_of[name]])
                cols = slice(co * P, (co + 1) * P)
                terms = [(y, ct) for y in range(SIDE[name]) for ct in range(CT)]
                for i, (y, ct) in enumerate(terms):
                    if name == "q":
                        at = 0
                        hi, lo = (t[ct][:, p * H // 2:(p + 1) * H // 2, :] for t in (q_hi, q_lo))
                    else:
                        at = FIRST[name] + y * POINTS[name] + p
                        hi, lo = (t[ct][:, p, y:y + H, :] for t in ((v_hi, v_lo) if name == "v" else (k_hi, k_lo)))
                    bank = acc[n % NACC][:, :]
                    pe.matmul(bank, w_hi[:, at, ct, cols], hi, start=(i == 0), stop=False)
                    pe.matmul(bank, w_hi[:, at, ct, cols], lo, start=False, stop=False)
                    m = pe.matmul(bank, w_lo[:, at, ct, cols], hi, start=False, stop=(i == len(terms) - 1))
                m.then_inc(conv_done, 1)

            pe.wait_ge(consts_in, 5 * 16)
            stats(0, 0)
            stats(0, 1)
            for m in range(4):
                transposes(0, m)

            def image(b, more):
                for n in range(NTILE):
                    products(b, n)
                    if more:
                        if n == STATS1_AFTER:
                            stats(b + 1, 0)
                        if n == STATS2_AFTER:
                            stats(b + 1, 1)
                        for m in range(4):
                            if n == TURN_AFTER[m]:
                                transposes(b + 1, m)
            over_images(pe, image)


def attention_phase(nc, q_s, k_s, v_s, ident16, ident, heads_out):
    D2 = 4 * HD
    ROWS = P
    K_ONE = 256.0
    NKT = 4
    NPT = 4
    VW = 32
    CH = 2
    NSB = 3
    UNITS = NT * CH
    CG4 = 4
    QW = N // CG4
    EXP_SCALE = HD ** -0.5 / QK_SCALE ** 2

    with ExitStack() as ctx:
        sb = lambda name, shape, dt=F32: ctx.enter_context(nc.sbuf_tensor(name, shape, dt))
        sem = lambda name: ctx.enter_context(nc.semaphore(name))
        pb = lambda name, shape, dt=F32: ctx.enter_context(nc.psum_tensor(name, shape, dt))

        raw = {c: [sb(f"raw_{c}{e}", [P, NT, HD]) for e in range(2)] for c in "qkv"}
        q_tok = [sb(f"q_tok{e}", [P, NT, ROWS], F16) for e in range(NKT)]
        k_tok = [sb(f"k_tok{e}", [P, NT, ROWS], F16) for e in range(NKT)]
        v_tok = [sb(f"v_tok{e}", [P, NT, VW]) for e in range(NKT)]
        k_t = [sb(f"k_t{e}", [ROWS, N], F16) for e in range(NKT)]
        qa_t = [sb(f"qa_t{e}", [ROWS, N], F16) for e in range(2)]
        qb_t = [sb(f"qb_t{e}", [ROWS, N], F16) for e in range(2)]
        probs = [sb(f"probs{e}", [P, N]) for e in range(NPT)]
        maxima = sb("maxima", [P, 2, NT, CH])
        neg_max = sb("neg_max", [P, NT])
        o_t = sb("o_t", [P, QW])
        inv_sum = sb("inv_sum", [P, 2, CG4])
        id16 = sb("id16", [P, P], F16)
        id32 = sb("id32", [P, P])

        a_bank = [pb(f"a_bank{i}", [P, BANK]) for i in range(NSB)]
        b_bank = [pb(f"b_bank{i}", [P, BANK]) for i in range(NSB)]
        pv_bank = pb("pv_bank", [P, BANK])
        t_bank = pb("t_bank", [P, BANK])
        t16 = t_bank[:, :].bitcast(F16)

        consts_in = sem("a_consts_in")
        raw_in = {c: [sem(f"raw_in_{c}{e}") for e in range(2)] for c in "qkv"}
        pads_set = sem("pads_set")
        passed = sem("passed")
        hi_cut = sem("hi_cut")
        tok_ready = sem("tok_ready")
        k_turned = sem("k_turned")
        qa_turned = sem("qa_turned")
        qb_turned = sem("qb_turned")
        o_turned = sem("o_turned")
        k_ready = sem("k_ready")
        qa_ready = sem("qa_ready")
        qb_ready = sem("qb_ready")
        a_done = sem("a_done")
        a_read = sem("a_read")
        max_ready = sem("max_ready")
        neg_hi_cut = sem("neg_hi_cut")
        max_rows_set = sem("max_rows_set")
        b_done = sem("b_done")
        exp_done = sem("exp_done")
        pv_done = sem("pv_done")
        o_copied = sem("o_copied")
        inv_done = sem("inv_done")
        o_out = sem("o_out")

        A_AHEAD = 3
        PV_LAG = 3
        ORDER = "BAbTatV"
        TURN = {"k": ((0, 1), (0, 1)), "qa": ((2, 1), (3, 0)), "o": ((4, 1), (4, 1)), "qb": ((6, 1), (6, 1))}
        READ = {"k": 0, "qa": 3, "o": 4, "qb": 6}
        READER = {"k": "act", "qa": "act", "qb": "dve"}
        LEAD = 2

        def over_heads(engine, body):
            exists = lambda x: 0 <= x < HEADS
            for h in range(-LEAD, 4):
                body(h, h % 4, exists)
            with engine.Fori(1, HEADS // 4 - 1) as i:
                for e in range(4):
                    body(4 * i + e, e, lambda x: True)
            for h in range(HEADS - 4, HEADS + 1):
                body(h, h % 4, exists)

        def there(exists, h, d):
            return exists(h + d) if isinstance(h, int) else True

        def read_turned(engine, name, h, e, t, ok):
            for what, lead, dst, turned, ready in (("k", LEAD, k_t[(e + LEAD) % 4], k_turned, k_ready),
                                                   ("qa", LEAD, qa_t[e % 2], qa_turned, qa_ready),
                                                   ("qb", 1, qb_t[(e + 1) % 2], qb_turned, qb_ready)):
                if READER[what] == name and t == READ[what] and ok(lead):
                    engine.wait_ge(turned, h + lead + 1)
                    if name == "act":
                        m = engine.activation(dst[:, :], t16[0:ROWS, :], ACT.Copy)
                    else:
                        m = engine.tensor_copy(dst[:, :], t16[0:ROWS, :])
                    m.then_inc(ready, 1)

        block = ctx.enter_context(nc.Block())

        @block.sync
        def _(sp):
            sp.dma_start(id16[:, :], ident16).then_inc(consts_in, 16)
            sp.dma_start(id32[:, :], ident).then_inc(consts_in, 16)

            def load(h, e):
                for c, src in (("q", q_s), ("k", k_s), ("v", v_s)):
                    wait(sp, tok_ready, h - 1)
                    sp.dma_start(raw[c][e % 2][:, :, :],
                                 src[bass.ds(h * HD, HD), :].rearrange("c (r t d) -> (c r) t d", t=NT, d=HD)
                                 ).then_inc(raw_in[c][e % 2], 16)
            for h in range(4):
                load(h, h % 4)
            with sp.Fori(1, HEADS // 4) as i:
                for e in range(4):
                    load(4 * i + e, e)

        @block.gpsimd
        def _(pool):
            for e in range(NKT):
                pool.memset(k_tok[e][:, :, D2:D2 + 2], K_ONE).then_inc(pads_set, 1)
                pool.memset(k_tok[e][:, :, D2 + 2:ROWS], 0.0).then_inc(pads_set, 1)
                pool.memset(q_tok[e][:, :, D2 + 2:ROWS], 0.0).then_inc(pads_set, 1)
                pool.memset(v_tok[e][:, :, HD:HD + 1], 1.0).then_inc(pads_set, 1)
                pool.memset(v_tok[e][:, :, HD + 1:VW], 0.0).then_inc(pads_set, 1)
            pool.wait_ge(pads_set, 5 * NKT)

            def cut(h, e):
                turn = 16 * (2 * h // 4 + 1) if isinstance(h, int) else None
                qv = q_tok[e][:, :, 0:D2].rearrange("p t (r l d) -> p t r l d", r=2, l=2)
                kv = k_tok[e][:, :, 0:D2].rearrange("p t (l r d) -> p t r l d", r=2, l=2)
                raws = {c: raw[c][e % 2][:, :, :].unsqueeze(2).broadcast_to([P, NT, 2, HD]) for c in "qk"}
                fills = (h - e % 2) // 2 + 1 if isinstance(h, int) else h_fills(h, e)
                wait(pool, qb_turned, h - NKT + 1)
                wait(pool, pv_done, NT * (h - NKT + 1))
                pool.wait_ge(raw_in["q"][e % 2], 16 * fills)
                pool.sem_inc(passed, 1)
                pool.memset(q_tok[e][:, :, D2:D2 + 2], 0.0)
                pool.tensor_copy(qv[:, :, :, 0], raws["q"]).then_inc(hi_cut, 1)
                pool.wait_ge(raw_in["k"][e % 2], 16 * fills)
                pool.sem_inc(passed, 1)
                pool.tensor_copy(kv[:, :, :, 0], raws["k"]).then_inc(hi_cut, 1)
                pool.wait_ge(raw_in["v"][e % 2], 16 * fills)
                pool.sem_inc(passed, 1)
                pool.tensor_copy(v_tok[e][:, :, 0:HD], raw["v"][e % 2][:, :, :])
                pool.wait_ge(hi_cut, 2 * h + 2)
                pool.tensor_tensor(qv[:, :, :, 1], raws["q"], qv[:, :, :, 0], ALU.subtract)
                pool.tensor_tensor(kv[:, :, :, 1], raws["k"], kv[:, :, :, 0], ALU.subtract).then_inc(tok_ready, 1)

            def h_fills(h, e):
                return (h - e) // 2 + e // 2 + 1

            for h in range(4):
                cut(h, h % 4)
            with pool.Fori(1, HEADS // 4) as i:
                for e in range(4):
                    cut(4 * i + e, e)

        @block.tensor
        def _(pe):
            pe.wait_ge(consts_in, 32)

            def last_use(u):
                return u - NSB + 1 if u >= NSB else (UNITS - 1 - u) // NSB * NSB + u + 1 - UNITS

            def turn_tokens(tok, half, done):
                for t in range(half * NT // 2, (half + 1) * NT // 2):
                    m = pe.transpose(t16[0:ROWS, t * P:(t + 1) * P], tok[:, t, :], id16[:, :])
                if half:
                    m.then_inc(done, 1)

            def scores_a(h, e, t, c):
                if t == 0 and c == 0:
                    pe.wait_ge(k_ready, h + 1)
                    pe.wait_ge(qa_ready, h + 1)
                u = CH * t + c
                wait(pe, a_read, h * UNITS + last_use(u))
                pe.matmul(a_bank[u % NSB][:, :], qa_t[e % 2][:, t * P:(t + 1) * P],
                          k_t[e][:, c * BANK:(c + 1) * BANK], start=True, stop=True).then_inc(a_done, 1)

            def scores_b(h, e, t, c):
                u = CH * t + c
                if u == 0:
                    pe.wait_ge(qb_ready, h + 1)
                wait(pe, exp_done, h * UNITS + last_use(u))
                pe.matmul(b_bank[u % NSB][:, :], k_t[e][:, t * P:(t + 1) * P],
                          qb_t[e % 2][:, c * BANK:(c + 1) * BANK], start=True, stop=True).then_inc(b_done, 1)

            def times_v(h, e, t):
                if t == 0:
                    wait(pe, o_copied, h)
                pe.wait_ge(exp_done, h * UNITS + CH * (t + 1))
                for j in range(CG4):
                    m = pe.matmul(pv_bank[VW * j:VW * (j + 1), 0:QW], v_tok[e][:, t, :],
                                  probs[t % NPT][:, j * QW:(j + 1) * QW], start=(t == 0), stop=(t == NT - 1),
                                  tile_position=(0, VW * j))
                m.then_inc(pv_done, 1)

            def head(h, e, exists):
                ok = lambda d: there(exists, h, d)
                def turn(what, half):
                    if what == "k" and ok(LEAD):
                        if half == 0:
                            pe.wait_ge(tok_ready, h + LEAD + 1)
                            wait(pe, qb_ready, h + 1)
                        turn_tokens(k_tok[(e + LEAD) % 4], half, k_turned)
                    if what == "qa" and ok(LEAD):
                        if half == 0:
                            wait(pe, k_ready, h + LEAD + 1)
                        turn_tokens(q_tok[(e + LEAD) % 4], half, qa_turned)
                    if what == "o" and ok(-1):
                        if half == 0:
                            wait(pe, qa_ready, min_heads(h + LEAD + 1))
                            pe.wait_ge(o_copied, h)
                        m = pe.transpose(t_bank[:, half * P:(half + 1) * P], o_t[:, half * P:(half + 1) * P], id32[:, :])
                        if half:
                            m.then_inc(o_turned, 1)
                    if what == "qb" and ok(1):
                        if half == 0:
                            pe.wait_ge(max_rows_set, h + 2)
                            wait(pe, qa_ready, min_heads(h + LEAD + 1))
                            wait(pe, o_out, h)
                        turn_tokens(q_tok[(e + 1) % 4], half, qb_turned)

                def turns(at):
                    for what, halves in TURN.items():
                        for half in range(2):
                            if halves[half] == at:
                                turn(what, half)

                for t in range(NT):
                    d = 1 + (t + A_AHEAD) // NT
                    a_tile = (h + d, (e + d) % 4, (t + A_AHEAD) % NT)
                    for what in ORDER:
                        if what in "Bb" and ok(0):
                            scores_b(h, e, t, 0 if what == "B" else 1)
                        if what in "Tt":
                            turns((t, 0 if what == "T" else 1))
                        if what in "Aa" and ok(d):
                            scores_a(*a_tile, 0 if what == "A" else 1)
                        if what == "V":
                            if t < PV_LAG and ok(-1):
                                times_v(h - 1, (e - 1) % 4, NT - PV_LAG + t)
                            if t >= PV_LAG and ok(0):
                                times_v(h, e, t - PV_LAG)

            def min_heads(v):
                return min(v, HEADS) if isinstance(v, int) else v

            over_heads(pe, head)

        @block.scalar
        def _(act):
            def head(h, e, exists):
                ok = lambda d: there(exists, h, d)
                for t in range(NT):
                    for c in range(CH):
                        if ok(0):
                            u = CH * t + c
                            act.wait_ge(b_done, h * UNITS + u + 1)
                            if c == 0:
                                wait(act, pv_done, h * NT + t - NPT + 1)
                            act.activation(probs[t % NPT][:, c * BANK:(c + 1) * BANK], b_bank[u % NSB][:, :],
                                           ACT.Exp, scale=EXP_SCALE).then_inc(exp_done, 1)
                    read_turned(act, "act", h, e, t, ok)
            over_heads(act, head)

        @block.vector
        def _(dve):
            def maximum(h, e):
                dve.wait_ge(a_read, (h + 1) * NT * CH)
                dve.tensor_reduce(neg_max[:, :], maxima[:, e % 2], AX.X, ALU.max, negate=True).then_inc(max_ready, 1)
                dve.wait_ge(max_ready, h + 1)
                hi = q_tok[e][:, :, D2:D2 + 1].rearrange("p t o -> p (t o)")
                lo = q_tok[e][:, :, D2 + 1:D2 + 2].rearrange("p t o -> p (t o)")
                dve.tensor_scalar(hi, neg_max[:, :], 1 / K_ONE, None, ALU.mult).then_inc(neg_hi_cut, 1)
                dve.wait_ge(neg_hi_cut, h + 1)
                dve.scalar_tensor_tensor(lo, neg_max[:, :], 1 / K_ONE, hi, ALU.mult,
                                         ALU.subtract).then_inc(max_rows_set, 1)

            def head(h, e, exists):
                ok = lambda d: there(exists, h, d)
                for t in range(NT):
                    d = 1 + (t + A_AHEAD) // NT
                    ta = (t + A_AHEAD) % NT
                    if ok(d):
                        for c in range(CH):
                            dve.wait_ge(a_done, ((h + d) * NT + ta) * CH + c + 1)
                            dve.tensor_reduce(maxima[:, (e + d) % 2, ta, c:c + 1], a_bank[(CH * ta + c) % NSB][:, :], AX.X,
                                              ALU.max).then_inc(a_read, 1)
                        if ta == NT - 1:
                            maximum(h + d, (e + d) % 4)
                    read_turned(dve, "dve", h, e, t, ok)
                    if t == PV_LAG - 1 and ok(-1):
                        dve.wait_ge(pv_done, h * NT)
                        dve.tensor_copy(o_t[:, :], pv_bank[:, 0:QW]).then_inc(o_copied, 1)
                    if t == READ["o"] and ok(-1):
                        dve.wait_ge(o_turned, h)
                        o = t_bank[:, 0:QW].rearrange("p (i j w) -> p i j w", i=2, w=VW)
                        dve.reciprocal(inv_sum[:, :, :], o[:, :, :, HD]).then_inc(inv_done, 1)
                        dve.wait_ge(inv_done, h)
                        dst = heads_out[:, :, bass.ds(h - 1, 1), :]
                        dve.tensor_tensor(dst.rearrange("p (j i) o d -> p (i o) j d", i=2),
                                          o[:, :, :, 0:HD],
                                          inv_sum[:, :, :].unsqueeze(3).broadcast_to([P, 2, CG4, HD]),
                                          ALU.mult).then_inc(o_out, 1)
            over_heads(dve, head)


def band_matrices(size):
    dec_lo = np.array([
        -0.00011747678400228192, 0.0006754494059985568, -0.0003917403729959771, -0.00487035299301066,
        0.008746094047015655, 0.013981027917015516, -0.04408825393106472, -0.01736930100202211,
        0.128747426620186, 0.00047248457399797254, -0.2840155429624281, -0.015829105256023893,
        0.5853546836548691, 0.6756307362980128, 0.3128715909144659, 0.05441584224308161], dtype=np.float64)
    taps = len(dec_lo)
    both = (dec_lo[::-1], dec_lo * (-1.0) ** np.arange(taps))
    m = np.zeros((2, size // 2, size + taps - 2))
    for band in range(2):
        for i in range(size // 2):
            m[band, i, 2 * i:2 * i + taps] = both[band]
    half = taps // 2
    return m[:, :, half - 1:-(half - 1)].astype(np.float32)


LEVELS = 3
TL = [16, 8, 4]
DL = [128, 64, 32]
DB = [8, 16, 32]
NB = [16, 4, 1]
DELTAS = range(-1, 5)


def wavelet_constants():
    def block(tm, dm, t_in, d_in, t_out, d_out, rev_in, rev_out):
        m = np.einsum("tT,dD->tdTD", tm, dm[d_in][:, d_out])
        m = m.reshape(P, P)
        if rev_in:
            m = m[::-1]
        if rev_out:
            m = m[:, ::-1]
        return np.ascontiguousarray(m)
    w = {n: band_matrices(n) for n in (8, 16, 32, 64, 128, 256)}
    bands = [(bt, bd) for bt in range(2) for bd in range(2)]
    out = {}
    eye4 = np.eye(4, dtype=np.float32)
    out["t_op"] = np.einsum("bih,wv->hwbiv", w[32], eye4).reshape(P, P)
    out["t_inv"] = np.einsum("bih,wv->biwhv", w[32][:, ::-1], eye4).reshape(P, P)
    out["d_op"] = w[256].transpose(2, 0, 1).reshape(CT, P, 2, P).transpose(1, 0, 2, 3).reshape(P, -1)
    rev = w[256].reshape(2, NB[0], DB[0], C)[:, :, ::-1].reshape(2, P, C)
    out["d_inv"] = rev.transpose(2, 0, 1).reshape(CT, P, 2, P).transpose(1, 0, 2, 3).reshape(P, -1)
    sl = lambda k, n: slice(k * n, (k + 1) * n)
    out["dwt1"] = np.concatenate([
        block(w[16][bt].T, w[128][bd].T, None, sl(4 + e, 8), None, sl(1, 16), True, False)
        for bt, bd in bands for e in DELTAS], 1)
    out["dwt2"] = np.concatenate([
        block(w[8][bt].T, w[64][bd].T, None, sl(k, 16), None, sl(0, 32), True, False)
        for bt, bd in bands for k in range(4)], 1)
    out["inv2"] = np.concatenate([
        block(w[8][bt], w[64][bd], None, sl(0, 32), None, sl(k, 16), True, True)
        for bt, bd in bands for k in range(4)], 1)
    out["inv1"] = np.concatenate([
        block(w[16][bt], w[128][bd], None, sl(1, 16), None, sl(4 + e, 8), True, True)
        for bt, bd in bands for e in DELTAS], 1)
    return {k: np.ascontiguousarray(v, dtype=np.float32) for k, v in out.items()}


KS = 11
KROWS, KCOLS = 31, 64
KY0, KX0 = 10, 26


def analysis_phase(nc, x, heads_out, wp, mean_op, ident, t_op, d_op, kernels, biases,
                   conv_ops, conv_bias, ktab_s, x1_s, bands_s):
    with ExitStack() as ctx:
        sb = lambda name, shape, dt=F32: ctx.enter_context(nc.sbuf_tensor(name, shape, dt))
        sem = lambda name: ctx.enter_context(nc.semaphore(name))
        pb = lambda name, shape, dt=F32: ctx.enter_context(nc.psum_tensor(name, shape, dt))

        bands = sb("bands", [P, 2, 2 * TL[0], C])
        o_in = [sb(f"o_in{e}", [P, NT, C]) for e in range(2)]
        x1 = [sb(f"x1_{e}", [P, NT, C]) for e in range(2)]
        xc = sb("xc", [P, NT, C])
        xn = sb("xn", [P, NT, C])
        o_t = sb("o_turned_sb", [P, CT, NT, P])
        rows = sb("rows", [P, CT, NT, P])
        wp_w = sb("wp_w", [P, CT, C])
        t_w = sb("t_w", [P, P])
        d_w = sb("d_w", [P, CT, 2, P])
        mean_w = sb("mean_w2", [P, P])
        id32 = sb("id32b", [P, P])
        group_part = sb("group_part2", [P, 2, G])
        spread = sb("spread2", [P, G])
        spread_inv = sb("spread_inv2", [P, G])
        eps = sb("eps2", [P, 1])
        ktab6 = sb("ktab6", [KS, 6, KS])
        kmean = sb("kmean", [KS, KS])
        ktab = sb("ktab", [KROWS, KCOLS])
        bias6 = sb("bias6", [P, 6])

        turned = [pb(f"turned2{i}", [P, BANK]) for i in range(2)]
        proj = [pb(f"proj{i}", [P, BANK]) for i in range(2)]
        cols = [pb(f"cols{i}", [P, BANK]) for i in range(2)]
        stat = pb("stat2", [P, BANK])

        consts_in = sem("f_consts_in")
        heads_in = [sem(f"heads_in{e}") for e in range(2)]
        x_in = [sem(f"x_in2{e}") for e in range(2)]
        eps_set = sem("eps_set")
        o_turned = sem("o_turned2")
        o_sb = sem("o_sb")
        proj_done = sem("proj_done")
        x1_done = sem("x1_done")
        x1_stored = [sem(f"x1_stored{e}") for e in range(2)]
        part_ready = sem("part_ready2")
        stat_ready = sem("stat_ready2")
        centred = sem("centred2")
        squared = sem("squared2")
        spread_ready = sem("spread_ready2")
        inv_ready = sem("inv_ready2")
        normed = sem("normed2")
        rows_done = sem("rows_done")
        rows_sb = sem("rows_sb")
        cols_done = sem("cols_done")
        cols_sb = sem("cols_sb")
        bands_stored = sem("bands_stored")
        k_zero = sem("k_zero")
        k_in = sem("k_in")
        k_step = sem("k_step")
        k_out = sem("k_out")
        ops_in = sem("ops_in")
        b_step = sem("b_step")

        block = ctx.enter_context(nc.Block())

        def over_images(engine, first, step, last):
            first()
            step(0, 0, 1)
            step(1, 1, 0)
            with engine.Fori(1, B // 2 - 1) as i:
                step(2 * i, 0, 1)
                step(2 * i + 1, 1, 0)
            step(B - 2, 0, 1)
            last()

        @block.sync
        def _(sp):
            for dst, src in ((wp_w[:, :, :], wp.rearrange("(k p) o -> p k o", p=P)), (id32[:, :], ident),
                             (mean_w[:, :], mean_op), (t_w[:, :], t_op),
                             (d_w[:, :, :, :].rearrange("p a b c -> p (a b c)"), d_op)):
                sp.dma_start(dst, src).then_inc(consts_in, 16)

            def front(b, e):
                wait(sp, part_ready, 2 * (b - 1))
                sp.dma_start(o_in[e][:, :, :].rearrange("p t (h d) -> p t h d", d=HD),
                             heads_out[:, :, bass.ds(b * NH, NH), :]).then_inc(heads_in[e], 16)
                wait(sp, centred, b - 1)
                wait(sp, x1_stored[e], 16 * ((b - e) // 2))
                sp.dma_start(x1[e][:, :, :], x[bass.ds(b * N, N), :].rearrange("(p t) c -> p t c", t=NT)
                             ).then_inc(x_in[e], 16)

            def store(b, e):
                sp.wait_ge(x1_done, 4 * b + 4)
                sp.dma_start(x1_s[bass.ds(b * N, N), :].rearrange("(p t) c -> p t c", t=NT),
                             x1[e][:, :, :]).then_inc(x1_stored[e], 16)

            def step(b, e, f):
                front(b + 1, f)
                store(b, e)
            def store_bands(half):
                sp.wait_ge(cols_sb, 4 * B // 2 * (half + 1))
                images = slice(half * C // 2, (half + 1) * C // 2)
                for bt, bd in ((1, 1), (0, 0), (0, 1), (1, 0)):
                    sp.dma_start(bands_s[2 * bt + bd].rearrange("i d m -> d i m")[:, :, images],
                                 bands[:, bd, bt * TL[0]:(bt + 1) * TL[0], images]).then_inc(bands_stored, 16)

            def last():
                store_bands(0)
                store(B - 1, 1)
                store_bands(1)
            over_images(sp, lambda: front(0, 0), step, last)
            sp.wait_ge(bands_stored, 2 * 64)
            for e in range(2):
                sp.wait_ge(x1_stored[e], 16 * B // 2)

        @block.gpsimd
        def _(pool):
            pool.memset(eps[:, :], EPS).then_inc(eps_set, 1)
            pool.memset(ktab6[:, :, :], 0.0).then_inc(k_zero, 1)
            pool.memset(ktab[:, :], 0.0).then_inc(k_zero, 1)
            pool.wait_ge(k_zero, 2)
            pool.dma_start(ktab_s.rearrange("o (y x) -> (o y) x", x=KCOLS), ktab[:, :]).then_inc(k_out, 16)
            for n, (kern, bias) in enumerate(zip(kernels, biases)):
                r = KS // 2
                pool.dma_start(ktab6[r - n:r + n + 1, n, r - n:r + n + 1], kern.rearrange("o y x -> (o y) x")).then_inc(k_in, 16)
                pool.dma_start(bias6[:, n:n + 1], bias.unsqueeze(0).broadcast_to([P, 1])).then_inc(k_in, 16)
            pool.wait_ge(k_in, 16 * 12)
            for n in range(1, 6):
                pool.tensor_tensor(ktab6[:, 0], ktab6[:, 0], ktab6[:, n], ALU.add).then_inc(k_step, 1)
                pool.tensor_tensor(bias6[:, 0:1], bias6[:, 0:1], bias6[:, n:n + 1], ALU.add).then_inc(b_step, 1)
                pool.wait_ge(k_step, n)
                pool.wait_ge(b_step, n)
            pool.tensor_scalar(kmean[:, :], ktab6[:, 0], 1 / 6, None, ALU.mult).then_inc(k_step, 1)
            pool.tensor_scalar(conv_bias[:, :], bias6[:, 0:1], 1 / 6, None, ALU.mult).then_inc(b_step, 1)
            pool.wait_ge(k_step, 6)
            pool.wait_ge(b_step, 6)
            pool.wait_ge(k_out, 16)
            pool.dma_start(ktab_s.rearrange("o (y x) -> (o y) x", x=KCOLS)[KY0:KY0 + KS, KX0:KX0 + KS],
                           kmean[:, :]).then_inc(k_out, 16)
            pool.wait_ge(k_out, 32)
            n = 0
            for level in range(LEVELS):
                t, nd = TL[level], DB[level]
                for k, op in enumerate(conv_ops[level]):
                    delta = k - len(conv_ops[level]) // 2
                    for i in range(t):
                        at = (i + KY0 + 6 - t) * KCOLS + KX0 + KS // 2 - (nd - 1) + nd * delta
                        src = bass.AP(tensor=ktab_s.tensor, offset=at, ap=[[1, nd], [KCOLS, t], [1, nd]])
                        pool.dma_start(op[i * nd:(i + 1) * nd, :].rearrange("p (i d) -> p i d", d=nd),
                                       src).then_inc(ops_in, 16)
                        n += 1
            pool.wait_ge(ops_in, 16 * n)

        @block.tensor
        def _(pe):
            pe.wait_ge(consts_in, 5 * 16)

            def project(b, e):
                pe.wait_ge(heads_in[e], 16 * ((b - e) // 2 + 1))
                for n in range(4):
                    half, kt = n // 2, n % 2
                    if n == 0:
                        wait(pe, rows_sb, 4 * (b - 1))
                    wait(pe, o_sb, bank_free(b, n))
                    for t in range(4):
                        m = pe.transpose(turned[n % 2][:, t * P:(t + 1) * P],
                                         o_in[e][:, 4 * half + t, kt * P:(kt + 1) * P], id32[:, :])
                    m.then_inc(o_turned, 1)
                for n in range(4):
                    pe.wait_ge(o_sb, 4 * b + (2 if n < 2 else 4))
                    wait(pe, x1_done, bank_free(b, n))
                    for t in range(2):
                        for kt in range(CT):
                            m = pe.matmul(proj[n % 2][:, t * C:(t + 1) * C], o_t[:, kt, 2 * n + t, :],
                                          wp_w[:, kt, :], start=(kt == 0), stop=(kt == CT - 1))
                    m.then_inc(proj_done, 1)

            def stats(b, k):
                pe.wait_ge(part_ready, 2 * b + k + 1)
                if k == 0:
                    wait(pe, spread_ready, b)
                pe.matmul(stat[:, k * G:(k + 1) * G], mean_w[:, :], group_part[:, k],
                          start=True, stop=True).then_inc(stat_ready, 1)

            def over_rows(b, projected):
                pe.wait_ge(normed, b + 1)
                for n in range(4):
                    ch, half = n // 2, n % 2
                    if n == 0:
                        pe.wait_ge(o_sb, 4 * projected)
                    wait(pe, rows_sb, bank_free(b, n))
                    for t in range(4):
                        m = pe.matmul(turned[n % 2][:, t * P:(t + 1) * P],
                                      xn[:, 4 * half + t, ch * P:(ch + 1) * P], t_w[:, :],
                                      start=True, stop=True)
                    m.then_inc(rows_done, 1)

            def over_columns(b):
                for n in range(4):
                    bd, half = n // 2, n % 2
                    pe.wait_ge(rows_sb, 4 * b + 4)
                    wait(pe, cols_sb, bank_free(b, n))
                    for ch in range(CT):
                        m = pe.matmul(cols[n % 2][:, :], d_w[:, ch, bd, :],
                                      rows[:, ch, 4 * half:4 * half + 4, :].rearrange("p t n -> p (t n)"),
                                      start=(ch == 0), stop=(ch == CT - 1))
                    m.then_inc(cols_done, 1)

            def first():
                project(0, 0)
                stats(0, 0)
                stats(0, 1)

            def step(b, e, f):
                project(b + 1, f)
                over_rows(b, b + 2)
                stats(b + 1, 0)
                over_columns(b)
                stats(b + 1, 1)

            def last():
                over_rows(B - 1, B)
                over_columns(B - 1)
            over_images(pe, first, step, last)

        @block.scalar
        def _(act):
            act.wait_ge(eps_set, 1)

            def project(b):
                for n in range(4):
                    half, kt = n // 2, n % 2
                    act.wait_ge(o_turned, 4 * b + n + 1)
                    if n == 0:
                        wait(act, proj_done, 4 * b)
                    act.activation(o_t[:, kt, 4 * half:4 * half + 4, :].rearrange("p t n -> p (t n)"),
                                   turned[n % 2][:, :], ACT.Copy).then_inc(o_sb, 1)

            def square(b, e):
                act.wait_ge(centred, b + 1)
                act.wait_ge(o_turned, 4 * b + 4)
                act.activation(o_in[e][:, :, :], xc[:, :, :], ACT.Square).then_inc(squared, 1)

            def spread_of(b):
                act.wait_ge(stat_ready, 2 * b + 2)
                act.activation(spread[:, :], stat[:, G:2 * G], ACT.Sqrt, bias=eps[:, 0:1]).then_inc(spread_ready, 1)

            def over_rows(b):
                for n in range(4):
                    ch, half = n // 2, n % 2
                    act.wait_ge(rows_done, 4 * b + n + 1)
                    if n == 0:
                        wait(act, cols_done, 4 * b)
                    act.activation(rows[:, ch, 4 * half:4 * half + 4, :].rearrange("p t n -> p (t n)"),
                                   turned[n % 2][:, :], ACT.Copy).then_inc(rows_sb, 1)

            def over_columns(b, which):
                for n in which:
                    bd, half = n // 2, n % 2
                    act.wait_ge(cols_done, 4 * b + n + 1)
                    dst = bands[:, bd, :, bass.ds(b * W, W)].rearrange("p r (w t) -> p t r w", t=NT)
                    act.activation(dst[:, 4 * half:4 * half + 4],
                                   cols[n % 2][:, :].rearrange("p (t r w) -> p t r w", t=4, w=4),
                                   ACT.Copy).then_inc(cols_sb, 1)

            def first():
                project(0)
                square(0, 0)
                spread_of(0)

            def step(b, e, f):
                project(b + 1)
                over_rows(b)
                over_columns(b, (0,))
                square(b + 1, f)
                over_columns(b, (1, 2, 3))
                spread_of(b + 1)

            def last():
                over_rows(B - 1)
                over_columns(B - 1, range(4))
            over_images(act, first, step, last)

        @block.vector
        def _(dve):
            over = lambda s: s.unsqueeze(1).unsqueeze(3).broadcast_to([P, NT, G, CG])
            tiled = lambda s: s[:, :, :].rearrange("p t (g c) -> p t g c", g=G)

            def group_sum(src, k):
                dve.tensor_reduce(group_part[:, k], src.rearrange("p t (g c) -> p g t c", g=G),
                                  AX.XY, ALU.add).then_inc(part_ready, 1)

            def add(b, e):
                dve.wait_ge(x_in[e], 16 * ((b - e) // 2 + 1))
                for n in range(4):
                    dve.wait_ge(proj_done, 4 * b + n + 1)
                    part = x1[e][:, 2 * n:2 * n + 2, :].rearrange("p t c -> p (t c)")
                    dve.tensor_tensor(part, proj[n % 2][:, :], part, ALU.add).then_inc(x1_done, 1)

            def centre(b, e):
                dve.wait_ge(x1_done, 4 * b + 4)
                group_sum(x1[e][:, :, :], 0)
                dve.wait_ge(stat_ready, 2 * b + 1)
                wait(dve, normed, b)
                dve.tensor_tensor(tiled(xc), tiled(x1[e]), over(stat[:, 0:G]), ALU.subtract).then_inc(centred, 1)
                dve.wait_ge(squared, b + 1)
                group_sum(o_in[e][:, :, :], 1)

            def scale(b):
                dve.wait_ge(spread_ready, b + 1)
                dve.reciprocal(spread_inv[:, :], spread[:, :]).then_inc(inv_ready, 1)
                dve.wait_ge(inv_ready, b + 1)
                wait(dve, rows_done, 4 * b)
                dve.tensor_tensor(tiled(xn), tiled(xc), over(spread_inv[:, :]), ALU.mult).then_inc(normed, 1)

            def image(b, e):
                add(b, e)
                centre(b, e)
                scale(b)
            over_images(dve, lambda: image(0, 0), lambda b, e, f: image(b + 1, f), lambda: None)


def bands_phase(nc, bands_s, conv_ops, conv_bias, ident, dwt1, dwt2, inv2, inv1, level0, z_in, synth_s):
    LL, LH, HL, HH = range(4)
    HIGH = (HH, LH, HL)
    IM = C
    HALF = IM // P
    ROUNDS = [d // 16 for d in DL]
    NMM, NST = 4, 4
    THR = -float(np.sqrt(2.0 * np.log(32.0)) / 0.6745)

    with ExitStack() as ctx:
        sb = lambda name, shape, dt=F32: ctx.enter_context(nc.sbuf_tensor(name, shape, dt))
        sem = lambda name: ctx.enter_context(nc.semaphore(name))
        pb = lambda name, shape, dt=F32: ctx.enter_context(nc.psum_tensor(name, shape, dt))

        raw = [None] + [sb(f"raw_l{v}", [P, 4, NB[v], IM]) for v in (1, 2)]
        raw0 = lambda band: level0[:, band % 2, band // 2]
        band_of = lambda v, band: raw[v][:, band] if v else raw0(band)
        ll0 = sb("ll0", [P, NB[0], IM])
        done = [None, sb("done_l1", [P, 4, NB[1], IM]), sb("done_l2", [P, 4, NB[2], IM])]
        ll1 = sb("ll1", [P, NB[1], IM])
        keys = [sb(f"keys_l{v}", [P, HALF, TL[v] * DL[v]]) for v in range(LEVELS)]
        eight = sb("eight", [P, HALF * TL[0], 8])
        thr_rows = [sb(f"thr_rows{v}", [P, HALF, P]) for v in range(LEVELS)]
        thr_sb = sb("thr_sb", [P, IM])
        clipped = sb("clipped", [P, 2, 4, IM])
        stage = sb("stage", [P, NST, 2, IM])
        id32 = sb("id32c", [P, P])
        w_dwt1 = sb("w_dwt1", [P, 4, len(DELTAS), P])
        w_dwt2 = sb("w_dwt2", [P, 4, NB[1], P])
        w_inv2 = sb("w_inv2", [P, 4, NB[1], P])
        w_inv1 = w_dwt1

        mm = [pb(f"mm{i}", [P, 2, IM]) for i in range(NMM)]
        kbank = [pb(f"kbank{i}", [P, BANK]) for i in range(2)]
        thr = pb("thr", [P, BANK])

        raw_in = [sem(f"raw_in{b}") for b in range(4)]
        w_in = {n: sem("in_" + n) for n in ("id", "dwt1", "dwt2", "inv2", "inv1")}
        key_done = sem("key_done")
        key_read = sem("key_read")
        keys_set = sem("keys_set")
        med = sem("med")
        thr_rows_set = sem("thr_rows_set")
        thr_done = sem("thr_done")
        thr_copied = sem("thr_copied")
        low_cut = sem("low_cut")
        clip_done = sem("clip_done")
        soft_done = sem("soft_done")
        mm_done = sem("mm_done")
        mm_read = sem("mm_read")
        stored = [sem(f"synth_stored{i}") for i in range(NST)]

        plan = [("conv", 0, LL, q) for q in range(8)]
        plan += [("dwt", 1, b, q) for b in (HH, LL, LH, HL) for q in range(2)]
        plan += [("conv", 1, LL, q) for q in range(2)]
        plan += [("dwt", 2, 2 * q, q) for q in range(2)]
        plan += [("conv", 0, b, q) for b in HIGH for q in range(8)]
        plan += [("conv", 1, b, q) for b in HIGH for q in range(2)]
        plan += [("conv", 2, 2 * q, q) for q in range(2)]
        plan += [("inv", 1, LL, q) for q in range(2)]
        plan += [("inv", 0, LL, q) for q in range(8)]
        number = {p: n for n, p in enumerate(plan)}
        staged = [n for n, p in enumerate(plan) if p[1] == 0 and (p[0] == "inv" or p[2] != LL)]
        stage_no = {n: s for s, n in enumerate(staged)}
        cuts = [(0, b, k, 4) for b in HIGH for k in range(0, 16, 4)]
        cuts += [(1, b, 0, 4) for b in HIGH] + [(2, LH, 0, 3)]
        cut_no = {c: n for n, c in enumerate(cuts)}
        key_banks = [8, 2, 1]
        keys_before = [0, 8, 10]

        block = ctx.enter_context(nc.Block())

        @block.sync
        def _(sp):
            def load_band(b):
                for i in range(TL[0]):
                    sp.dma_start(raw0(b)[i * DB[0]:(i + 1) * DB[0]],
                                 bands_s[b, i].rearrange("(k d) m -> d k m", d=DB[0])).then_inc(raw_in[b], 16)
            sp.dma_start(id32[:, :], ident).then_inc(w_in["id"], 16)
            load_band(HH)
            load_band(LL)
            for n, (t, src) in (("dwt1", (w_dwt1, dwt1)), ("dwt2", (w_dwt2, dwt2))):
                sp.dma_start(t[:, :, :, :].rearrange("p a b c -> p (a b c)"), src).then_inc(w_in[n], 16)
            load_band(LH)
            load_band(HL)
            for n, (t, src) in (("inv2", (w_inv2, inv2)), ("inv1", (w_inv1, inv1))):
                if n == "inv1":
                    sp.wait_ge(mm_read, number[("dwt", 1, HL, 1)] + 1)
                sp.dma_start(t[:, :, :, :].rearrange("p a b c -> p (a b c)"), src).then_inc(w_in[n], 16)
            for s, n in enumerate(staged):
                _, _, band, q = plan[n]
                sp.wait_ge(mm_read, n + 1)
                sp.dma_start(synth_s[band, :, 2 * q:2 * q + 2, :], stage[:, s % NST]).then_inc(stored[s % NST], 16)
                if s % 8 == 7:
                    for slot in stored:
                        slot_turns = 2 * (s // 8 + 1)
                        sp.wait_ge(slot, 16 * slot_turns)
                    for k in range(NB[0]):
                        sp.dma_start(raw0(band)[k * DB[0]:(k + 1) * DB[0]],
                                     synth_s[band, :, k, :].rearrange("(i d) m -> d i m", d=DB[0])
                                     ).then_inc(z_in, 16)
            sp.wait_ge(z_in, 16 * 4 * NB[0])

        @block.tensor
        def _(pe):
            def turn_keys(v):
                src = band_of(v, HH)
                n = keys_before[v]
                jobs = {0: [(h, range(4 * g, 4 * g + 4)) for h in range(HALF) for g in range(4)],
                        1: [(h, range(4)) for h in range(HALF)], 2: [(None, None)]}[v]
                if v == 0:
                    pe.wait_ge(raw_in[HH], 16 * TL[0])
                    pe.wait_ge(w_in["id"], 16)
                else:
                    pe.wait_ge(mm_read, number[("dwt", v, HH if v == 1 else HL, 1)] + 1)
                for h, blocks in jobs:
                    wait(pe, key_read, n - 1)
                    if v == 2:
                        pieces = [(src[:, 0, hh * P:(hh + 1) * P]) for hh in range(HALF)]
                    else:
                        pieces = [src[:, k, h * P:(h + 1) * P] for k in blocks]
                    for j, piece in enumerate(pieces):
                        m = pe.transpose(kbank[n % 2][:, j * P:(j + 1) * P], piece, id32[:, :])
                    m.then_inc(key_done, 1)
                    n += 1

            def spread_thr(v):
                pe.wait_ge(thr_rows_set, v + 1)
                wait(pe, thr_copied, v)
                for h in range(HALF):
                    m = pe.matmul(thr[:, h * P:(h + 1) * P], thr_rows[v][:, h, :], id32[:, :], start=True, stop=True)
                m.then_inc(thr_done, 1)

            def conv(v, band, q, bank):
                if v == 2:
                    if band:
                        pe.wait_ge(soft_done, len(cuts))
                    else:
                        pe.wait_ge(soft_done, len(cuts))
                    return pe.matmul(bank[:, :, :], conv_ops[2][0][:, :], raw[2][:, band:band + 2, 0, :],
                                     start=True, stop=True)
                if band == LL:
                    if v == 0:
                        pe.wait_ge(raw_in[LL], 16 * TL[0])
                    else:
                        pe.wait_ge(mm_read, number[("dwt", 1, LL, 1)] + 1)
                else:
                    k = min((2 * q + 2) // 4 * 4, NB[v] - 4)
                    pe.wait_ge(soft_done, cut_no[(v, band, k, 4)] + 1)
                src = band_of(v, band)
                m = pe.matmul(bank[:, :, :], conv_ops[v][1][:, :], src[:, 2 * q:2 * q + 2, :], start=True, stop=False)
                lo, hi = (1 if q == 0 else 0), (1 if 2 * q + 2 == NB[v] else 2)
                m = pe.matmul(bank[:, lo:2, :], conv_ops[v][0][:, :], src[:, 2 * q - 1 + lo:2 * q + 1, :],
                              start=False, stop=False)
                return pe.matmul(bank[:, 0:hi, :], conv_ops[v][2][:, :], src[:, 2 * q + 1:2 * q + 1 + hi, :],
                                 start=False, stop=True)

            def dwt(v, band, q, bank):
                if v == 2:
                    pe.wait_ge(w_in["dwt2"], 16)
                    pe.wait_ge(mm_read, number[("conv", 1, LL, 1)] + 1)
                    for b in range(2):
                        for k in range(NB[1]):
                            m = pe.matmul(bank[:, b, :], w_dwt2[:, band + b, k, :], done[1][:, LL, k, :],
                                          start=(k == 0), stop=(k == NB[1] - 1))
                    return m
                pe.wait_ge(w_in["dwt1"], 16)
                pe.wait_ge(mm_read, number[("conv", 0, LL, 7)] + 1)
                terms = [(0, 0), (1, 0), (2, 0), (3, 0), (-1, 0), (4, 0)]
                for n, (delta, _) in enumerate(terms):
                    js = [j for j in range(2) if 0 <= 4 * (2 * q + j) + delta < NB[0]]
                    a, z = js[0], js[-1] + 1
                    first = 4 * (2 * q + a) + delta
                    m = pe.matmul(bank[:, a:z, :], w_dwt1[:, band, delta + 1, :],
                                  ll0[:, first:first + 4 * (z - a - 1) + 1:4, :], start=(n == 0), stop=(n == 5))
                return m

            def inv(v, q, bank):
                if v == 1:
                    pe.wait_ge(w_in["inv2"], 16)
                    pe.wait_ge(mm_read, number[("conv", 2, HL, 1)] + 1)
                    for j in range(2):
                        for b in range(4):
                            m = pe.matmul(bank[:, j, :], w_inv2[:, b, 2 * q + j, :], done[2][:, b, 0, :],
                                          start=(b == 0), stop=(b == 3))
                    return m
                pe.wait_ge(w_in["inv1"], 16)
                pe.wait_ge(mm_read, number[("inv", 1, LL, 1)] + 1)
                for j in range(2):
                    terms = [(b, k) for b in range(4) for k in range(NB[1]) if -1 <= 2 * q + j - 4 * k <= 4]
                    for n, (b, k) in enumerate(terms):
                        src = ll1[:, k, :] if b == LL else done[1][:, b, k, :]
                        m = pe.matmul(bank[:, j, :], w_inv1[:, b, 2 * q + j - 4 * k + 1, :], src,
                                      start=(n == 0), stop=(n == len(terms) - 1))
                return m

            turn_keys(0)
            for n, (what, v, band, q) in enumerate(plan):
                if n == number[("conv", 0, HH, 0)]:
                    turn_keys(1)
                    turn_keys(2)
                    spread_thr(0)
                if n == number[("conv", 1, HH, 0)]:
                    spread_thr(1)
                if n == number[("conv", 2, LL, 0)]:
                    spread_thr(2)
                wait(pe, mm_read, n - NMM + 1)
                bank = mm[n % NMM]
                if what == "conv":
                    m = conv(v, band, q, bank)
                elif what == "dwt":
                    m = dwt(v, band, q, bank)
                else:
                    m = inv(v, q, bank)
                m.then_inc(mm_done, 1)

        @block.scalar
        def _(act):
            def magnitudes(v):
                t, d, nd = TL[v], DL[v], DB[v]
                flat = keys[v][:, :, :]
                for j in range(key_banks[v]):
                    n = keys_before[v] + j
                    act.wait_ge(key_done, n + 1)
                    if v == 2:
                        src = kbank[n % 2][:, 0:HALF * P].rearrange("p (h n) -> p h n", h=HALF)
                        dst = flat
                    else:
                        h, g = j // (key_banks[v] // HALF), j % (key_banks[v] // HALF)
                        src = kbank[n % 2][:, :].rearrange("p (k i d) -> p k i d", k=4, d=nd)
                        dst = flat[:, h].rearrange("p (i k d) -> p k i d", i=t, d=nd)[:, 4 * g:4 * g + 4]
                    act.activation(dst, src, ACT.Abs).then_inc(key_read, 1)

            magnitudes(0)
            for n, (what, v, band, q) in enumerate(plan):
                if n == number[("conv", 0, HH, 0)]:
                    magnitudes(1)
                    magnitudes(2)
                act.wait_ge(mm_done, n + 1)
                if n in stage_no:
                    s = stage_no[n]
                    wait(act, stored[s % NST], 16 * (s // NST))
                    dst = stage[:, s % NST]
                elif what == "dwt":
                    dst = raw[v][:, band, 2 * q:2 * q + 2, :] if v == 1 else raw[2][:, band:band + 2, 0, :]
                elif what == "inv":
                    dst = ll1[:, 2 * q:2 * q + 2, :]
                elif v == 0:
                    dst = ll0[:, 2 * q:2 * q + 2, :]
                else:
                    dst = done[1][:, band, 2 * q:2 * q + 2, :] if v == 1 else done[2][:, band:band + 2, 0, :]
                if what == "conv":
                    act.activation(dst, mm[n % NMM][:, :, :], ACT.Identity, bias=conv_bias[:, 0:1]).then_inc(mm_read, 1)
                else:
                    act.activation(dst, mm[n % NMM][:, :, :], ACT.Copy).then_inc(mm_read, 1)

        @block.vector
        def _(dve):
            steps = [0]

            def medians(v):
                t, d, nd = TL[v], DL[v], DB[v]
                flat = keys[v][:, :, :]
                dve.wait_ge(key_read, keys_before[v] + key_banks[v])
                dve.tensor_scalar(flat, flat, -1.0, None, ALU.mult).then_inc(keys_set, 1)
                dve.wait_ge(keys_set, v + 1)
                for r in range(ROUNDS[v]):
                    begin = steps[0]
                    for row in range(HALF * t):
                        part = keys[v][:, row // t, row % t * d:(row % t + 1) * d]
                        if r:
                            dve.wait_ge(med, begin - HALF * t + row + 1)
                        dve.max(eight[:, row, :], part).then_inc(med, 1)
                    steps[0] += HALF * t
                    if r == ROUNDS[v] - 1:
                        break
                    for row in range(HALF * t):
                        part = keys[v][:, row // t, row % t * d:(row % t + 1) * d]
                        dve.wait_ge(med, steps[0] - HALF * t + row + 1)
                        dve.match_replace(part, eight[:, row, :], part, -3.0e38).then_inc(med, 1)
                    steps[0] += HALF * t
                dve.wait_ge(med, steps[0])
                dve.tensor_scalar(thr_rows[v][:, :, :].rearrange("p h (i d) -> p (h i) d", d=nd),
                                  eight[:, 0:HALF * t, 7:8].broadcast_to([P, HALF * t, nd]),
                                  THR, None, ALU.mult).then_inc(thr_rows_set, 1)

            def clip(n, v, band, k, blocks):
                part = band_of(v, band)[:, k:k + blocks, :] if v < 2 else raw[2][:, LH:HH + 1, 0, :]
                dst = clipped[:, n % 2, 0:blocks, :]
                bound = thr_sb[:, :].unsqueeze(1).broadcast_to([P, blocks, IM])
                wait(dve, soft_done, n - 1)
                if v == 0:
                    dve.wait_ge(raw_in[band], 16 * TL[0])
                dve.tensor_tensor(dst, part, bound, ALU.min).then_inc(low_cut, 1)
                dve.wait_ge(low_cut, n + 1)
                dve.scalar_tensor_tensor(dst, bound, -1.0, dst, ALU.mult, ALU.max).then_inc(clip_done, 1)

            def take_thr(v):
                dve.wait_ge(thr_done, v + 1)
                wait(dve, clip_done, sum(c[0] < v for c in cuts))
                dve.tensor_copy(thr_sb[:, :], thr[:, 0:IM]).then_inc(thr_copied, 1)
                dve.wait_ge(thr_copied, v + 1)

            medians(0)
            take_thr(0)
            for n, cut in enumerate(cuts):
                if cut == (0, HIGH[2], 0, 4):
                    medians(1)
                    medians(2)
                if cut[0] and cut[0] != cuts[n - 1][0]:
                    take_thr(cut[0])
                clip(n, *cut)

        @block.gpsimd
        def _(pool):
            for n, (v, band, k, blocks) in enumerate(cuts):
                part = band_of(v, band)[:, k:k + blocks, :] if v < 2 else raw[2][:, LH:HH + 1, 0, :]
                pool.wait_ge(clip_done, n + 1)
                pool.tensor_tensor(part, part, clipped[:, n % 2, 0:blocks, :], ALU.subtract).then_inc(soft_done, 1)


def synthesis_phase(nc, z, x1_s, out_w, out_b, d_inv, t_inv, out):
    with ExitStack() as ctx:
        sb = lambda name, shape, dt=F32: ctx.enter_context(nc.sbuf_tensor(name, shape, dt))
        sem = lambda name: ctx.enter_context(nc.semaphore(name))
        pb = lambda name, shape, dt=F32: ctx.enter_context(nc.psum_tensor(name, shape, dt))
        R = 2 * TL[0]

        z = z[:, :, :, :, :].rearrange("p d b r m -> p d (b r) m")
        zc = [sb(f"zc{e}", [P, 2, NT, R, 4]) for e in range(2)]
        x1 = [sb(f"x1s_{e}", [P, NT, C]) for e in range(2)]
        res = [sb(f"res{e}", [P, NT, C]) for e in range(2)]
        v_sb = [sb(f"v_sb{e}", [P, BANK]) for e in range(2)]
        w_out = sb("w_out", [P, CT, C])
        w_dinv = sb("w_dinv", [P, CT, 2, P])
        wd = sb("wd", [P, 2, C])
        w_tinv = sb("w_tinv", [P, P])
        b_out = sb("b_out", [P, C])

        vbank = [pb(f"vbank{i}", [P, BANK]) for i in range(2)]
        fbank = [pb(f"fbank{i}", [P, BANK]) for i in range(2)]
        wbank = pb("wbank", [P, BANK])

        consts_in = sem("s_consts_in")
        x1_in = [sem(f"x1_in{e}") for e in range(2)]
        wd_done = sem("wd_done")
        wd_ready = sem("wd_ready")
        zc_ready = sem("zc_ready")
        with_bias = sem("with_bias")
        v_done = sem("v_done")
        v_ready = sem("v_ready")
        f_done = sem("f_done")
        res_ready = sem("res_ready")
        out_stored = [sem(f"out_stored{e}") for e in range(2)]

        block = ctx.enter_context(nc.Block())

        def over_images(engine, body):
            body(0, 0)
            body(1, 1)
            with engine.Fori(1, B // 2) as i:
                body(2 * i, 0)
                body(2 * i + 1, 1)

        def over_all_but_last(engine, body):
            body(0, 0)
            body(1, 1)
            with engine.Fori(1, B // 2 - 1) as i:
                body(2 * i, 0)
                body(2 * i + 1, 1)
            body(B - 2, 0)

        @block.sync
        def _(sp):
            for dst, src in ((w_out[:, :, :], out_w.rearrange("(k p) o -> p k o", p=P)),
                             (w_dinv[:, :, :, :].rearrange("p a b c -> p (a b c)"), d_inv),
                             (w_tinv[:, :], t_inv),
                             (b_out[:, :], out_b.unsqueeze(0).broadcast_to([P, C]))):
                sp.dma_start(dst, src).then_inc(consts_in, 16)

            def load(b, e):
                wait(sp, res_ready, 4 * (b - 1))
                sp.dma_start(x1[e][:, :, :], x1_s[bass.ds(b * N, N), :].rearrange("(p t) c -> p t c", t=NT)
                             ).then_inc(x1_in[e], 16)

            def store(b, e):
                sp.wait_ge(res_ready, 4 * b + 4)
                sp.dma_start(out[bass.ds(b * N, N), :].rearrange("(p t) c -> p t c", t=NT),
                             res[e][:, :, :]).then_inc(out_stored[e], 16)

            def image(b, e):
                load(b + 1, 1 - e)
                store(b, e)
            load(0, 0)
            over_all_but_last(sp, image)
            store(B - 1, 1)
            for s in out_stored:
                sp.wait_ge(s, 16 * B // 2)

        @block.gpsimd
        def _(pool):
            pool.wait_ge(consts_in, 64)

            def image(b, e):
                pool.wait_ge(x1_in[e], 16 * ((b - e) // 2 + 1))
                pool.tensor_tensor(x1[e][:, :, :], x1[e][:, :, :],
                                   b_out[:, :].unsqueeze(1).broadcast_to([P, NT, C]), ALU.add).then_inc(with_bias, 1)
            over_images(pool, image)

        @block.tensor
        def _(pe):
            pe.wait_ge(consts_in, 64)
            for bd in range(2):
                for kt in range(CT):
                    m = pe.matmul(wbank[:, bd * C:(bd + 1) * C], w_dinv[:, kt, bd, :], w_out[:, kt, :],
                                  start=(kt == 0), stop=(kt == CT - 1))
            m.then_inc(wd_done, 1)
            pe.wait_ge(wd_ready, 1)

            def columns(b, e, n):
                if n == 0:
                    pe.wait_ge(zc_ready, b + 1)
                wait(pe, v_ready, bank_free(b, n))
                for t in range(2):
                    for bd in range(2):
                        m = pe.matmul(vbank[n % 2][:, t * C:(t + 1) * C],
                                      zc[e][:, bd, 2 * n + t].rearrange("p r w -> p (r w)"),
                                      wd[:, bd, :], start=(bd == 0), stop=(bd == 1))
                m.then_inc(v_done, 1)

            def rows(b, e, n):
                pe.wait_ge(v_ready, 4 * b + n + 1)
                wait(pe, res_ready, bank_free(b, n))
                pe.matmul(fbank[n % 2][:, :], w_tinv[:, :], v_sb[n % 2][:, :],
                          start=True, stop=True).then_inc(f_done, 1)

            def image(b, e):
                for n in range(4):
                    columns(b, e, n)
                    if n:
                        rows(b, e, n - 1)
                rows(b, e, 3)
            over_images(pe, image)

        @block.scalar
        def _(act):
            act.wait_ge(wd_done, 1)
            act.activation(wd[:, :, :].rearrange("p a b -> p (a b)"), wbank[:, :], ACT.Copy).then_inc(wd_ready, 1)

            def image(b, e):
                for n in range(4):
                    act.wait_ge(v_done, 4 * b + n + 1)
                    wait(act, f_done, bank_free(b, n))
                    act.activation(v_sb[n % 2][:, :], vbank[n % 2][:, :], ACT.Copy).then_inc(v_ready, 1)
            over_images(act, image)

        @block.vector
        def _(dve):
            def columns_of(b, e):
                wait(dve, v_done, 4 * b - 4)
                for bd in range(2):
                    src = z[:, bd, :, bass.ds(b * W, W)].rearrange("p r (w t) -> p t r w", t=NT)
                    m = dve.tensor_copy(zc[e][:, bd], src)
                m.then_inc(zc_ready, 1)

            def image(b, e):
                columns_of(b + 1, 1 - e)
                add(b, e)

            def add(b, e):
                dve.wait_ge(with_bias, b + 1)
                wait(dve, out_stored[e], 16 * ((b - e) // 2))
                for n in range(4):
                    dve.wait_ge(f_done, 4 * b + n + 1)
                    cols = lambda s: s[:, 2 * n:2 * n + 2, :].rearrange("p t c -> p (t c)")
                    dve.tensor_tensor(cols(res[e]), fbank[n % 2][:, :], cols(x1[e]), ALU.add).then_inc(res_ready, 1)
            columns_of(0, 0)
            over_all_but_last(dve, image)
            add(B - 1, 1)


def build(nc, a):
    scratch = lambda name, *shape: nc.dram_tensor(name, shape, F32).ap()
    q_s, k_s, v_s = (scratch(n, B * C, N) for n in ("q_s", "k_s", "v_s"))
    conv_phase(nc, a["x"], a["wq"], a["wv"], a["wk"], a["bq"], a["bv"], a["bk"], a["mean_op"], a["ident"],
               q_s, k_s, v_s)
    x1_s = scratch("x1_s", B * N, C)
    bands_s = scratch("bands_s", 4, TL[0], DL[0], C)
    synth_s = scratch("synth_s", 4, P, NB[0], C)
    ktab_s = scratch("ktab_s", 1, KROWS * KCOLS)
    with ExitStack() as ctx:
        sb = lambda name, shape: ctx.enter_context(nc.sbuf_tensor(name, shape, F32))
        conv_ops = [[sb(f"conv_op{v}{k}", [P, P]) for k in range(3 if NB[v] > 1 else 1)] for v in range(LEVELS)]
        conv_bias = sb("conv_bias", [P, 1])
        with nc.sbuf_tensor("heads_out", [P, NT, HEADS, HD], F32) as heads_out:
            attention_phase(nc, q_s, k_s, v_s, a["ident16"], a["ident"], heads_out)
            analysis_phase(nc, a["x"], heads_out, a["wp"], a["mean_op"], a["ident"], a["t_op"], a["d_op"],
                           [a[f"w{i}"] for i in range(6)], [a[f"b{i}"] for i in range(6)],
                           conv_ops, conv_bias, ktab_s, x1_s, bands_s)
        level0 = ctx.enter_context(nc.sbuf_tensor("level0", [P, 2, 2, NB[0], C], F32))
        z_in = ctx.enter_context(nc.semaphore("z_in"))
        bands_phase(nc, bands_s, conv_ops, conv_bias, a["ident"], a["dwt1"], a["dwt2"], a["inv2"], a["inv1"],
                    level0, z_in, synth_s)
        synthesis_phase(nc, level0, x1_s, a["out_w"], a["out_b"], a["d_inv"], a["t_inv"], a["out"])


def arrays_of(inputs):
    taps_first = lambda w: np.ascontiguousarray(np.transpose(w, (2, 3, 1, 0))).reshape(-1, C)
    a = {
        "x": np.ascontiguousarray(inputs["x"]).reshape(B * N, C),
        "wq": taps_first(inputs["L0_conv_w3"]), "bq": inputs["L0_conv_b3"],
        "wv": taps_first(inputs["L0_conv_w5"]), "bv": inputs["L0_conv_b5"],
        "wk": taps_first(inputs["L0_conv_w7"]), "bk": inputs["L0_conv_b7"],
        "wp": np.ascontiguousarray(np.transpose(inputs["L0_conv_wp"])),
        "out_w": np.ascontiguousarray(np.transpose(inputs["L1_conv_out_w"])), "out_b": inputs["L1_conv_out_b"],
        "mean_op": np.full((P, P), 1.0 / (N * CG), np.float32),
        "ident": np.eye(P, dtype=np.float32), "ident16": np.eye(P, dtype=np.float16),
        **wavelet_constants(),
    }
    for i in range(6):
        a[f"w{i}"] = np.ascontiguousarray(inputs[f"L1_conv_w{i}"]).reshape(1, 2 * i + 1, 2 * i + 1)
        a[f"b{i}"] = inputs[f"L1_conv_b{i}"]
    return a


def kernel(**inputs):
    import concourse.bacc as bacc
    from concourse.bass_utils import run_bass_kernel_spmd

    arrays = {f"in_{k}": np.ascontiguousarray(v) for k, v in arrays_of(inputs).items()}
    nc = bacc.Bacc("TRN2", target_bir_lowering=False, num_devices=1)
    a = {k[3:]: nc.dram_tensor(k, v.shape, mybir.dt.from_np(v.dtype), kind="ExternalInput").ap()
         for k, v in arrays.items()}
    a["out"] = nc.dram_tensor("out_0", (B * N, C), F32, kind="ExternalOutput").ap()
    build(nc, a)
    results = run_bass_kernel_spmd(nc, [arrays], core_ids=[0]).results
    return results[0]["out_0"].reshape(B, H, W, C)
```

```python
from contextlib import ExitStack

import numpy as np

import concourse.bass as bass
from concourse import mybir
from concourse.alu_op_type import AluOpType as ALU

F32 = mybir.dt.float32
F16 = mybir.dt.float16
ACT = mybir.ActivationFunctionType
AX = mybir.AxisListType

P = 128
B, H, W, C = 8, 32, 32, 256
N = H * W
CT = C // P
G = 32
CG = C // G
NT = N // P
HD = 16
NH = C // HD
HEADS = B * NH
EPS = 1e-5
BANK = 512

PAD = 2
PW = W + 2 * PAD
PH = H + 2 * PAD
X_SCALE = 64.0
W_SCALE = 256.0
QK_SCALE = 16.0


def wait(engine, sem, value):
    if not (isinstance(value, int) and value <= 0):
        engine.wait_ge(sem, value)


def bank_free(b, n):
    return 4 * b + max(n - 1, 0)


POINTS = {"v": 4, "k": 8}


def conv_phase(nc, x, wq, wv, wk, bq, bv, bk, mean_op, ident, q_s, k_s, v_s):
    tiles = [("q", co, half) for co in range(CT) for half in range(2)]
    tiles += [("v", co, p) for co in range(CT) for p in (1, 2, 0, 3)]
    tiles += [("k", co, r) for co in range(CT) for r in range(4)]
    K_PAIRS = ((1, 2), (3, 4), (5, 6), (0, 7))
    KG = PW // 4
    GROUPS = PH * KG
    NTILE = len(tiles)
    Q_TILES, V_TILES = 4, 8
    NACC = 4
    NSTAGE = 3
    SIDE = {"q": 1, "v": 3, "k": 5}
    HALF_W = W // 2
    FIRST = {"q": 0, "v": 1, "k": 1 + 3 * POINTS["v"]}
    NSIDES = FIRST["k"] + 5 * POINTS["k"]
    pieces = [("q", wq, 0, 1, kt, 0) for kt in range(CT)]
    pieces += [(n, w, y * SIDE[n], SIDE[n], kt, FIRST[n] + y * POINTS[n])
               for n, w in (("v", wv), ("k", wk)) for y in range(SIDE[n]) for kt in range(CT)]
    parts_of = {"q": CT, "v": CT * 4, "k": CT * 9}
    STATS1_AFTER, STATS2_AFTER, TURN_AFTER = 12, 14, (16, 16, 17, 17)

    with ExitStack() as ctx:
        sb = lambda name, shape, dt=F32: ctx.enter_context(nc.sbuf_tensor(name, shape, dt))
        sem = lambda name: ctx.enter_context(nc.semaphore(name))

        w_hi = sb("w_hi", [P, NSIDES, CT, C], F16)
        w_lo = sb("w_lo", [P, NSIDES, CT, C], F16)
        w_work = sb("w_work", [P, 8, C])
        x_tok = sb("x_tok", [P, NT, C])
        x_flat = [sb(f"x_flat{ct}", [P, PH * PW + 8]) for ct in range(CT)]
        x_pad = [t[:, 0:PH * PW].rearrange("p (y x) -> p y x", x=PW) for t in x_flat]
        q_hi = [sb(f"q_hi{ct}", [P, H, W], F16) for ct in range(CT)]
        q_lo = [sb(f"q_lo{ct}", [P, H, W], F16) for ct in range(CT)]
        v_hi = [sb(f"v_hi{ct}", [P, POINTS["v"], H + 2, HALF_W], F16) for ct in range(CT)]
        v_lo = [sb(f"v_lo{ct}", [P, POINTS["v"], H + 2, HALF_W], F16) for ct in range(CT)]
        k_mem = sb("k_mem", [P, CT * 2 * POINTS["k"] * GROUPS], F16)
        k_parts = k_mem[:, :].rearrange("p (c h a g) -> p c h a g", c=CT, h=2, g=GROUPS)
        k_hi, k_lo = ([k_parts[:, ct, h] for ct in range(CT)] for h in range(2))
        early = k_mem[:, :].bitcast(F32)[:, 0:18 * C].rearrange("p (a c) -> p a c", c=C)
        w_stages = (early[:, 0:5], early[:, 5:10], x_tok[:, 0:5])
        w_works = (w_work, early[:, 10:18])
        work = sb("work", [P, 4 * 2 * GROUPS])
        x_sq = work[:, 0:NT * C].rearrange("p (t c) -> p t c", c=C)
        DIFF = PH * (PW - 2)
        diff = work[:, 0:DIFF].rearrange("p (y x) -> p y x", y=PH)
        side = work[:, DIFF:DIFF + 2 * PH * HALF_W].rearrange("p (i y x) -> p i y x", i=2, y=PH)
        pairs_k = [work[:, 2 * GROUPS * i:2 * GROUPS * (i + 1)].rearrange("p (g s) -> p g s", s=2) for i in range(4)]
        w_flat = w_work[:, :, :].rearrange("p a c -> p (a c)")
        side_k = [w_flat[:, 2 * GROUPS * i:2 * GROUPS * (i + 1)].rearrange("p (i g) -> p i g", i=2) for i in range(2)]
        group_part = sb("group_part", [P, 2, G])
        spread = sb("spread", [P, G])
        spread_inv = sb("spread_inv", [P, G])
        eps = sb("eps", [P, 1])
        bias = sb("bias", [P, 3, CT])
        bias_s = sb("bias_s", [P, 3, CT])
        mean_w = sb("mean_w", [P, P])
        ident_w = sb("ident_w", [P, P])
        prod = sb("prod", [P, 3, BANK])
        both = sb("both", [P, 2, BANK])
        QUAD = BANK // 2
        second = prod[:, 2, 0:QUAD]
        sd = prod[:, 0].rearrange("p (i n) -> p i n", i=2)
        ends = prod[:, 1].rearrange("p (i n) -> p i n", i=2)
        ys = both[:, :, :].rearrange("p a (b n) -> p (a b) n", b=2)
        out_stage = sb("out_stage", [P, 2, N])

        acc = [ctx.enter_context(nc.psum_tensor(f"acc{i}", [P, BANK], F32)) for i in range(NACC)]
        stat = ctx.enter_context(nc.psum_tensor("stat", [P, BANK], F32))
        turned = [ctx.enter_context(nc.psum_tensor(f"turned{i}", [P, BANK], F32)) for i in range(2)]

        consts_in = sem("consts_in")
        piece_in = [sem(f"piece_in{i}") for i in range(NSTAGE)]
        w_step = sem("w_step")
        w_made = sem("w_made")
        w_scaled = sem("w_scaled")
        w_hi_ready = sem("w_hi_ready")
        w_lo_ready = sem("w_lo_ready")
        piece_done = sem("piece_done")
        x_in = sem("x_in")
        borders_set = sem("borders_set")
        bias_ready = sem("bias_ready")
        part_ready = sem("part_ready")
        stat_ready = sem("stat_ready")
        centred = sem("centred")
        squared = sem("squared")
        spread_ready = sem("spread_ready")
        inv_ready = sem("inv_ready")
        normed = sem("normed")
        turned_ready = sem("turned_ready")
        pad_ready = sem("pad_ready")
        q_hi_ready = sem("q_hi_ready")
        q_ready = sem("q_ready")
        v_made = sem("v_made")
        v_hi_ready = sem("v_hi_ready")
        v_ready = sem("v_ready")
        k_step = sem("k_step")
        k_made = sem("k_made")
        k_hi_ready = sem("k_hi_ready")
        k_ready = sem("k_ready")
        conv_done = sem("conv_done")
        emptied = {e: sem("emptied_by_" + e) for e in ("act", "dve")}
        summed = sem("summed")
        out_q = sem("out_q")
        k_copied = sem("k_copied")
        out_vk = sem("out_vk")
        out_k_mid = sem("out_k_mid")
        out_stored = [sem(f"out_stored{i}") for i in range(CT)]

        by = ["dve" if (name == "v" and p == 2) or (name == "k" and p < 3) else "act"
              for name, _, p in tiles]
        place = [by[:n].count(by[n]) for n in range(NTILE)]
        per_image = {e: by.count(e) for e in ("act", "dve")}
        number = {t: n for n, t in enumerate(tiles)}
        SLOT = {("v", 1): 0, ("v", 0): 1, ("v", 3): 2}
        SUMS = {"v": 4, "k": 16}
        SUMS_IMAGE = CT * (SUMS["v"] + SUMS["k"])
        SUMS_BEFORE = {("v", 0): 0, ("v", 1): 4, ("k", 0): 8, ("k", 1): 24}

        block = ctx.enter_context(nc.Block())

        def over_images(engine, body):
            body(0, True)
            with engine.Fori(1, B - 1) as b:
                body(b, True)
            body(B - 1, False)

        def filter_cuts(name):
            if name == "q":
                return ((slice(0, 1), ("stage", 0), W_SCALE),)
            if name == "v":
                return ((slice(1, 3), ("made", 0), W_SCALE / 2), (slice(0, 1), ("stage", 0), -W_SCALE),
                        (slice(3, 4), ("stage", 2), W_SCALE))
            return ((slice(1, 3), ("made", 0), -W_SCALE * 2 / 9), (slice(3, 5), ("made", 2), W_SCALE / 90),
                    (slice(5, 7), ("made", 4), W_SCALE * 2 / 45),
                    (slice(0, 1), ("stage", 0), -W_SCALE), (slice(7, 8), ("stage", 4), W_SCALE))

        def cut_source(n, source):
            kind, at = source
            return w_stages[stage_of[n]][:, at:at + 1] if kind == "stage" else w_works[n % 2][:, at:at + 2]

        cuts_before = [sum(len(filter_cuts(p[0])) for p in pieces[:n]) for n in range(len(pieces) + 1)]
        made_in = {"q": 0, "v": 1, "k": 3}
        made_before = [sum(made_in[p[0]] for p in pieces[:n]) for n in range(len(pieces) + 1)]
        stage_of = [n % 2 if n < 8 else (n - 8) % NSTAGE for n in range(len(pieces))]
        fills = [stage_of[:n + 1].count(stage_of[n]) for n in range(len(pieces))]
        EARLY, MIDDLE, LATE = range(0, 5), range(5, 8), range(8, len(pieces))

        def out_scale(name):
            return (1.0 if name == "v" else QK_SCALE) / (X_SCALE * W_SCALE)

        @block.sync
        def _(sp):
            sp.dma_start(x_tok[:, :, :], x[0:N, :].rearrange("(t p) c -> p t c", p=P)).then_inc(x_in, 16)
            sp.dma_start(mean_w[:, :], mean_op).then_inc(consts_in, 16)
            sp.dma_start(ident_w[:, :], ident).then_inc(consts_in, 16)
            for i, b in enumerate((bq, bv, bk)):
                sp.dma_start(bias[:, i, :], b.rearrange("(a p) -> p a", p=P),
                             allow_slow_non_contiguous=True).then_inc(consts_in, 16)

            def load_piece(n):
                _, w, t0, taps, kt, _ = pieces[n]
                if fills[n] > 1:
                    sp.wait_ge(piece_done, max(m for m in range(n) if stage_of[m] == stage_of[n]) + 1)
                elif stage_of[n] == 2:
                    sp.wait_ge(turned_ready, 4)
                rows = w.rearrange("(t k p) c -> k p t c", k=CT, p=P)[kt][:, t0:t0 + taps]
                sp.dma_start(w_stages[stage_of[n]][:, 0:taps], rows).then_inc(piece_in[stage_of[n]], 16)

            def next_x(b):
                sp.wait_ge(turned_ready, 4 * b + 4)
                sp.dma_start(x_tok[:, :, :],
                             x[bass.ds((b + 1) * N, N), :].rearrange("(t p) c -> p t c", p=P)).then_inc(x_in, 16)

            def store(b, c, co):
                if c == 0:
                    sp.wait_ge(out_q, 4 * b + 2 * co + 2)
                else:
                    sp.wait_ge(out_vk, 4 * b + 2 * (c - 1) + co + 1)
                dst = (q_s, v_s, k_s)[c]
                sp.dma_start(dst[bass.ds(b * C + co * P, P), :], out_stage[:, co]).then_inc(out_stored[co], 16)

            stores = [(c, co) for c in range(3) for co in range(CT)]

            for n in range(len(pieces)):
                if n == LATE[4] + NSTAGE:
                    for c, co in stores[:3]:
                        store(0, c, co)
                load_piece(n)
            sp.wait_ge(piece_done, len(pieces))
            next_x(0)

            def image(b, more):
                first = isinstance(b, int) and b == 0
                if more and not first:
                    next_x(b)
                for c, co in stores[3 if first else 0:]:
                    store(b, c, co)
            over_images(sp, image)
            for s in out_stored:
                sp.wait_ge(s, 16 * 3 * B)

        @block.gpsimd
        def _(pool):
            for ct in range(CT):
                pool.memset(x_flat[ct][:, :], 0.0).then_inc(borders_set, 1)
            pool.memset(eps[:, :], EPS / X_SCALE ** 2).then_inc(borders_set, 1)

            for n, (name, _, _, _, kt, first) in enumerate(pieces):
                for i, (sides, source, _) in enumerate(filter_cuts(name)):
                    at = slice(first + sides.start, first + sides.stop)
                    pool.wait_ge(w_hi_ready, cuts_before[n] + i + 1)
                    pool.tensor_tensor(w_lo[:, at, kt], cut_source(n, source), w_hi[:, at, kt],
                                       ALU.subtract).then_inc(w_lo_ready, 1)
                pool.wait_ge(w_lo_ready, cuts_before[n + 1])
                pool.sem_inc(piece_done, 1)

        def inside(pad, half):
            return pad[:, PAD + half * H // 2:PAD + (half + 1) * H // 2, PAD:PAD + W]

        VY = slice(PAD - 1, PAD + H + 1)

        def columns(a, c):
            return a[:, :, c:c + 2 * HALF_W - 1:2]

        def v_sources():
            return (diff[:, VY, 1:1 + W].rearrange("p y (j s) -> p s y j", s=2), side[:, :, VY])

        V_SIDES = (slice(0, 4, 3), slice(1, 3))
        K_SIDES = (slice(0, 8, 7), slice(1, 3), slice(3, 5), slice(5, 7))

        def k_side(r):
            return pairs_k[0].rearrange("p g s -> p s g") if r == 0 else side_k[(r - 1) % 2]

        @block.vector
        def _(dve):
            over = lambda s: s.unsqueeze(1).unsqueeze(3).broadcast_to([P, NT, G, CG])
            tiled = x_tok[:, :, :].rearrange("p t (g c) -> p t g c", g=G)
            steps = [0]

            def make_filters(which):
                def step(instruction):
                    steps[0] += 1
                    instruction.then_inc(w_step, 1)

                def settle():
                    dve.wait_ge(w_step, steps[0])

                for n in which:
                    name = pieces[n][0]
                    tap = lambda i: w_stages[stage_of[n]][:, i]
                    taps = lambda i: w_stages[stage_of[n]][:, i:i + 2]
                    made, sums = w_works[n % 2][:, 0:6], w_works[n % 2][:, 6:8]
                    even, odd = sums[:, 0], sums[:, 1]
                    if name == "q":
                        continue
                    dve.wait_ge(piece_in[stage_of[n]], 16 * fills[n])
                    wait(dve, w_lo_ready, cuts_before[n - 1])
                    if name == "v":
                        step(dve.tensor_tensor(even, tap(0), tap(2), ALU.add))
                        settle()
                        dve.tensor_tensor(made[:, 0], even, tap(1), ALU.add)
                        dve.tensor_tensor(made[:, 1], even, tap(1), ALU.subtract).then_inc(w_made, 1)
                    if name == "k":
                        step(dve.tensor_tensor(sums, taps(0), taps(2), ALU.add))
                        settle()
                        step(dve.tensor_tensor(even, even, tap(4), ALU.add))
                        settle()
                        dve.tensor_tensor(made[:, 0], even, odd, ALU.add)
                        dve.tensor_tensor(made[:, 1], even, odd, ALU.subtract).then_inc(w_made, 1)
                        dve.wait_ge(w_made, made_before[n] + 1)
                        step(dve.scalar_tensor_tensor(sums, taps(2), 4.0, taps(0), ALU.mult, ALU.add))
                        settle()
                        step(dve.scalar_tensor_tensor(even, tap(4), 16.0, even, ALU.mult, ALU.add))
                        settle()
                        dve.scalar_tensor_tensor(made[:, 2], odd, 2.0, even, ALU.mult, ALU.add)
                        dve.scalar_tensor_tensor(made[:, 3], odd, -2.0, even, ALU.mult, ALU.add).then_inc(w_made, 1)
                        dve.wait_ge(w_made, made_before[n] + 2)
                        step(dve.scalar_tensor_tensor(sums, taps(0), 4.0, taps(2), ALU.mult, ALU.add))
                        settle()
                        step(dve.scalar_tensor_tensor(even, even, 4.0, tap(4), ALU.mult, ALU.add))
                        settle()
                        dve.scalar_tensor_tensor(made[:, 4], odd, 2.0, even, ALU.mult, ALU.add)
                        dve.scalar_tensor_tensor(made[:, 5], odd, -2.0, even, ALU.mult, ALU.add).then_inc(w_made, 1)

            def first_sum(b):
                dve.wait_ge(x_in, 16 * (b + 1))
                dve.tensor_reduce(group_part[:, 0], x_tok[:, :, :].rearrange("p t (g c) -> p g t c", g=G),
                                  AX.XY, ALU.add).then_inc(part_ready, 1)

            def centre(b):
                dve.wait_ge(stat_ready, 2 * b + 1)
                dve.tensor_tensor(tiled, tiled, over(stat[:, 0:G]), ALU.subtract).then_inc(centred, 1)

            def second_sum(b):
                dve.wait_ge(squared, b + 1)
                dve.tensor_reduce(group_part[:, 1], x_sq.rearrange("p t (g c) -> p g t c", g=G),
                                  AX.XY, ALU.add).then_inc(part_ready, 1)

            def scale(b):
                dve.wait_ge(spread_ready, b + 1)
                dve.reciprocal(spread_inv[:, :], spread[:, :]).then_inc(inv_ready, 1)
                dve.wait_ge(inv_ready, b + 1)
                dve.tensor_tensor(tiled, tiled, over(spread_inv[:, :]), ALU.mult).then_inc(normed, 1)

            def pad(b, n):
                ct, half = n // 2, n % 2
                dve.wait_ge(turned_ready, 4 * b + n + 1)
                dve.tensor_copy(inside(x_pad[ct], half),
                                turned[n % 2][:, :].rearrange("p (h w) -> p h w", w=W)).then_inc(pad_ready, 1)

            def cut_q(b):
                for ct in range(CT):
                    dve.wait_ge(q_hi_ready, 2 * b + ct + 1)
                    dve.tensor_tensor(q_lo[ct][:, :, :], x_pad[ct][:, PAD:PAD + H, PAD:PAD + W],
                                      q_hi[ct][:, :, :], ALU.subtract).then_inc(q_ready, 1)

            def sides_v(b):
                dve.wait_ge(pad_ready, 4 * b + 4)
                for ct in range(CT):
                    a = x_pad[ct]
                    wait(dve, v_ready, 4 * b + 2 * ct)
                    dve.tensor_tensor(diff[:, VY], a[:, VY, 2:PW], a[:, VY, 0:PW - 2],
                                      ALU.subtract).then_inc(v_made, 1)
                    dve.tensor_tensor(side[:, 0, VY], columns(a, 3)[:, VY], columns(a, 2)[:, VY], ALU.add)
                    dve.tensor_tensor(side[:, 1, VY], columns(a, 3)[:, VY], columns(a, 2)[:, VY],
                                      ALU.subtract).then_inc(v_made, 1)
                    for i, (src, sides) in enumerate(zip(v_sources(), V_SIDES)):
                        n = 4 * b + 2 * ct + i
                        dve.wait_ge(v_hi_ready, n + 1)
                        dve.tensor_tensor(v_lo[ct][:, sides], src, v_hi[ct][:, sides], ALU.subtract).then_inc(v_ready, 1)

            def sides_k(b, ct):
                two = lambda c: x_flat[ct][:, c:c + 4 * GROUPS].rearrange("p (g s) -> p g s", s=4)[:, :, 0:2]
                w0, w1, w2, w3 = pairs_k
                before, made = 16 * b + 8 * ct, 8 * b + 4 * ct
                stt = lambda out, a, f, c: dve.scalar_tensor_tensor(out, a, f, c, ALU.mult, ALU.add)
                wait(dve, k_ready, made)
                dve.tensor_tensor(w3, two(2), two(4), ALU.subtract).then_inc(k_step, 1)
                dve.tensor_tensor(w0, two(6), two(0), ALU.subtract).then_inc(k_step, 1)
                dve.tensor_tensor(w1, two(5), two(1), ALU.add).then_inc(k_step, 1)
                dve.wait_ge(k_step, before + 2)
                stt(w0, w3, 21 / 4, w0).then_inc(k_made, 1)
                stt(w2, two(1), 1 / 4, two(5)).then_inc(k_step, 1)
                dve.wait_ge(k_step, before + 4)
                stt(w1, two(3), -17 / 4, w1).then_inc(k_step, 1)
                stt(w2, two(3), -5 / 4, w2).then_inc(k_step, 1)
                dve.wait_ge(k_made, made + 1)
                stt(w3, two(1), 4.0, two(5)).then_inc(k_step, 1)
                dve.wait_ge(k_step, before + 7)
                stt(w3, two(3), -5.0, w3).then_inc(k_step, 1)
                dve.wait_ge(k_step, before + 8)

                def make(r):
                    if r == 3:
                        dve.wait_ge(k_ready, made + 2)
                    w, f = ((w1, 1.0), (w2, 2.0), (w3, 0.5))[r - 1]
                    stt(k_side(r)[:, 0], w[:, :, 0], f, w[:, :, 1])
                    stt(k_side(r)[:, 1], w[:, :, 0], -f, w[:, :, 1]).then_inc(k_made, 1)

                def cut(r):
                    dve.wait_ge(k_made, made + r + 1)
                    dve.wait_ge(k_hi_ready, made + r + 1)
                    dve.tensor_tensor(k_lo[ct][:, K_SIDES[r]], k_side(r), k_hi[ct][:, K_SIDES[r]],
                                      ALU.subtract).then_inc(k_ready, 1)

                make(1)
                make(2)
                cut(0)
                cut(1)
                make(3)
                cut(2)
                cut(3)

            def take_v(b, co):
                n = number["v", co, 2]
                s = SUMS_IMAGE * b + SUMS_BEFORE["v", co]
                psum = acc[n % NACC][:, :]
                dve.wait_ge(emptied["act"], per_image["act"] * b + place[n - 1] + 1)
                dve.wait_ge(conv_done, NTILE * b + n + 1)
                dve.tensor_tensor(both[:, 0], psum, prod[:, 0], ALU.add).then_inc(summed, 1)
                dve.scalar_tensor_tensor(both[:, 1], psum, -1.0, prod[:, 0], ALU.mult, ALU.add).then_inc(summed, 1)
                dve.wait_ge(summed, s + 2)
                dve.sem_inc(emptied["dve"], 1)

            def take_k(b, co, r):
                n = number["k", co, r]
                s = SUMS_IMAGE * b + SUMS_BEFORE["k", co] + (0, 2, 8)[r]
                first_of = acc[n % NACC][:, 0:QUAD]
                stt = lambda out, a, f, c: dve.scalar_tensor_tensor(out, a, f, c, ALU.mult, ALU.add).then_inc(summed, 1)
                total, difference = (ys[:, 2], ys[:, 3]) if r == 0 else (sd[:, 0], sd[:, 1])
                dve.wait_ge(k_copied, 6 * b + 3 * co + r + 1)
                dve.tensor_tensor(total, first_of, second, ALU.add).then_inc(summed, 1)
                dve.tensor_tensor(difference, first_of, second, ALU.subtract).then_inc(summed, 1)
                dve.wait_ge(summed, s + 2)
                dve.sem_inc(emptied["dve"], 1)
                if r == 1:
                    stt(ys[:, 0], total, 1.0, ys[:, 2])
                    stt(ys[:, 1], difference, 2.0, ys[:, 3])
                    dve.wait_ge(summed, s + 4)
                    stt(ys[:, 2], total, 4.0, ys[:, 2])
                    stt(ys[:, 3], difference, 8.0, ys[:, 3])
                if r == 2:
                    for i in range(4):
                        stt(ys[:, i], sd[:, i % 2], 0.5 ** i, ys[:, i])
                if r:
                    dve.wait_ge(summed, s + 6)

            def put_k(b, co):
                n = number["k", co, 3]
                s = SUMS_IMAGE * b + SUMS_BEFORE["k", co] + 14
                dve.wait_ge(emptied["act"], per_image["act"] * b + place[n] + 1)
                dve.wait_ge(out_stored[co], 16 * (3 * b + 2))
                for i, y in enumerate((0, 3)):
                    dve.scalar_tensor_tensor(out_stage[:, co, y:N:4], ys[:, y], out_scale("k"), ends[:, i],
                                             ALU.mult, ALU.add).then_inc(summed, 1)
                dve.wait_ge(summed, s + 2)
                dve.wait_ge(out_k_mid, 2 * b + co + 1)
                dve.sem_inc(out_vk, 1)

            def put_v(b, co):
                s = SUMS_IMAGE * b + SUMS_BEFORE["v", co] + 2
                for i, p in enumerate((0, 3)):
                    n = number["v", co, p]
                    dve.wait_ge(emptied["act"], per_image["act"] * b + place[n] + 1)
                    if i == 0:
                        dve.wait_ge(out_stored[co], 16 * (3 * b + 1))
                    dve.scalar_tensor_tensor(out_stage[:, co, i:N:2], both[:, i], out_scale("v"),
                                             prod[:, 1 + i], ALU.mult, ALU.add).then_inc(summed, 1)
                dve.wait_ge(summed, s + 2)
                dve.sem_inc(out_vk, 1)

            def ready(b):
                for n in range(4):
                    pad(b, n)
                cut_q(b)
                sides_v(b)

            dve.wait_ge(consts_in, 5 * 16)
            dve.tensor_scalar(bias_s[:, :, :], bias[:, :, :], QK_SCALE, None, ALU.mult).then_inc(bias_ready, 1)
            dve.wait_ge(borders_set, CT + 1)
            first_sum(0)
            make_filters(EARLY)
            centre(0)
            make_filters(MIDDLE)
            second_sum(0)
            scale(0)
            ready(0)

            def image(b, more):
                first = isinstance(b, int) and b == 0
                if first:
                    make_filters(LATE[:4])
                else:
                    sides_k(b, 0)
                take_v(b, 0)
                put_v(b, 0)
                if first:
                    make_filters(LATE[4:])
                    dve.wait_ge(w_lo_ready, cuts_before[len(pieces)])
                    sides_k(b, 0)
                sides_k(b, 1)
                take_v(b, 1)
                put_v(b, 1)
                if more:
                    first_sum(b + 1)
                take_k(b, 0, 0)
                if more:
                    centre(b + 1)
                take_k(b, 0, 1)
                if more:
                    second_sum(b + 1)
                take_k(b, 0, 2)
                if more:
                    scale(b + 1)
                put_k(b, 0)
                take_k(b, 1, 0)
                if more:
                    pad(b + 1, 0)
                    pad(b + 1, 1)
                take_k(b, 1, 1)
                if more:
                    pad(b + 1, 2)
                    pad(b + 1, 3)
                    cut_q(b + 1)
                    sides_v(b + 1)
                take_k(b, 1, 2)
                put_k(b, 1)
            over_images(dve, image)

        @block.scalar
        def _(act):
            def cut_filters(which):
                for n in which:
                    name, _, _, _, kt, first = pieces[n]
                    act.wait_ge(piece_in[stage_of[n]], 16 * fills[n])
                    for sides, source, scale in filter_cuts(name):
                        if source[0] == "made":
                            act.wait_ge(w_made, made_before[n] + source[1] // 2 + 1)
                        act.activation(cut_source(n, source), cut_source(n, source), ACT.Copy,
                                       scale=scale).then_inc(w_scaled, 1)
                    for i, (sides, source, _) in enumerate(filter_cuts(name)):
                        at = slice(first + sides.start, first + sides.stop)
                        act.wait_ge(w_scaled, cuts_before[n] + i + 1)
                        act.activation(w_hi[:, at, kt], cut_source(n, source), ACT.Copy).then_inc(w_hi_ready, 1)

            def square(b):
                act.wait_ge(centred, b + 1)
                wait(act, k_ready, 8 * b)
                act.activation(x_sq, x_tok[:, :, :], ACT.Square).then_inc(squared, 1)

            def spread_of(b):
                act.wait_ge(stat_ready, 2 * b + 2)
                act.activation(spread[:, :], stat[:, G:2 * G], ACT.Sqrt, bias=eps[:, 0:1],
                               scale=X_SCALE ** -2).then_inc(spread_ready, 1)

            def high_q(b):
                for ct in range(CT):
                    act.wait_ge(pad_ready, 4 * b + 2 * ct + 2)
                    act.activation(q_hi[ct][:, :, :], x_pad[ct][:, PAD:PAD + H, PAD:PAD + W], ACT.Copy).then_inc(q_hi_ready, 1)

            def high_v(b):
                for ct in range(CT):
                    for i, (src, sides) in enumerate(zip(v_sources(), V_SIDES)):
                        act.wait_ge(v_made, 4 * b + 2 * ct + i + 1)
                        act.activation(v_hi[ct][:, sides], src, ACT.Copy).then_inc(v_hi_ready, 1)

            def high_k(b, ct):
                wait(act, conv_done, NTILE * b)
                if isinstance(b, int) and b == 0 and ct == 1:
                    act.wait_ge(w_lo_ready, cuts_before[len(pieces)])
                for r in range(4):
                    act.wait_ge(k_made, 8 * b + 4 * ct + r + 1)
                    act.activation(k_hi[ct][:, K_SIDES[r]], k_side(r), ACT.Copy).then_inc(k_hi_ready, 1)

            def empty(b, n):
                name, co, p = tiles[n]
                act.wait_ge(conv_done, NTILE * b + n + 1)
                psum = acc[n % NACC][:, :]
                if name == "q":
                    if p == 0:
                        wait(act, out_stored[co], 48 * b)
                    act.activation(out_stage[:, co, p * BANK:(p + 1) * BANK], psum, ACT.Identity,
                                   bias=bias_s[:, 0, co:co + 1], scale=out_scale("q")).then_inc(emptied["act"], 1)
                    act.wait_ge(emptied["act"], per_image["act"] * b + place[n] + 1)
                    act.sem_inc(out_q, 1)
                    return
                s = SUMS_IMAGE * b + SUMS_BEFORE[name, co]
                if name == "k":
                    s += (0, 2, 4, 0)[p]
                wait(act, summed, s)
                if name == "k" and p < 3:
                    act.activation(second, acc[n % NACC][:, QUAD:BANK], ACT.Copy).then_inc(k_copied, 1)
                elif name == "k":
                    act.activation(prod[:, 1], psum, ACT.Identity, bias=bias_s[:, 2, co:co + 1],
                                   scale=out_scale("k")).then_inc(emptied["act"], 1)
                    act.wait_ge(summed, s + 14)
                    act.wait_ge(out_stored[co], 16 * (3 * b + 2))
                    act.activation(out_stage[:, co].rearrange("p (n i) -> p i n", i=4)[:, 1:3], ys[:, 1:3],
                                   ACT.Identity, bias=bias_s[:, 2, co:co + 1],
                                   scale=out_scale("k")).then_inc(out_k_mid, 1)
                elif SLOT[name, p] == 0:
                    act.activation(prod[:, 0], psum, ACT.Copy).then_inc(emptied["act"], 1)
                else:
                    act.activation(prod[:, SLOT[name, p]], psum, ACT.Identity, bias=bias[:, 1, co:co + 1],
                                   scale=out_scale("v")).then_inc(emptied["act"], 1)

            act.wait_ge(borders_set, CT + 1)
            cut_filters(EARLY)
            square(0)
            cut_filters(MIDDLE)
            spread_of(0)
            high_q(0)
            high_v(0)
            act.wait_ge(bias_ready, 1)

            def image(b, more):
                for n in range(NTILE):
                    first = isinstance(b, int) and b == 0
                    if n == 4:
                        if first:
                            cut_filters(LATE[:4])
                        else:
                            high_k(b, 0)
                    if n == 8:
                        if first:
                            cut_filters(LATE[4:])
                            act.wait_ge(w_lo_ready, cuts_before[len(pieces)])
                            high_k(b, 0)
                        high_k(b, 1)
                    if tiles[n][0] == "k" or by[n] == "act":
                        empty(b, n)
                    if more:
                        if n == 12:
                            square(b + 1)
                        if n == 14:
                            spread_of(b + 1)
                        if n == 17:
                            high_q(b + 1)
                            high_v(b + 1)
            over_images(act, image)

        @block.tensor
        def _(pe):
            def stats(b, k):
                pe.wait_ge(part_ready, 2 * b + k + 1)
                if k == 0:
                    wait(pe, spread_ready, b)
                pe.matmul(stat[:, k * G:(k + 1) * G], mean_w[:, :], group_part[:, k],
                          start=True, stop=True).then_inc(stat_ready, 1)

            def transposes(b, n):
                ct, half = n // 2, n % 2
                pe.wait_ge(normed, b + 1)
                wait(pe, pad_ready, 4 * b + max(n - 1, 0))
                for t in range(4):
                    m = pe.transpose(turned[n % 2][:, t * P:(t + 1) * P],
                                     x_tok[:, 4 * half + t, ct * P:(ct + 1) * P], ident_w[:, :])
                m.then_inc(turned_ready, 1)

            def products(b, n):
                name, co, p = tiles[n]
                last = n - NACC
                if last >= 0:
                    pe.wait_ge(emptied[by[last]], per_image[by[last]] * b + place[last] + 1)
                elif not (isinstance(b, int) and b == 0):
                    last += NTILE
                    pe.wait_ge(emptied[by[last]], per_image[by[last]] * (b - 1) + place[last] + 1)
                if n == 0:
                    pe.wait_ge(q_ready, 2 * b + 2)
                if n == Q_TILES:
                    pe.wait_ge(v_ready, 4 * b + 4)
                if n == Q_TILES + V_TILES:
                    pe.wait_ge(k_ready, 8 * b + 8)
                if n in (0, Q_TILES, Q_TILES + V_TILES) and isinstance(b, int) and b == 0:
                    pe.wait_ge(w_lo_ready, cuts_before[parts_of[name]])
                cols = slice(co * P, (co + 1) * P)
                terms = [(y, ct) for y in range(SIDE[name]) for ct in range(CT)]
                for j, point in enumerate(K_PAIRS[p] if name == "k" else (p,)):
                    for i, (y, ct) in enumerate(terms):
                        if name == "q":
                            at = 0
                            hi, lo = (t[ct][:, p * H // 2:(p + 1) * H // 2, :] for t in (q_hi, q_lo))
                        else:
                            at = FIRST[name] + y * POINTS[name] + point
                        if name == "v":
                            hi, lo = (t[ct][:, point, y:y + H, :] for t in (v_hi, v_lo))
                        if name == "k":
                            hi, lo = (t[ct][:, point].rearrange("p (y x) -> p y x", x=KG)[:, y:y + H, 0:W // 4]
                                      for t in (k_hi, k_lo))
                        bank = acc[n % NACC][:, j * QUAD:(j + 1) * QUAD] if name == "k" else acc[n % NACC][:, :]
                        pe.matmul(bank, w_hi[:, at, ct, cols], hi, start=(i == 0), stop=False)
                        pe.matmul(bank, w_hi[:, at, ct, cols], lo, start=False, stop=False)
                        m = pe.matmul(bank, w_lo[:, at, ct, cols], hi, start=False, stop=(i == len(terms) - 1))
                m.then_inc(conv_done, 1)

            pe.wait_ge(consts_in, 5 * 16)
            stats(0, 0)
            stats(0, 1)
            for m in range(4):
                transposes(0, m)

            def image(b, more):
                for n in range(NTILE):
                    products(b, n)
                    if more:
                        if n == STATS1_AFTER:
                            stats(b + 1, 0)
                        if n == STATS2_AFTER:
                            stats(b + 1, 1)
                        for m in range(4):
                            if n == TURN_AFTER[m]:
                                transposes(b + 1, m)
            over_images(pe, image)


def attention_phase(nc, q_s, k_s, v_s, ident16, ident, heads_out):
    D2 = 4 * HD
    ROWS = P
    K_ONE = 256.0
    NKT = 4
    NPT = 4
    VW = 32
    CH = 2
    NSB = 3
    UNITS = NT * CH
    CG4 = 4
    QW = N // CG4
    EXP_SCALE = HD ** -0.5 / QK_SCALE ** 2

    with ExitStack() as ctx:
        sb = lambda name, shape, dt=F32: ctx.enter_context(nc.sbuf_tensor(name, shape, dt))
        sem = lambda name: ctx.enter_context(nc.semaphore(name))
        pb = lambda name, shape, dt=F32: ctx.enter_context(nc.psum_tensor(name, shape, dt))

        raw = {c: [sb(f"raw_{c}{e}", [P, NT, HD]) for e in range(2)] for c in "qkv"}
        q_tok = [sb(f"q_tok{e}", [P, NT, ROWS], F16) for e in range(NKT)]
        k_tok = [sb(f"k_tok{e}", [P, NT, ROWS], F16) for e in range(NKT)]
        v_tok = [sb(f"v_tok{e}", [P, NT, VW]) for e in range(NKT)]
        k_t = [sb(f"k_t{e}", [ROWS, N], F16) for e in range(NKT)]
        qa_t = [sb(f"qa_t{e}", [ROWS, N], F16) for e in range(2)]
        qb_t = [sb(f"qb_t{e}", [ROWS, N], F16) for e in range(2)]
        probs = [sb(f"probs{e}", [P, N]) for e in range(NPT)]
        maxima = sb("maxima", [P, 2, NT, CH])
        neg_max = sb("neg_max", [P, NT])
        o_t = sb("o_t", [P, QW])
        inv_sum = sb("inv_sum", [P, 2, CG4])
        id16 = sb("id16", [P, P], F16)
        id32 = sb("id32", [P, P])

        a_bank = [pb(f"a_bank{i}", [P, BANK]) for i in range(NSB)]
        b_bank = [pb(f"b_bank{i}", [P, BANK]) for i in range(NSB)]
        pv_bank = pb("pv_bank", [P, BANK])
        t_bank = pb("t_bank", [P, BANK])
        t16 = t_bank[:, :].bitcast(F16)

        consts_in = sem("a_consts_in")
        raw_in = {c: [sem(f"raw_in_{c}{e}") for e in range(2)] for c in "qkv"}
        pads_set = sem("pads_set")
        passed = sem("passed")
        hi_cut = sem("hi_cut")
        tok_ready = sem("tok_ready")
        k_turned = sem("k_turned")
        qa_turned = sem("qa_turned")
        qb_turned = sem("qb_turned")
        o_turned = sem("o_turned")
        k_ready = sem("k_ready")
        qa_ready = sem("qa_ready")
        qb_ready = sem("qb_ready")
        a_done = sem("a_done")
        a_read = sem("a_read")
        max_ready = sem("max_ready")
        neg_hi_cut = sem("neg_hi_cut")
        max_rows_set = sem("max_rows_set")
        b_done = sem("b_done")
        exp_done = sem("exp_done")
        pv_done = sem("pv_done")
        o_copied = sem("o_copied")
        inv_done = sem("inv_done")
        o_out = sem("o_out")

        A_AHEAD = 3
        PV_LAG = 3
        ORDER = "BAbTatV"
        TURN = {"k": ((0, 1), (0, 1)), "qa": ((2, 1), (3, 0)), "o": ((4, 1), (4, 1)), "qb": ((6, 1), (6, 1))}
        READ = {"k": 0, "qa": 3, "o": 4, "qb": 6}
        READER = {"k": "act", "qa": "act", "qb": "dve"}
        LEAD = 2

        def over_heads(engine, body):
            exists = lambda x: 0 <= x < HEADS
            for h in range(-LEAD, 4):
                body(h, h % 4, exists)
            with engine.Fori(1, HEADS // 4 - 1) as i:
                for e in range(4):
                    body(4 * i + e, e, lambda x: True)
            for h in range(HEADS - 4, HEADS + 1):
                body(h, h % 4, exists)

        def there(exists, h, d):
            return exists(h + d) if isinstance(h, int) else True

        def read_turned(engine, name, h, e, t, ok):
            for what, lead, dst, turned, ready in (("k", LEAD, k_t[(e + LEAD) % 4], k_turned, k_ready),
                                                   ("qa", LEAD, qa_t[e % 2], qa_turned, qa_ready),
                                                   ("qb", 1, qb_t[(e + 1) % 2], qb_turned, qb_ready)):
                if READER[what] == name and t == READ[what] and ok(lead):
                    engine.wait_ge(turned, h + lead + 1)
                    if name == "act":
                        m = engine.activation(dst[:, :], t16[0:ROWS, :], ACT.Copy)
                    else:
                        m = engine.tensor_copy(dst[:, :], t16[0:ROWS, :])
                    m.then_inc(ready, 1)

        block = ctx.enter_context(nc.Block())

        @block.sync
        def _(sp):
            sp.dma_start(id16[:, :], ident16).then_inc(consts_in, 16)
            sp.dma_start(id32[:, :], ident).then_inc(consts_in, 16)

            def load(h, e):
                for c, src in (("q", q_s), ("k", k_s), ("v", v_s)):
                    wait(sp, tok_ready, h - 1)
                    sp.dma_start(raw[c][e % 2][:, :, :],
                                 src[bass.ds(h * HD, HD), :].rearrange("c (r t d) -> (c r) t d", t=NT, d=HD)
                                 ).then_inc(raw_in[c][e % 2], 16)
            for h in range(4):
                load(h, h % 4)
            with sp.Fori(1, HEADS // 4) as i:
                for e in range(4):
                    load(4 * i + e, e)

        @block.gpsimd
        def _(pool):
            for e in range(NKT):
                pool.memset(k_tok[e][:, :, D2:D2 + 2], K_ONE).then_inc(pads_set, 1)
                pool.memset(k_tok[e][:, :, D2 + 2:ROWS], 0.0).then_inc(pads_set, 1)
                pool.memset(q_tok[e][:, :, D2 + 2:ROWS], 0.0).then_inc(pads_set, 1)
                pool.memset(v_tok[e][:, :, HD:HD + 1], 1.0).then_inc(pads_set, 1)
                pool.memset(v_tok[e][:, :, HD + 1:VW], 0.0).then_inc(pads_set, 1)
            pool.wait_ge(pads_set, 5 * NKT)

            def cut(h, e):
                turn = 16 * (2 * h // 4 + 1) if isinstance(h, int) else None
                qv = q_tok[e][:, :, 0:D2].rearrange("p t (r l d) -> p t r l d", r=2, l=2)
                kv = k_tok[e][:, :, 0:D2].rearrange("p t (l r d) -> p t r l d", r=2, l=2)
                raws = {c: raw[c][e % 2][:, :, :].unsqueeze(2).broadcast_to([P, NT, 2, HD]) for c in "qk"}
                fills = (h - e % 2) // 2 + 1 if isinstance(h, int) else h_fills(h, e)
                wait(pool, qb_turned, h - NKT + 1)
                wait(pool, pv_done, NT * (h - NKT + 1))
                pool.wait_ge(raw_in["q"][e % 2], 16 * fills)
                pool.sem_inc(passed, 1)
                pool.memset(q_tok[e][:, :, D2:D2 + 2], 0.0)
                pool.tensor_copy(qv[:, :, :, 0], raws["q"]).then_inc(hi_cut, 1)
                pool.wait_ge(raw_in["k"][e % 2], 16 * fills)
                pool.sem_inc(passed, 1)
                pool.tensor_copy(kv[:, :, :, 0], raws["k"]).then_inc(hi_cut, 1)
                pool.wait_ge(raw_in["v"][e % 2], 16 * fills)
                pool.sem_inc(passed, 1)
                pool.tensor_copy(v_tok[e][:, :, 0:HD], raw["v"][e % 2][:, :, :])
                pool.wait_ge(hi_cut, 2 * h + 2)
                pool.tensor_tensor(qv[:, :, :, 1], raws["q"], qv[:, :, :, 0], ALU.subtract)
                pool.tensor_tensor(kv[:, :, :, 1], raws["k"], kv[:, :, :, 0], ALU.subtract).then_inc(tok_ready, 1)

            def h_fills(h, e):
                return (h - e) // 2 + e // 2 + 1

            for h in range(4):
                cut(h, h % 4)
            with pool.Fori(1, HEADS // 4) as i:
                for e in range(4):
                    cut(4 * i + e, e)

        @block.tensor
        def _(pe):
            pe.wait_ge(consts_in, 32)

            def last_use(u):
                return u - NSB + 1 if u >= NSB else (UNITS - 1 - u) // NSB * NSB + u + 1 - UNITS

            def turn_tokens(tok, half, done):
                for t in range(half * NT // 2, (half + 1) * NT // 2):
                    m = pe.transpose(t16[0:ROWS, t * P:(t + 1) * P], tok[:, t, :], id16[:, :])
                if half:
                    m.then_inc(done, 1)

            def scores_a(h, e, t, c):
                if t == 0 and c == 0:
                    pe.wait_ge(k_ready, h + 1)
                    pe.wait_ge(qa_ready, h + 1)
                u = CH * t + c
                wait(pe, a_read, h * UNITS + last_use(u))
                pe.matmul(a_bank[u % NSB][:, :], qa_t[e % 2][:, t * P:(t + 1) * P],
                          k_t[e][:, c * BANK:(c + 1) * BANK], start=True, stop=True).then_inc(a_done, 1)

            def scores_b(h, e, t, c):
                u = CH * t + c
                if u == 0:
                    pe.wait_ge(qb_ready, h + 1)
                wait(pe, exp_done, h * UNITS + last_use(u))
                pe.matmul(b_bank[u % NSB][:, :], k_t[e][:, t * P:(t + 1) * P],
                          qb_t[e % 2][:, c * BANK:(c + 1) * BANK], start=True, stop=True).then_inc(b_done, 1)

            def times_v(h, e, t):
                if t == 0:
                    wait(pe, o_copied, h)
                pe.wait_ge(exp_done, h * UNITS + CH * (t + 1))
                for j in range(CG4):
                    m = pe.matmul(pv_bank[VW * j:VW * (j + 1), 0:QW], v_tok[e][:, t, :],
                                  probs[t % NPT][:, j * QW:(j + 1) * QW], start=(t == 0), stop=(t == NT - 1),
                                  tile_position=(0, VW * j))
                m.then_inc(pv_done, 1)

            def head(h, e, exists):
                ok = lambda d: there(exists, h, d)
                def turn(what, half):
                    if what == "k" and ok(LEAD):
                        if half == 0:
                            pe.wait_ge(tok_ready, h + LEAD + 1)
                            wait(pe, qb_ready, h + 1)
                        turn_tokens(k_tok[(e + LEAD) % 4], half, k_turned)
                    if what == "qa" and ok(LEAD):
                        if half == 0:
                            wait(pe, k_ready, h + LEAD + 1)
                        turn_tokens(q_tok[(e + LEAD) % 4], half, qa_turned)
                    if what == "o" and ok(-1):
                        if half == 0:
                            wait(pe, qa_ready, min_heads(h + LEAD + 1))
                            pe.wait_ge(o_copied, h)
                        m = pe.transpose(t_bank[:, half * P:(half + 1) * P], o_t[:, half * P:(half + 1) * P], id32[:, :])
                        if half:
                            m.then_inc(o_turned, 1)
                    if what == "qb" and ok(1):
                        if half == 0:
                            pe.wait_ge(max_rows_set, h + 2)
                            wait(pe, qa_ready, min_heads(h + LEAD + 1))
                            wait(pe, o_out, h)
                        turn_tokens(q_tok[(e + 1) % 4], half, qb_turned)

                def turns(at):
                    for what, halves in TURN.items():
                        for half in range(2):
                            if halves[half] == at:
                                turn(what, half)

                for t in range(NT):
                    d = 1 + (t + A_AHEAD) // NT
                    a_tile = (h + d, (e + d) % 4, (t + A_AHEAD) % NT)
                    for what in ORDER:
                        if what in "Bb" and ok(0):
                            scores_b(h, e, t, 0 if what == "B" else 1)
                        if what in "Tt":
                            turns((t, 0 if what == "T" else 1))
                        if what in "Aa" and ok(d):
                            scores_a(*a_tile, 0 if what == "A" else 1)
                        if what == "V":
                            if t < PV_LAG and ok(-1):
                                times_v(h - 1, (e - 1) % 4, NT - PV_LAG + t)
                            if t >= PV_LAG and ok(0):
                                times_v(h, e, t - PV_LAG)

            def min_heads(v):
                return min(v, HEADS) if isinstance(v, int) else v

            over_heads(pe, head)

        @block.scalar
        def _(act):
            def head(h, e, exists):
                ok = lambda d: there(exists, h, d)
                for t in range(NT):
                    for c in range(CH):
                        if ok(0):
                            u = CH * t + c
                            act.wait_ge(b_done, h * UNITS + u + 1)
                            if c == 0:
                                wait(act, pv_done, h * NT + t - NPT + 1)
                            act.activation(probs[t % NPT][:, c * BANK:(c + 1) * BANK], b_bank[u % NSB][:, :],
                                           ACT.Exp, scale=EXP_SCALE).then_inc(exp_done, 1)
                    read_turned(act, "act", h, e, t, ok)
            over_heads(act, head)

        @block.vector
        def _(dve):
            def maximum(h, e):
                dve.wait_ge(a_read, (h + 1) * NT * CH)
                dve.tensor_reduce(neg_max[:, :], maxima[:, e % 2], AX.X, ALU.max, negate=True).then_inc(max_ready, 1)
                dve.wait_ge(max_ready, h + 1)
                hi = q_tok[e][:, :, D2:D2 + 1].rearrange("p t o -> p (t o)")
                lo = q_tok[e][:, :, D2 + 1:D2 + 2].rearrange("p t o -> p (t o)")
                dve.tensor_scalar(hi, neg_max[:, :], 1 / K_ONE, None, ALU.mult).then_inc(neg_hi_cut, 1)
                dve.wait_ge(neg_hi_cut, h + 1)
                dve.scalar_tensor_tensor(lo, neg_max[:, :], 1 / K_ONE, hi, ALU.mult,
                                         ALU.subtract).then_inc(max_rows_set, 1)

            def head(h, e, exists):
                ok = lambda d: there(exists, h, d)
                for t in range(NT):
                    d = 1 + (t + A_AHEAD) // NT
                    ta = (t + A_AHEAD) % NT
                    if ok(d):
                        for c in range(CH):
                            dve.wait_ge(a_done, ((h + d) * NT + ta) * CH + c + 1)
                            dve.tensor_reduce(maxima[:, (e + d) % 2, ta, c:c + 1], a_bank[(CH * ta + c) % NSB][:, :], AX.X,
                                              ALU.max).then_inc(a_read, 1)
                        if ta == NT - 1:
                            maximum(h + d, (e + d) % 4)
                    read_turned(dve, "dve", h, e, t, ok)
                    if t == PV_LAG - 1 and ok(-1):
                        dve.wait_ge(pv_done, h * NT)
                        dve.tensor_copy(o_t[:, :], pv_bank[:, 0:QW]).then_inc(o_copied, 1)
                    if t == READ["o"] and ok(-1):
                        dve.wait_ge(o_turned, h)
                        o = t_bank[:, 0:QW].rearrange("p (i j w) -> p i j w", i=2, w=VW)
                        dve.reciprocal(inv_sum[:, :, :], o[:, :, :, HD]).then_inc(inv_done, 1)
                        dve.wait_ge(inv_done, h)
                        dst = heads_out[:, :, bass.ds(h - 1, 1), :]
                        dve.tensor_tensor(dst.rearrange("p (j i) o d -> p (i o) j d", i=2),
                                          o[:, :, :, 0:HD],
                                          inv_sum[:, :, :].unsqueeze(3).broadcast_to([P, 2, CG4, HD]),
                                          ALU.mult).then_inc(o_out, 1)
            over_heads(dve, head)


def band_matrices(size):
    dec_lo = np.array([
        -0.00011747678400228192, 0.0006754494059985568, -0.0003917403729959771, -0.00487035299301066,
        0.008746094047015655, 0.013981027917015516, -0.04408825393106472, -0.01736930100202211,
        0.128747426620186, 0.00047248457399797254, -0.2840155429624281, -0.015829105256023893,
        0.5853546836548691, 0.6756307362980128, 0.3128715909144659, 0.05441584224308161], dtype=np.float64)
    taps = len(dec_lo)
    both = (dec_lo[::-1], dec_lo * (-1.0) ** np.arange(taps))
    m = np.zeros((2, size // 2, size + taps - 2))
    for band in range(2):
        for i in range(size // 2):
            m[band, i, 2 * i:2 * i + taps] = both[band]
    half = taps // 2
    return m[:, :, half - 1:-(half - 1)].astype(np.float32)


LEVELS = 3
TL = [16, 8, 4]
DL = [128, 64, 32]
DB = [8, 16, 32]
NB = [16, 4, 1]
DELTAS = range(-1, 5)


def wavelet_constants():
    def block(tm, dm, t_in, d_in, t_out, d_out, rev_in, rev_out):
        m = np.einsum("tT,dD->tdTD", tm, dm[d_in][:, d_out])
        m = m.reshape(P, P)
        if rev_in:
            m = m[::-1]
        if rev_out:
            m = m[:, ::-1]
        return np.ascontiguousarray(m)
    w = {n: band_matrices(n) for n in (8, 16, 32, 64, 128, 256)}
    bands = [(bt, bd) for bt in range(2) for bd in range(2)]
    out = {}
    eye4 = np.eye(4, dtype=np.float32)
    out["t_op"] = np.einsum("bih,wv->hwbiv", w[32], eye4).reshape(P, P)
    out["t_inv"] = np.einsum("bih,wv->biwhv", w[32][:, ::-1], eye4).reshape(P, P)
    out["d_op"] = w[256].transpose(2, 0, 1).reshape(CT, P, 2, P).transpose(1, 0, 2, 3).reshape(P, -1)
    rev = w[256].reshape(2, NB[0], DB[0], C)[:, :, ::-1].reshape(2, P, C)
    out["d_inv"] = rev.transpose(2, 0, 1).reshape(CT, P, 2, P).transpose(1, 0, 2, 3).reshape(P, -1)
    sl = lambda k, n: slice(k * n, (k + 1) * n)
    out["dwt1"] = np.concatenate([
        block(w[16][bt].T, w[128][bd].T, None, sl(4 + e, 8), None, sl(1, 16), True, False)
        for bt, bd in bands for e in DELTAS], 1)
    out["dwt2"] = np.concatenate([
        block(w[8][bt].T, w[64][bd].T, None, sl(k, 16), None, sl(0, 32), True, False)
        for bt, bd in bands for k in range(4)], 1)
    out["inv2"] = np.concatenate([
        block(w[8][bt], w[64][bd], None, sl(0, 32), None, sl(k, 16), True, True)
        for bt, bd in bands for k in range(4)], 1)
    out["inv1"] = np.concatenate([
        block(w[16][bt], w[128][bd], None, sl(1, 16), None, sl(4 + e, 8), True, True)
        for bt, bd in bands for e in DELTAS], 1)
    return {k: np.ascontiguousarray(v, dtype=np.float32) for k, v in out.items()}


KS = 11
KROWS, KCOLS = 31, 64
KY0, KX0 = 10, 26


def analysis_phase(nc, x, heads_out, wp, mean_op, ident, t_op, d_op, kernels, biases,
                   conv_ops, conv_bias, ktab_s, x1_s, bands_s):
    with ExitStack() as ctx:
        sb = lambda name, shape, dt=F32: ctx.enter_context(nc.sbuf_tensor(name, shape, dt))
        sem = lambda name: ctx.enter_context(nc.semaphore(name))
        pb = lambda name, shape, dt=F32: ctx.enter_context(nc.psum_tensor(name, shape, dt))

        bands = sb("bands", [P, 2, 2 * TL[0], C])
        o_in = [sb(f"o_in{e}", [P, NT, C]) for e in range(2)]
        x1 = [sb(f"x1_{e}", [P, NT, C]) for e in range(2)]
        xc = sb("xc", [P, NT, C])
        xn = sb("xn", [P, NT, C])
        o_t = sb("o_turned_sb", [P, CT, NT, P])
        rows = sb("rows", [P, CT, NT, P])
        wp_w = sb("wp_w", [P, CT, C])
        t_w = sb("t_w", [P, P])
        d_w = sb("d_w", [P, CT, 2, P])
        mean_w = sb("mean_w2", [P, P])
        id32 = sb("id32b", [P, P])
        group_part = sb("group_part2", [P, 2, G])
        spread = sb("spread2", [P, G])
        spread_inv = sb("spread_inv2", [P, G])
        eps = sb("eps2", [P, 1])
        ktab6 = sb("ktab6", [KS, 6, KS])
        kmean = sb("kmean", [KS, KS])
        ktab = sb("ktab", [KROWS, KCOLS])
        bias6 = sb("bias6", [P, 6])

        turned = [pb(f"turned2{i}", [P, BANK]) for i in range(2)]
        proj = [pb(f"proj{i}", [P, BANK]) for i in range(2)]
        cols = [pb(f"cols{i}", [P, BANK]) for i in range(2)]
        stat = pb("stat2", [P, BANK])

        consts_in = sem("f_consts_in")
        heads_in = [sem(f"heads_in{e}") for e in range(2)]
        x_in = [sem(f"x_in2{e}") for e in range(2)]
        eps_set = sem("eps_set")
        o_turned = sem("o_turned2")
        o_sb = sem("o_sb")
        proj_done = sem("proj_done")
        x1_done = sem("x1_done")
        x1_stored = [sem(f"x1_stored{e}") for e in range(2)]
        part_ready = sem("part_ready2")
        stat_ready = sem("stat_ready2")
        centred = sem("centred2")
        squared = sem("squared2")
        spread_ready = sem("spread_ready2")
        inv_ready = sem("inv_ready2")
        normed = sem("normed2")
        rows_done = sem("rows_done")
        rows_sb = sem("rows_sb")
        cols_done = sem("cols_done")
        cols_sb = sem("cols_sb")
        bands_stored = sem("bands_stored")
        k_zero = sem("k_zero")
        k_in = sem("k_in")
        k_step = sem("k_step")
        k_out = sem("k_out")
        ops_in = sem("ops_in")
        b_step = sem("b_step")

        block = ctx.enter_context(nc.Block())

        def over_images(engine, first, step, last):
            first()
            step(0, 0, 1)
            step(1, 1, 0)
            with engine.Fori(1, B // 2 - 1) as i:
                step(2 * i, 0, 1)
                step(2 * i + 1, 1, 0)
            step(B - 2, 0, 1)
            last()

        @block.sync
        def _(sp):
            for dst, src in ((wp_w[:, :, :], wp.rearrange("(k p) o -> p k o", p=P)), (id32[:, :], ident),
                             (mean_w[:, :], mean_op), (t_w[:, :], t_op),
                             (d_w[:, :, :, :].rearrange("p a b c -> p (a b c)"), d_op)):
                sp.dma_start(dst, src).then_inc(consts_in, 16)

            def front(b, e):
                wait(sp, part_ready, 2 * (b - 1))
                sp.dma_start(o_in[e][:, :, :].rearrange("p t (h d) -> p t h d", d=HD),
                             heads_out[:, :, bass.ds(b * NH, NH), :]).then_inc(heads_in[e], 16)
                wait(sp, centred, b - 1)
                wait(sp, x1_stored[e], 16 * ((b - e) // 2))
                sp.dma_start(x1[e][:, :, :], x[bass.ds(b * N, N), :].rearrange("(p t) c -> p t c", t=NT)
                             ).then_inc(x_in[e], 16)

            def store(b, e):
                sp.wait_ge(x1_done, 4 * b + 4)
                sp.dma_start(x1_s[bass.ds(b * N, N), :].rearrange("(p t) c -> p t c", t=NT),
                             x1[e][:, :, :]).then_inc(x1_stored[e], 16)

            def step(b, e, f):
                front(b + 1, f)
                store(b, e)
            def store_bands(half):
                sp.wait_ge(cols_sb, 4 * B // 2 * (half + 1))
                images = slice(half * C // 2, (half + 1) * C // 2)
                for bt, bd in ((1, 1), (0, 0), (0, 1), (1, 0)):
                    sp.dma_start(bands_s[2 * bt + bd].rearrange("i d m -> d i m")[:, :, images],
                                 bands[:, bd, bt * TL[0]:(bt + 1) * TL[0], images]).then_inc(bands_stored, 16)

            def last():
                store_bands(0)
                store(B - 1, 1)
                store_bands(1)
            over_images(sp, lambda: front(0, 0), step, last)
            sp.wait_ge(bands_stored, 2 * 64)
            for e in range(2):
                sp.wait_ge(x1_stored[e], 16 * B // 2)

        @block.gpsimd
        def _(pool):
            pool.memset(eps[:, :], EPS).then_inc(eps_set, 1)
            pool.memset(ktab6[:, :, :], 0.0).then_inc(k_zero, 1)
            pool.memset(ktab[:, :], 0.0).then_inc(k_zero, 1)
            pool.wait_ge(k_zero, 2)
            pool.dma_start(ktab_s.rearrange("o (y x) -> (o y) x", x=KCOLS), ktab[:, :]).then_inc(k_out, 16)
            for n, (kern, bias) in enumerate(zip(kernels, biases)):
                r = KS // 2
                pool.dma_start(ktab6[r - n:r + n + 1, n, r - n:r + n + 1], kern.rearrange("o y x -> (o y) x")).then_inc(k_in, 16)
                pool.dma_start(bias6[:, n:n + 1], bias.unsqueeze(0).broadcast_to([P, 1])).then_inc(k_in, 16)
            pool.wait_ge(k_in, 16 * 12)
            for n in range(1, 6):
                pool.tensor_tensor(ktab6[:, 0], ktab6[:, 0], ktab6[:, n], ALU.add).then_inc(k_step, 1)
                pool.tensor_tensor(bias6[:, 0:1], bias6[:, 0:1], bias6[:, n:n + 1], ALU.add).then_inc(b_step, 1)
                pool.wait_ge(k_step, n)
                pool.wait_ge(b_step, n)
            pool.tensor_scalar(kmean[:, :], ktab6[:, 0], 1 / 6, None, ALU.mult).then_inc(k_step, 1)
            pool.tensor_scalar(conv_bias[:, :], bias6[:, 0:1], 1 / 6, None, ALU.mult).then_inc(b_step, 1)
            pool.wait_ge(k_step, 6)
            pool.wait_ge(b_step, 6)
            pool.wait_ge(k_out, 16)
            pool.dma_start(ktab_s.rearrange("o (y x) -> (o y) x", x=KCOLS)[KY0:KY0 + KS, KX0:KX0 + KS],
                           kmean[:, :]).then_inc(k_out, 16)
            pool.wait_ge(k_out, 32)
            n = 0
            for level in range(LEVELS):
                t, nd = TL[level], DB[level]
                for k, op in enumerate(conv_ops[level]):
                    delta = k - len(conv_ops[level]) // 2
                    for i in range(t):
                        at = (i + KY0 + 6 - t) * KCOLS + KX0 + KS // 2 - (nd - 1) + nd * delta
                        src = bass.AP(tensor=ktab_s.tensor, offset=at, ap=[[1, nd], [KCOLS, t], [1, nd]])
                        pool.dma_start(op[i * nd:(i + 1) * nd, :].rearrange("p (i d) -> p i d", d=nd),
                                       src).then_inc(ops_in, 16)
                        n += 1
            pool.wait_ge(ops_in, 16 * n)

        @block.tensor
        def _(pe):
            pe.wait_ge(consts_in, 5 * 16)

            def project(b, e):
                pe.wait_ge(heads_in[e], 16 * ((b - e) // 2 + 1))
                for n in range(4):
                    half, kt = n // 2, n % 2
                    if n == 0:
                        wait(pe, rows_sb, 4 * (b - 1))
                    wait(pe, o_sb, bank_free(b, n))
                    for t in range(4):
                        m = pe.transpose(turned[n % 2][:, t * P:(t + 1) * P],
                                         o_in[e][:, 4 * half + t, kt * P:(kt + 1) * P], id32[:, :])
                    m.then_inc(o_turned, 1)
                for n in range(4):
                    pe.wait_ge(o_sb, 4 * b + (2 if n < 2 else 4))
                    wait(pe, x1_done, bank_free(b, n))
                    for t in range(2):
                        for kt in range(CT):
                            m = pe.matmul(proj[n % 2][:, t * C:(t + 1) * C], o_t[:, kt, 2 * n + t, :],
                                          wp_w[:, kt, :], start=(kt == 0), stop=(kt == CT - 1))
                    m.then_inc(proj_done, 1)

            def stats(b, k):
                pe.wait_ge(part_ready, 2 * b + k + 1)
                if k == 0:
                    wait(pe, spread_ready, b)
                pe.matmul(stat[:, k * G:(k + 1) * G], mean_w[:, :], group_part[:, k],
                          start=True, stop=True).then_inc(stat_ready, 1)

            def over_rows(b, projected):
                pe.wait_ge(normed, b + 1)
                for n in range(4):
                    ch, half = n // 2, n % 2
                    if n == 0:
                        pe.wait_ge(o_sb, 4 * projected)
                    wait(pe, rows_sb, bank_free(b, n))
                    for t in range(4):
                        m = pe.matmul(turned[n % 2][:, t * P:(t + 1) * P],
                                      xn[:, 4 * half + t, ch * P:(ch + 1) * P], t_w[:, :],
                                      start=True, stop=True)
                    m.then_inc(rows_done, 1)

            def over_columns(b):
                for n in range(4):
                    bd, half = n // 2, n % 2
                    pe.wait_ge(rows_sb, 4 * b + 4)
                    wait(pe, cols_sb, bank_free(b, n))
                    for ch in range(CT):
                        m = pe.matmul(cols[n % 2][:, :], d_w[:, ch, bd, :],
                                      rows[:, ch, 4 * half:4 * half + 4, :].rearrange("p t n -> p (t n)"),
                                      start=(ch == 0), stop=(ch == CT - 1))
                    m.then_inc(cols_done, 1)

            def first():
                project(0, 0)
                stats(0, 0)
                stats(0, 1)

            def step(b, e, f):
                project(b + 1, f)
                over_rows(b, b + 2)
                stats(b + 1, 0)
                over_columns(b)
                stats(b + 1, 1)

            def last():
                over_rows(B - 1, B)
                over_columns(B - 1)
            over_images(pe, first, step, last)

        @block.scalar
        def _(act):
            act.wait_ge(eps_set, 1)

            def project(b):
                for n in range(4):
                    half, kt = n // 2, n % 2
                    act.wait_ge(o_turned, 4 * b + n + 1)
                    if n == 0:
                        wait(act, proj_done, 4 * b)
                    act.activation(o_t[:, kt, 4 * half:4 * half + 4, :].rearrange("p t n -> p (t n)"),
                                   turned[n % 2][:, :], ACT.Copy).then_inc(o_sb, 1)

            def square(b, e):
                act.wait_ge(centred, b + 1)
                act.wait_ge(o_turned, 4 * b + 4)
                act.activation(o_in[e][:, :, :], xc[:, :, :], ACT.Square).then_inc(squared, 1)

            def spread_of(b):
                act.wait_ge(stat_ready, 2 * b + 2)
                act.activation(spread[:, :], stat[:, G:2 * G], ACT.Sqrt, bias=eps[:, 0:1]).then_inc(spread_ready, 1)

            def over_rows(b):
                for n in range(4):
                    ch, half = n // 2, n % 2
                    act.wait_ge(rows_done, 4 * b + n + 1)
                    if n == 0:
                        wait(act, cols_done, 4 * b)
                    act.activation(rows[:, ch, 4 * half:4 * half + 4, :].rearrange("p t n -> p (t n)"),
                                   turned[n % 2][:, :], ACT.Copy).then_inc(rows_sb, 1)

            def over_columns(b, which):
                for n in which:
                    bd, half = n // 2, n % 2
                    act.wait_ge(cols_done, 4 * b + n + 1)
                    dst = bands[:, bd, :, bass.ds(b * W, W)].rearrange("p r (w t) -> p t r w", t=NT)
                    act.activation(dst[:, 4 * half:4 * half + 4],
                                   cols[n % 2][:, :].rearrange("p (t r w) -> p t r w", t=4, w=4),
                                   ACT.Copy).then_inc(cols_sb, 1)

            def first():
                project(0)
                square(0, 0)
                spread_of(0)

            def step(b, e, f):
                project(b + 1)
                over_rows(b)
                over_columns(b, (0,))
                square(b + 1, f)
                over_columns(b, (1, 2, 3))
                spread_of(b + 1)

            def last():
                over_rows(B - 1)
                over_columns(B - 1, range(4))
            over_images(act, first, step, last)

        @block.vector
        def _(dve):
            over = lambda s: s.unsqueeze(1).unsqueeze(3).broadcast_to([P, NT, G, CG])
            tiled = lambda s: s[:, :, :].rearrange("p t (g c) -> p t g c", g=G)

            def group_sum(src, k):
                dve.tensor_reduce(group_part[:, k], src.rearrange("p t (g c) -> p g t c", g=G),
                                  AX.XY, ALU.add).then_inc(part_ready, 1)

            def add(b, e):
                dve.wait_ge(x_in[e], 16 * ((b - e) // 2 + 1))
                for n in range(4):
                    dve.wait_ge(proj_done, 4 * b + n + 1)
                    part = x1[e][:, 2 * n:2 * n + 2, :].rearrange("p t c -> p (t c)")
                    dve.tensor_tensor(part, proj[n % 2][:, :], part, ALU.add).then_inc(x1_done, 1)

            def centre(b, e):
                dve.wait_ge(x1_done, 4 * b + 4)
                group_sum(x1[e][:, :, :], 0)
                dve.wait_ge(stat_ready, 2 * b + 1)
                wait(dve, normed, b)
                dve.tensor_tensor(tiled(xc), tiled(x1[e]), over(stat[:, 0:G]), ALU.subtract).then_inc(centred, 1)
                dve.wait_ge(squared, b + 1)
                group_sum(o_in[e][:, :, :], 1)

            def scale(b):
                dve.wait_ge(spread_ready, b + 1)
                dve.reciprocal(spread_inv[:, :], spread[:, :]).then_inc(inv_ready, 1)
                dve.wait_ge(inv_ready, b + 1)
                wait(dve, rows_done, 4 * b)
                dve.tensor_tensor(tiled(xn), tiled(xc), over(spread_inv[:, :]), ALU.mult).then_inc(normed, 1)

            def image(b, e):
                add(b, e)
                centre(b, e)
                scale(b)
            over_images(dve, lambda: image(0, 0), lambda b, e, f: image(b + 1, f), lambda: None)


def bands_phase(nc, bands_s, conv_ops, conv_bias, ident, dwt1, dwt2, inv2, inv1, level0, z_in, synth_s):
    LL, LH, HL, HH = range(4)
    HIGH = (HH, LH, HL)
    IM = C
    HALF = IM // P
    ROUNDS = [d // 16 for d in DL]
    NMM, NST = 4, 4
    THR = -float(np.sqrt(2.0 * np.log(32.0)) / 0.6745)

    with ExitStack() as ctx:
        sb = lambda name, shape, dt=F32: ctx.enter_context(nc.sbuf_tensor(name, shape, dt))
        sem = lambda name: ctx.enter_context(nc.semaphore(name))
        pb = lambda name, shape, dt=F32: ctx.enter_context(nc.psum_tensor(name, shape, dt))

        raw = [None] + [sb(f"raw_l{v}", [P, 4, NB[v], IM]) for v in (1, 2)]
        raw0 = lambda band: level0[:, band % 2, band // 2]
        band_of = lambda v, band: raw[v][:, band] if v else raw0(band)
        ll0 = sb("ll0", [P, NB[0], IM])
        done = [None, sb("done_l1", [P, 4, NB[1], IM]), sb("done_l2", [P, 4, NB[2], IM])]
        ll1 = sb("ll1", [P, NB[1], IM])
        keys = [sb(f"keys_l{v}", [P, HALF, TL[v] * DL[v]]) for v in range(LEVELS)]
        eight = sb("eight", [P, HALF * TL[0], 8])
        thr_rows = [sb(f"thr_rows{v}", [P, HALF, P]) for v in range(LEVELS)]
        thr_sb = sb("thr_sb", [P, IM])
        clipped = sb("clipped", [P, 2, 4, IM])
        stage = sb("stage", [P, NST, 2, IM])
        id32 = sb("id32c", [P, P])
        w_dwt1 = sb("w_dwt1", [P, 4, len(DELTAS), P])
        w_dwt2 = sb("w_dwt2", [P, 4, NB[1], P])
        w_inv2 = sb("w_inv2", [P, 4, NB[1], P])
        w_inv1 = w_dwt1

        mm = [pb(f"mm{i}", [P, 2, IM]) for i in range(NMM)]
        kbank = [pb(f"kbank{i}", [P, BANK]) for i in range(2)]
        thr = pb("thr", [P, BANK])

        raw_in = [sem(f"raw_in{b}") for b in range(4)]
        w_in = {n: sem("in_" + n) for n in ("id", "dwt1", "dwt2", "inv2", "inv1")}
        key_done = sem("key_done")
        key_read = sem("key_read")
        keys_set = sem("keys_set")
        med = sem("med")
        thr_rows_set = sem("thr_rows_set")
        thr_done = sem("thr_done")
        thr_copied = sem("thr_copied")
        low_cut = sem("low_cut")
        clip_done = sem("clip_done")
        soft_done = sem("soft_done")
        mm_done = sem("mm_done")
        mm_read = sem("mm_read")
        stored = [sem(f"synth_stored{i}") for i in range(NST)]

        plan = [("conv", 0, LL, q) for q in range(8)]
        plan += [("dwt", 1, b, q) for b in (HH, LL, LH, HL) for q in range(2)]
        plan += [("conv", 1, LL, q) for q in range(2)]
        plan += [("dwt", 2, 2 * q, q) for q in range(2)]
        plan += [("conv", 0, b, q) for b in HIGH for q in range(8)]
        plan += [("conv", 1, b, q) for b in HIGH for q in range(2)]
        plan += [("conv", 2, 2 * q, q) for q in range(2)]
        plan += [("inv", 1, LL, q) for q in range(2)]
        plan += [("inv", 0, LL, q) for q in range(8)]
        number = {p: n for n, p in enumerate(plan)}
        staged = [n for n, p in enumerate(plan) if p[1] == 0 and (p[0] == "inv" or p[2] != LL)]
        stage_no = {n: s for s, n in enumerate(staged)}
        cuts = [(0, b, k, 4) for b in HIGH for k in range(0, 16, 4)]
        cuts += [(1, b, 0, 4) for b in HIGH] + [(2, LH, 0, 3)]
        cut_no = {c: n for n, c in enumerate(cuts)}
        key_banks = [8, 2, 1]
        keys_before = [0, 8, 10]

        def key_part(v, j):
            if v == 2:
                return keys[v][:, :, :]
            h, g = j // (key_banks[v] // HALF), j % (key_banks[v] // HALF)
            return keys[v][:, h].rearrange("p (i k d) -> p k i d", i=TL[v], d=DB[v])[:, 4 * g:4 * g + 4]

        block = ctx.enter_context(nc.Block())

        @block.sync
        def _(sp):
            def load_band(b):
                for i in range(TL[0]):
                    sp.dma_start(raw0(b)[i * DB[0]:(i + 1) * DB[0]],
                                 bands_s[b, i].rearrange("(k d) m -> d k m", d=DB[0])).then_inc(raw_in[b], 16)
            sp.dma_start(id32[:, :], ident).then_inc(w_in["id"], 16)
            load_band(HH)
            load_band(LL)
            for n, (t, src) in (("dwt1", (w_dwt1, dwt1)), ("dwt2", (w_dwt2, dwt2))):
                sp.dma_start(t[:, :, :, :].rearrange("p a b c -> p (a b c)"), src).then_inc(w_in[n], 16)
            load_band(LH)
            load_band(HL)
            for n, (t, src) in (("inv2", (w_inv2, inv2)), ("inv1", (w_inv1, inv1))):
                if n == "inv1":
                    sp.wait_ge(mm_read, number[("dwt", 1, HL, 1)] + 1)
                sp.dma_start(t[:, :, :, :].rearrange("p a b c -> p (a b c)"), src).then_inc(w_in[n], 16)
            def load_z(band, k):
                sp.dma_start(raw0(band)[k * DB[0]:(k + 1) * DB[0]],
                             synth_s[band, :, k, :].rearrange("(i d) m -> d i m", d=DB[0])).then_inc(z_in, 16)

            def load_pair(s):
                q = plan[staged[s]][3]
                sp.wait_ge(stored[s % NST], 16 * (s // NST + 1))
                load_z(LL, 2 * q)
                load_z(LL, 2 * q + 1)

            for s, n in enumerate(staged):
                _, _, band, q = plan[n]
                sp.wait_ge(mm_read, n + 1)
                sp.dma_start(synth_s[band, :, 2 * q:2 * q + 2, :], stage[:, s % NST]).then_inc(stored[s % NST], 16)
                if band == LL:
                    if q:
                        load_pair(s - 1)
                elif q == 7:
                    for slot in stored:
                        sp.wait_ge(slot, 16 * 2 * (s // 8 + 1))
                    for k in range(NB[0]):
                        load_z(band, k)
            load_pair(len(staged) - 1)
            sp.wait_ge(z_in, 16 * 4 * NB[0])

        @block.tensor
        def _(pe):
            def turn_keys(v):
                src = band_of(v, HH)
                n = keys_before[v]
                jobs = {0: [(h, range(4 * g, 4 * g + 4)) for h in range(HALF) for g in range(4)],
                        1: [(h, range(4)) for h in range(HALF)], 2: [(None, None)]}[v]
                if v == 0:
                    pe.wait_ge(raw_in[HH], 16 * TL[0])
                    pe.wait_ge(w_in["id"], 16)
                else:
                    pe.wait_ge(mm_read, number[("dwt", v, HH if v == 1 else HL, 1)] + 1)
                for h, blocks in jobs:
                    wait(pe, key_read, n - 1)
                    if v == 2:
                        pieces = [(src[:, 0, hh * P:(hh + 1) * P]) for hh in range(HALF)]
                    else:
                        pieces = [src[:, k, h * P:(h + 1) * P] for k in blocks]
                    for j, piece in enumerate(pieces):
                        m = pe.transpose(kbank[n % 2][:, j * P:(j + 1) * P], piece, id32[:, :])
                    m.then_inc(key_done, 1)
                    n += 1

            def spread_thr(v):
                pe.wait_ge(thr_rows_set, v + 1)
                wait(pe, thr_copied, v)
                for h in range(HALF):
                    m = pe.matmul(thr[:, h * P:(h + 1) * P], thr_rows[v][:, h, :], id32[:, :], start=True, stop=True)
                m.then_inc(thr_done, 1)

            def conv(v, band, q, bank):
                if v == 2:
                    pe.wait_ge(soft_done, len(cuts))
                    return pe.matmul(bank[:, :, :], conv_ops[2][0][:, :], raw[2][:, band:band + 2, 0, :],
                                     start=True, stop=True)
                if band == LL:
                    if v == 0:
                        pe.wait_ge(raw_in[LL], 16 * TL[0])
                    else:
                        pe.wait_ge(mm_read, number[("dwt", 1, LL, 1)] + 1)
                else:
                    k = min((2 * q + 2) // 4 * 4, NB[v] - 4)
                    pe.wait_ge(soft_done, cut_no[(v, band, k, 4)] + 1)
                src = band_of(v, band)
                m = pe.matmul(bank[:, :, :], conv_ops[v][1][:, :], src[:, 2 * q:2 * q + 2, :], start=True, stop=False)
                lo, hi = (1 if q == 0 else 0), (1 if 2 * q + 2 == NB[v] else 2)
                m = pe.matmul(bank[:, lo:2, :], conv_ops[v][0][:, :], src[:, 2 * q - 1 + lo:2 * q + 1, :],
                              start=False, stop=False)
                return pe.matmul(bank[:, 0:hi, :], conv_ops[v][2][:, :], src[:, 2 * q + 1:2 * q + 1 + hi, :],
                                 start=False, stop=True)

            def dwt(v, band, q, bank):
                if v == 2:
                    pe.wait_ge(w_in["dwt2"], 16)
                    pe.wait_ge(mm_read, number[("conv", 1, LL, 1)] + 1)
                    for b in range(2):
                        for k in range(NB[1]):
                            m = pe.matmul(bank[:, b, :], w_dwt2[:, band + b, k, :], done[1][:, LL, k, :],
                                          start=(k == 0), stop=(k == NB[1] - 1))
                    return m
                pe.wait_ge(w_in["dwt1"], 16)
                pe.wait_ge(mm_read, number[("conv", 0, LL, 7)] + 1)
                terms = [(0, 0), (1, 0), (2, 0), (3, 0), (-1, 0), (4, 0)]
                for n, (delta, _) in enumerate(terms):
                    js = [j for j in range(2) if 0 <= 4 * (2 * q + j) + delta < NB[0]]
                    a, z = js[0], js[-1] + 1
                    first = 4 * (2 * q + a) + delta
                    m = pe.matmul(bank[:, a:z, :], w_dwt1[:, band, delta + 1, :],
                                  ll0[:, first:first + 4 * (z - a - 1) + 1:4, :], start=(n == 0), stop=(n == 5))
                return m

            def inv(v, q, bank):
                if v == 1:
                    pe.wait_ge(w_in["inv2"], 16)
                    pe.wait_ge(mm_read, number[("conv", 2, HL, 1)] + 1)
                    for j in range(2):
                        for b in range(4):
                            m = pe.matmul(bank[:, j, :], w_inv2[:, b, 2 * q + j, :], done[2][:, b, 0, :],
                                          start=(b == 0), stop=(b == 3))
                    return m
                pe.wait_ge(w_in["inv1"], 16)
                pe.wait_ge(mm_read, number[("inv", 1, LL, 1)] + 1)
                for j in range(2):
                    terms = [(b, k) for b in range(4) for k in range(NB[1]) if -1 <= 2 * q + j - 4 * k <= 4]
                    for n, (b, k) in enumerate(terms):
                        src = ll1[:, k, :] if b == LL else done[1][:, b, k, :]
                        m = pe.matmul(bank[:, j, :], w_inv1[:, b, 2 * q + j - 4 * k + 1, :], src,
                                      start=(n == 0), stop=(n == len(terms) - 1))
                return m

            turn_keys(0)
            for n, (what, v, band, q) in enumerate(plan):
                if n == number[("conv", 0, HH, 0)]:
                    turn_keys(1)
                    turn_keys(2)
                    spread_thr(0)
                if n == number[("conv", 1, HH, 0)]:
                    spread_thr(1)
                if n == number[("conv", 2, LL, 0)]:
                    spread_thr(2)
                wait(pe, mm_read, n - NMM + 1)
                bank = mm[n % NMM]
                if what == "conv":
                    m = conv(v, band, q, bank)
                elif what == "dwt":
                    m = dwt(v, band, q, bank)
                else:
                    m = inv(v, q, bank)
                m.then_inc(mm_done, 1)

        @block.scalar
        def _(act):
            def magnitudes(v):
                t, d, nd = TL[v], DL[v], DB[v]
                for j in range(key_banks[v]):
                    n = keys_before[v] + j
                    act.wait_ge(key_done, n + 1)
                    if v == 2:
                        src = kbank[n % 2][:, 0:HALF * P].rearrange("p (h n) -> p h n", h=HALF)
                    else:
                        src = kbank[n % 2][:, :].rearrange("p (k i d) -> p k i d", k=4, d=nd)
                    dst = key_part(v, j)
                    act.activation(dst, src, ACT.Abs).then_inc(key_read, 1)

            magnitudes(0)
            for n, (what, v, band, q) in enumerate(plan):
                if n == number[("conv", 0, HH, 0)]:
                    magnitudes(1)
                    magnitudes(2)
                act.wait_ge(mm_done, n + 1)
                if n in stage_no:
                    s = stage_no[n]
                    wait(act, stored[s % NST], 16 * (s // NST))
                    dst = stage[:, s % NST]
                elif what == "dwt":
                    dst = raw[v][:, band, 2 * q:2 * q + 2, :] if v == 1 else raw[2][:, band:band + 2, 0, :]
                elif what == "inv":
                    dst = ll1[:, 2 * q:2 * q + 2, :]
                elif v == 0:
                    dst = ll0[:, 2 * q:2 * q + 2, :]
                else:
                    dst = done[1][:, band, 2 * q:2 * q + 2, :] if v == 1 else done[2][:, band:band + 2, 0, :]
                if what == "conv":
                    act.activation(dst, mm[n % NMM][:, :, :], ACT.Identity, bias=conv_bias[:, 0:1]).then_inc(mm_read, 1)
                else:
                    act.activation(dst, mm[n % NMM][:, :, :], ACT.Copy).then_inc(mm_read, 1)

        @block.vector
        def _(dve):
            steps = [0]

            def medians(v):
                t, d, nd = TL[v], DL[v], DB[v]
                for j in range(key_banks[v]):
                    part = key_part(v, j)
                    dve.wait_ge(key_read, keys_before[v] + j + 1)
                    dve.tensor_scalar(part, part, -1.0, None, ALU.mult).then_inc(keys_set, 1)
                dve.wait_ge(keys_set, keys_before[v] + key_banks[v])
                for r in range(ROUNDS[v]):
                    begin = steps[0]
                    for row in range(HALF * t):
                        part = keys[v][:, row // t, row % t * d:(row % t + 1) * d]
                        if r:
                            dve.wait_ge(med, begin - HALF * t + row + 1)
                        dve.max(eight[:, row, :], part).then_inc(med, 1)
                    steps[0] += HALF * t
                    if r == ROUNDS[v] - 1:
                        break
                    for row in range(HALF * t):
                        part = keys[v][:, row // t, row % t * d:(row % t + 1) * d]
                        dve.wait_ge(med, steps[0] - HALF * t + row + 1)
                        dve.match_replace(part, eight[:, row, :], part, -3.0e38).then_inc(med, 1)
                    steps[0] += HALF * t
                dve.wait_ge(med, steps[0])
                dve.tensor_scalar(thr_rows[v][:, :, :].rearrange("p h (i d) -> p (h i) d", d=nd),
                                  eight[:, 0:HALF * t, 7:8].broadcast_to([P, HALF * t, nd]),
                                  THR, None, ALU.mult).then_inc(thr_rows_set, 1)

            def clip(n, v, band, k, blocks):
                part = band_of(v, band)[:, k:k + blocks, :] if v < 2 else raw[2][:, LH:HH + 1, 0, :]
                dst = clipped[:, n % 2, 0:blocks, :]
                bound = thr_sb[:, :].unsqueeze(1).broadcast_to([P, blocks, IM])
                wait(dve, soft_done, n - 1)
                if v == 0:
                    dve.wait_ge(raw_in[band], 16 * TL[0])
                dve.tensor_tensor(dst, part, bound, ALU.min).then_inc(low_cut, 1)
                dve.wait_ge(low_cut, n + 1)
                dve.scalar_tensor_tensor(dst, bound, -1.0, dst, ALU.mult, ALU.max).then_inc(clip_done, 1)

            def take_thr(v):
                dve.wait_ge(thr_done, v + 1)
                wait(dve, clip_done, sum(c[0] < v for c in cuts))
                dve.tensor_copy(thr_sb[:, :], thr[:, 0:IM]).then_inc(thr_copied, 1)
                dve.wait_ge(thr_copied, v + 1)

            medians(0)
            take_thr(0)
            for n, cut in enumerate(cuts):
                if cut == (0, HIGH[2], 0, 4):
                    medians(1)
                    medians(2)
                if cut[0] and cut[0] != cuts[n - 1][0]:
                    take_thr(cut[0])
                clip(n, *cut)

        @block.gpsimd
        def _(pool):
            for n, (v, band, k, blocks) in enumerate(cuts):
                part = band_of(v, band)[:, k:k + blocks, :] if v < 2 else raw[2][:, LH:HH + 1, 0, :]
                pool.wait_ge(clip_done, n + 1)
                pool.tensor_tensor(part, part, clipped[:, n % 2, 0:blocks, :], ALU.subtract).then_inc(soft_done, 1)


def synthesis_phase(nc, z, x1_s, out_w, out_b, d_inv, t_inv, out):
    with ExitStack() as ctx:
        sb = lambda name, shape, dt=F32: ctx.enter_context(nc.sbuf_tensor(name, shape, dt))
        sem = lambda name: ctx.enter_context(nc.semaphore(name))
        pb = lambda name, shape, dt=F32: ctx.enter_context(nc.psum_tensor(name, shape, dt))
        R = 2 * TL[0]

        z = z[:, :, :, :, :].rearrange("p d b r m -> p d (b r) m")
        zc = [sb(f"zc{e}", [P, 2, NT, R, 4]) for e in range(2)]
        x1 = [sb(f"x1s_{e}", [P, NT, C]) for e in range(2)]
        res = [sb(f"res{e}", [P, NT, C]) for e in range(2)]
        v_sb = [sb(f"v_sb{e}", [P, BANK]) for e in range(2)]
        w_out = sb("w_out", [P, CT, C])
        w_dinv = sb("w_dinv", [P, CT, 2, P])
        wd = sb("wd", [P, 2, C])
        w_tinv = sb("w_tinv", [P, P])
        b_out = sb("b_out", [P, C])

        vbank = [pb(f"vbank{i}", [P, BANK]) for i in range(2)]
        fbank = [pb(f"fbank{i}", [P, BANK]) for i in range(2)]
        wbank = pb("wbank", [P, BANK])

        consts_in = sem("s_consts_in")
        x1_in = [sem(f"x1_in{e}") for e in range(2)]
        wd_done = sem("wd_done")
        wd_ready = sem("wd_ready")
        zc_ready = sem("zc_ready")
        with_bias = sem("with_bias")
        v_done = sem("v_done")
        v_ready = sem("v_ready")
        f_done = sem("f_done")
        res_ready = sem("res_ready")
        out_stored = [sem(f"out_stored{e}") for e in range(2)]

        block = ctx.enter_context(nc.Block())

        def over_images(engine, body):
            body(0, 0)
            body(1, 1)
            with engine.Fori(1, B // 2) as i:
                body(2 * i, 0)
                body(2 * i + 1, 1)

        def over_all_but_last(engine, body):
            body(0, 0)
            body(1, 1)
            with engine.Fori(1, B // 2 - 1) as i:
                body(2 * i, 0)
                body(2 * i + 1, 1)
            body(B - 2, 0)

        @block.sync
        def _(sp):
            for dst, src in ((w_out[:, :, :], out_w.rearrange("(k p) o -> p k o", p=P)),
                             (w_dinv[:, :, :, :].rearrange("p a b c -> p (a b c)"), d_inv),
                             (w_tinv[:, :], t_inv),
                             (b_out[:, :], out_b.unsqueeze(0).broadcast_to([P, C]))):
                sp.dma_start(dst, src).then_inc(consts_in, 16)

            def load(b, e):
                wait(sp, res_ready, 4 * (b - 1))
                sp.dma_start(x1[e][:, :, :], x1_s[bass.ds(b * N, N), :].rearrange("(p t) c -> p t c", t=NT)
                             ).then_inc(x1_in[e], 16)

            def store(b, e):
                sp.wait_ge(res_ready, 4 * b + 4)
                sp.dma_start(out[bass.ds(b * N, N), :].rearrange("(p t) c -> p t c", t=NT),
                             res[e][:, :, :]).then_inc(out_stored[e], 16)

            def image(b, e):
                load(b + 1, 1 - e)
                store(b, e)
            load(0, 0)
            over_all_but_last(sp, image)
            store(B - 1, 1)
            for s in out_stored:
                sp.wait_ge(s, 16 * B // 2)

        @block.gpsimd
        def _(pool):
            pool.wait_ge(consts_in, 64)

            def image(b, e):
                pool.wait_ge(x1_in[e], 16 * ((b - e) // 2 + 1))
                pool.tensor_tensor(x1[e][:, :, :], x1[e][:, :, :],
                                   b_out[:, :].unsqueeze(1).broadcast_to([P, NT, C]), ALU.add).then_inc(with_bias, 1)
            over_images(pool, image)

        @block.tensor
        def _(pe):
            pe.wait_ge(consts_in, 64)
            for bd in range(2):
                for kt in range(CT):
                    m = pe.matmul(wbank[:, bd * C:(bd + 1) * C], w_dinv[:, kt, bd, :], w_out[:, kt, :],
                                  start=(kt == 0), stop=(kt == CT - 1))
            m.then_inc(wd_done, 1)
            pe.wait_ge(wd_ready, 1)

            def columns(b, e, n):
                if n == 0:
                    pe.wait_ge(zc_ready, b + 1)
                wait(pe, v_ready, bank_free(b, n))
                for t in range(2):
                    for bd in range(2):
                        m = pe.matmul(vbank[n % 2][:, t * C:(t + 1) * C],
                                      zc[e][:, bd, 2 * n + t].rearrange("p r w -> p (r w)"),
                                      wd[:, bd, :], start=(bd == 0), stop=(bd == 1))
                m.then_inc(v_done, 1)

            def rows(b, e, n):
                pe.wait_ge(v_ready, 4 * b + n + 1)
                wait(pe, res_ready, bank_free(b, n))
                pe.matmul(fbank[n % 2][:, :], w_tinv[:, :], v_sb[n % 2][:, :],
                          start=True, stop=True).then_inc(f_done, 1)

            def image(b, e):
                for n in range(4):
                    columns(b, e, n)
                    if n:
                        rows(b, e, n - 1)
                rows(b, e, 3)
            over_images(pe, image)

        @block.scalar
        def _(act):
            act.wait_ge(wd_done, 1)
            act.activation(wd[:, :, :].rearrange("p a b -> p (a b)"), wbank[:, :], ACT.Copy).then_inc(wd_ready, 1)

            def image(b, e):
                for n in range(4):
                    act.wait_ge(v_done, 4 * b + n + 1)
                    wait(act, f_done, bank_free(b, n))
                    act.activation(v_sb[n % 2][:, :], vbank[n % 2][:, :], ACT.Copy).then_inc(v_ready, 1)
            over_images(act, image)

        @block.vector
        def _(dve):
            def columns_of(b, e):
                wait(dve, v_done, 4 * b - 4)
                for bd in range(2):
                    src = z[:, bd, :, bass.ds(b * W, W)].rearrange("p r (w t) -> p t r w", t=NT)
                    m = dve.tensor_copy(zc[e][:, bd], src)
                m.then_inc(zc_ready, 1)

            def image(b, e):
                columns_of(b + 1, 1 - e)
                add(b, e)

            def add(b, e):
                dve.wait_ge(with_bias, b + 1)
                wait(dve, out_stored[e], 16 * ((b - e) // 2))
                for n in range(4):
                    dve.wait_ge(f_done, 4 * b + n + 1)
                    cols = lambda s: s[:, 2 * n:2 * n + 2, :].rearrange("p t c -> p (t c)")
                    dve.tensor_tensor(cols(res[e]), fbank[n % 2][:, :], cols(x1[e]), ALU.add).then_inc(res_ready, 1)
            columns_of(0, 0)
            over_all_but_last(dve, image)
            add(B - 1, 1)


def build(nc, a):
    scratch = lambda name, *shape: nc.dram_tensor(name, shape, F32).ap()
    q_s, k_s, v_s = (scratch(n, B * C, N) for n in ("q_s", "k_s", "v_s"))
    conv_phase(nc, a["x"], a["wq"], a["wv"], a["wk"], a["bq"], a["bv"], a["bk"], a["mean_op"], a["ident"],
               q_s, k_s, v_s)
    x1_s = scratch("x1_s", B * N, C)
    bands_s = scratch("bands_s", 4, TL[0], DL[0], C)
    synth_s = scratch("synth_s", 4, P, NB[0], C)
    ktab_s = scratch("ktab_s", 1, KROWS * KCOLS)
    with ExitStack() as ctx:
        sb = lambda name, shape: ctx.enter_context(nc.sbuf_tensor(name, shape, F32))
        conv_ops = [[sb(f"conv_op{v}{k}", [P, P]) for k in range(3 if NB[v] > 1 else 1)] for v in range(LEVELS)]
        conv_bias = sb("conv_bias", [P, 1])
        with nc.sbuf_tensor("heads_out", [P, NT, HEADS, HD], F32) as heads_out:
            attention_phase(nc, q_s, k_s, v_s, a["ident16"], a["ident"], heads_out)
            analysis_phase(nc, a["x"], heads_out, a["wp"], a["mean_op"], a["ident"], a["t_op"], a["d_op"],
                           [a[f"w{i}"] for i in range(6)], [a[f"b{i}"] for i in range(6)],
                           conv_ops, conv_bias, ktab_s, x1_s, bands_s)
        level0 = ctx.enter_context(nc.sbuf_tensor("level0", [P, 2, 2, NB[0], C], F32))
        z_in = ctx.enter_context(nc.semaphore("z_in"))
        bands_phase(nc, bands_s, conv_ops, conv_bias, a["ident"], a["dwt1"], a["dwt2"], a["inv2"], a["inv1"],
                    level0, z_in, synth_s)
        synthesis_phase(nc, level0, x1_s, a["out_w"], a["out_b"], a["d_inv"], a["t_inv"], a["out"])


def arrays_of(inputs):
    taps_first = lambda w: np.ascontiguousarray(np.transpose(w, (2, 3, 1, 0))).reshape(-1, C)
    a = {
        "x": np.ascontiguousarray(inputs["x"]).reshape(B * N, C),
        "wq": taps_first(inputs["L0_conv_w3"]), "bq": inputs["L0_conv_b3"],
        "wv": taps_first(inputs["L0_conv_w5"]), "bv": inputs["L0_conv_b5"],
        "wk": taps_first(inputs["L0_conv_w7"]), "bk": inputs["L0_conv_b7"],
        "wp": np.ascontiguousarray(np.transpose(inputs["L0_conv_wp"])),
        "out_w": np.ascontiguousarray(np.transpose(inputs["L1_conv_out_w"])), "out_b": inputs["L1_conv_out_b"],
        "mean_op": np.full((P, P), 1.0 / (N * CG), np.float32),
        "ident": np.eye(P, dtype=np.float32), "ident16": np.eye(P, dtype=np.float16),
        **wavelet_constants(),
    }
    for i in range(6):
        a[f"w{i}"] = np.ascontiguousarray(inputs[f"L1_conv_w{i}"]).reshape(1, 2 * i + 1, 2 * i + 1)
        a[f"b{i}"] = inputs[f"L1_conv_b{i}"]
    return a


def kernel(**inputs):
    import concourse.bacc as bacc
    from concourse.bass_utils import run_bass_kernel_spmd

    arrays = {f"in_{k}": np.ascontiguousarray(v) for k, v in arrays_of(inputs).items()}
    nc = bacc.Bacc("TRN2", target_bir_lowering=False, num_devices=1)
    a = {k[3:]: nc.dram_tensor(k, v.shape, mybir.dt.from_np(v.dtype), kind="ExternalInput").ap()
         for k, v in arrays.items()}
    a["out"] = nc.dram_tensor("out_0", (B * N, C), F32, kind="ExternalOutput").ap()
    build(nc, a)
    results = run_bass_kernel_spmd(nc, [arrays], core_ids=[0]).results
    return results[0]["out_0"].reshape(B, H, W, C)
```
